# Optimizing a Trainium2 kernel written in Bass

```python
import numpy as np
import jax
import jax.numpy as jnp

def _softmax(x, axis=-1):
    return jax.nn.softmax(x, axis=axis)

def _gelu(x):
    return jax.nn.gelu(x, approximate=True)

def _silu(x):
    return jax.nn.silu(x)

def _sigmoid(x):
    return jax.nn.sigmoid(x)

def _layernorm(x, axis=-1, eps=1e-05):
    m = jnp.mean(x, axis=axis, keepdims=True)
    v = jnp.var(x, axis=axis, keepdims=True)
    return (x - m) / jnp.sqrt(v + eps)

def _scatter_add(tgt, idx, src, axis=0):
    return tgt.at[idx].add(src)

def _segment_sum(src, seg, n):
    return jax.ops.segment_sum(src, seg, n)
kernel_name = 'mk_seq_preln_d2_jaxref_r4_5b9f25'

def setup_inputs(seed: int=0):
    np.random.seed(seed)
    _w = jnp.asarray

    def _L0_attn_setup():
        import jax, jax.numpy as jnp
        import numpy as np
        from jax import lax
        D_MODEL, D_STATE, D_CONV, D_INNER, DT_RANK = (256, 16, 4, 512, 64)
        B_SZ, L_SEQ = (2, 1024)

        def _silu(v):
            return v * jax.nn.sigmoid(v)

        def _layernorm(v, w, b, eps=1e-05):
            mu = jnp.mean(v, axis=-1, keepdims=True)
            var = jnp.var(v, axis=-1, keepdims=True)
            return (v - mu) * lax.rsqrt(var + eps) * w + b

        def _selective_scan(u, delta, A, Bm, Cm, Dp):
            Bb, L, d_inner = u.shape
            N = A.shape[1]

            def step(h, inp):
                dt_t, u_t, B_t, C_t = inp
                A_bar = jnp.exp(dt_t[..., None] * A)
                h = A_bar * h + dt_t[..., None] * B_t[:, None, :] * u_t[..., None]
                y = jnp.sum(h * C_t[:, None, :], axis=-1)
                return (h, y)
            h0 = jnp.zeros((Bb, d_inner, N), u.dtype)
            xs = (jnp.swapaxes(delta, 0, 1), jnp.swapaxes(u, 0, 1), jnp.swapaxes(Bm, 0, 1), jnp.swapaxes(Cm, 0, 1))
            _, ys = lax.scan(step, h0, xs)
            y = jnp.swapaxes(ys, 0, 1)
            return y + u * Dp[None, None, :]
        key = jax.random.key(seed)
        ks = jax.random.split(key, 12)
        s = 0.02
        x = jax.random.normal(ks[0], (B_SZ, L_SEQ, D_MODEL), jnp.float32)
        norm_w = jnp.ones((D_MODEL,), jnp.float32)
        norm_b = jnp.zeros((D_MODEL,), jnp.float32)
        W_in = jax.random.normal(ks[1], (D_MODEL, 2 * D_INNER), jnp.float32) * s
        conv_w = jax.random.normal(ks[2], (D_INNER, 1, D_CONV), jnp.float32) * 0.5
        conv_b = jnp.zeros((D_INNER,), jnp.float32)
        W_x = jax.random.normal(ks[3], (D_INNER, DT_RANK + 2 * D_STATE), jnp.float32) * s
        W_dt = jax.random.normal(ks[4], (DT_RANK, D_INNER), jnp.float32) * s
        dt_init = jnp.exp(jax.random.uniform(ks[5], (D_INNER,)) * (np.log(0.1) - np.log(0.001)) + np.log(0.001))
        dt_init = jnp.clip(dt_init, 0.0001, None)
        b_dt = dt_init + jnp.log(-jnp.expm1(-dt_init))
        A_log = jnp.log(jnp.broadcast_to(jnp.arange(1, D_STATE + 1, dtype=jnp.float32)[None, :], (D_INNER, D_STATE)))
        D = jnp.ones((D_INNER,), jnp.float32)
        W_out = jax.random.normal(ks[6], (D_INNER, D_MODEL), jnp.float32) * s
        return {'x': x, 'norm_w': norm_w, 'norm_b': norm_b, 'W_in': W_in, 'conv_w': conv_w, 'conv_b': conv_b, 'W_x': W_x, 'W_dt': W_dt, 'b_dt': b_dt, 'A_log': A_log, 'D': D, 'W_out': W_out}
    _L0_attn_in = _L0_attn_setup()

    def _L0_ffn_setup():
        import jax, jax.numpy as jnp
        import numpy as np
        HIDDEN = 256
        HEAD_DIM = 64
        N_EXPERTS = 16
        MIN_EXPERTS = 2
        B, T = (4, 512)

        def _normalize(x, axis):
            n = jnp.sqrt(jnp.sum(x * x, axis=axis, keepdims=True))
            return x / jnp.maximum(n, 1e-12)

        def _ste(x):
            hard = jax.lax.stop_gradient((x > 0).astype(x.dtype))
            return hard + x - jax.lax.stop_gradient(x)

        def _gating(hidden_states, sim_matrix, gates):
            b, t, c = hidden_states.shape
            flat = hidden_states.reshape(b * t, c)
            logits = _normalize(flat, -1) @ _normalize(sim_matrix, 0) - jax.nn.sigmoid(gates)
            gated = jax.nn.relu(logits)
            mask = _ste(gated)
            inactive = jnp.sum(mask, axis=1) == 0
            _, fb_idx = jax.lax.top_k(logits, MIN_EXPERTS)
            fb = jnp.zeros_like(mask).at[jnp.arange(b * t)[:, None], fb_idx].set(1.0)
            fb_applied = inactive[:, None] & (fb > 0)
            mask = jnp.where(fb_applied, 1.0, mask)
            masked_logits = jnp.where(mask > 0, gated, -jnp.inf)
            return jax.nn.softmax(masked_logits, axis=-1).reshape(b, t, -1)
        key = jax.random.key(seed)
        ks = jax.random.split(key, 6)
        xav_qkv = float(np.sqrt(6.0 / (HIDDEN + HEAD_DIM)))
        return {'hidden_states': jax.random.normal(ks[0], (B, T, HIDDEN), dtype=jnp.float32), 'sim_matrix': jax.random.normal(ks[1], (HIDDEN, N_EXPERTS), dtype=jnp.float32), 'gates': jnp.zeros((N_EXPERTS,), dtype=jnp.float32), 'q_proj': jax.random.uniform(ks[2], (N_EXPERTS, HIDDEN, HEAD_DIM), jnp.float32, -xav_qkv, xav_qkv), 'k_proj': jax.random.uniform(ks[3], (N_EXPERTS, HIDDEN, HEAD_DIM), jnp.float32, -xav_qkv, xav_qkv), 'v_proj': jax.random.uniform(ks[4], (N_EXPERTS, HIDDEN, HEAD_DIM), jnp.float32, -xav_qkv, xav_qkv), 'o_proj': jax.random.uniform(ks[5], (N_EXPERTS, HEAD_DIM, HIDDEN), jnp.float32, -xav_qkv, xav_qkv)}
    _L0_ffn_in = _L0_ffn_setup()

    def _L1_attn_setup():
        import jax, jax.numpy as jnp
        import numpy as np
        DIM, H, G = (256, 16, 4)
        HD = DIM // H
        HKV = H // G

        def rotate_half(x):
            return jnp.concatenate([-x[..., 1::2], x[..., ::2]], axis=-1)

        def rope_tables(seq_len, dim, dtype):
            inv_freq = 1.0 / 10000.0 ** (jnp.arange(0, dim, 2, dtype=jnp.float32) / dim)
            pos = jnp.arange(seq_len, dtype=jnp.float32)
            sinusoid = pos[:, None] * inv_freq[None, :]
            sin = jnp.concatenate([jnp.sin(sinusoid)] * 2, -1)
            cos = jnp.concatenate([jnp.cos(sinusoid)] * 2, -1)
            return (sin.astype(dtype)[None, :, None, :], cos.astype(dtype)[None, :, None, :])
        key = jax.random.key(seed)
        ks = jax.random.split(key, 9)
        s = 0.02
        return {'hidden_states': jax.random.normal(ks[0], (2, 512, DIM), jnp.float32), 'Wq': jax.random.normal(ks[1], (DIM, DIM), jnp.float32) * s, 'bq': jnp.zeros((DIM,), jnp.float32), 'Wk': jax.random.normal(ks[2], (DIM // G, DIM), jnp.float32) * s, 'bk': jnp.zeros((DIM // G,), jnp.float32), 'Wv': jax.random.normal(ks[3], (DIM // G, DIM), jnp.float32) * s, 'bv': jnp.zeros((DIM // G,), jnp.float32), 'Wo': jax.random.normal(ks[4], (DIM, DIM), jnp.float32) * s, 'bo': jnp.zeros((DIM,), jnp.float32)}
    _L1_attn_in = _L1_attn_setup()

    def _L1_ffn_setup():
        import math
        import jax, jax.numpy as jnp
        import numpy as np
        B, S, H, BOT, RD, N, K = (4, 512, 256, 128, 48, 1024, 8)
        key = jax.random.key(seed)
        ks = jax.random.split(key, 12)
        hidden_states = jax.random.normal(ks[0], (B, S, H), jnp.float32)
        q_proj_w = jax.random.normal(ks[1], (BOT, H), jnp.float32) * (1.0 / math.sqrt(H))
        router_w = jax.random.normal(ks[2], (RD, BOT), jnp.float32) * (1.0 / math.sqrt(BOT))
        aux_keys = jax.random.normal(ks[3], (N, BOT), jnp.float32) * 0.01
        aux_values = jax.random.normal(ks[4], (N, H), jnp.float32) * 0.02
        reliability_mask = jax.random.uniform(ks[5], (N,), jnp.float32)
        unc_w1 = jax.random.normal(ks[6], (H // 4, H), jnp.float32) * (1.0 / math.sqrt(H))
        unc_b1 = jnp.zeros((H // 4,), jnp.float32)
        unc_w2 = jax.random.normal(ks[7], (1, H // 4), jnp.float32) * 0.02
        unc_b2 = jnp.zeros((1,), jnp.float32)
        gate_w1 = jnp.asarray(0.5, jnp.float32)
        gate_bias = jnp.asarray(-1.0, jnp.float32)
        return {'hidden_states': hidden_states, 'q_proj_w': q_proj_w, 'router_w': router_w, 'aux_keys': aux_keys, 'aux_values': aux_values, 'reliability_mask': reliability_mask, 'unc_w1': unc_w1, 'unc_b1': unc_b1, 'unc_w2': unc_w2, 'unc_b2': unc_b2, 'gate_w1': gate_w1, 'gate_bias': gate_bias}
    _L1_ffn_in = _L1_ffn_setup()
    _d = {'L0_attn_x': _L0_attn_in['x'], 'L0_attn_norm_w': _L0_attn_in['norm_w'], 'L0_attn_norm_b': _L0_attn_in['norm_b'], 'L0_attn_W_in': _L0_attn_in['W_in'], 'L0_attn_conv_w': _L0_attn_in['conv_w'], 'L0_attn_conv_b': _L0_attn_in['conv_b'], 'L0_attn_W_x': _L0_attn_in['W_x'], 'L0_attn_W_dt': _L0_attn_in['W_dt'], 'L0_attn_b_dt': _L0_attn_in['b_dt'], 'L0_attn_A_log': _L0_attn_in['A_log'], 'L0_attn_D': _L0_attn_in['D'], 'L0_attn_W_out': _L0_attn_in['W_out'], 'L0_ffn_sim_matrix': _L0_ffn_in['sim_matrix'], 'L0_ffn_gates': _L0_ffn_in['gates'], 'L0_ffn_q_proj': _L0_ffn_in['q_proj'], 'L0_ffn_k_proj': _L0_ffn_in['k_proj'], 'L0_ffn_v_proj': _L0_ffn_in['v_proj'], 'L0_ffn_o_proj': _L0_ffn_in['o_proj'], 'L1_attn_Wq': _L1_attn_in['Wq'], 'L1_attn_bq': _L1_attn_in['bq'], 'L1_attn_Wk': _L1_attn_in['Wk'], 'L1_attn_bk': _L1_attn_in['bk'], 'L1_attn_Wv': _L1_attn_in['Wv'], 'L1_attn_bv': _L1_attn_in['bv'], 'L1_attn_Wo': _L1_attn_in['Wo'], 'L1_attn_bo': _L1_attn_in['bo'], 'L1_ffn_q_proj_w': _L1_ffn_in['q_proj_w'], 'L1_ffn_router_w': _L1_ffn_in['router_w'], 'L1_ffn_aux_keys': _L1_ffn_in['aux_keys'], 'L1_ffn_aux_values': _L1_ffn_in['aux_values'], 'L1_ffn_reliability_mask': _L1_ffn_in['reliability_mask'], 'L1_ffn_unc_w1': _L1_ffn_in['unc_w1'], 'L1_ffn_unc_b1': _L1_ffn_in['unc_b1'], 'L1_ffn_unc_w2': _L1_ffn_in['unc_w2'], 'L1_ffn_unc_b2': _L1_ffn_in['unc_b2'], 'L1_ffn_gate_w1': _L1_ffn_in['gate_w1'], 'L1_ffn_gate_bias': _L1_ffn_in['gate_bias']}
    _x0 = _d['L0_attn_x']
    _d['L0_attn_x'] = jax.random.normal(jax.random.fold_in(jax.random.key(seed), 1), (2, 2048, 256), dtype=_x0.dtype)
    del _x0
    return _d

def reference(L0_attn_x, L0_attn_norm_w, L0_attn_norm_b, L0_attn_W_in, L0_attn_conv_w, L0_attn_conv_b, L0_attn_W_x, L0_attn_W_dt, L0_attn_b_dt, L0_attn_A_log, L0_attn_D, L0_attn_W_out, L0_ffn_sim_matrix, L0_ffn_gates, L0_ffn_q_proj, L0_ffn_k_proj, L0_ffn_v_proj, L0_ffn_o_proj, L1_attn_Wq, L1_attn_bq, L1_attn_Wk, L1_attn_bk, L1_attn_Wv, L1_attn_bv, L1_attn_Wo, L1_attn_bo, L1_ffn_q_proj_w, L1_ffn_router_w, L1_ffn_aux_keys, L1_ffn_aux_values, L1_ffn_reliability_mask, L1_ffn_unc_w1, L1_ffn_unc_b1, L1_ffn_unc_w2, L1_ffn_unc_b2, L1_ffn_gate_w1, L1_ffn_gate_bias):

    def _L0_attn_ref(x, norm_w, norm_b, W_in, conv_w, conv_b, W_x, W_dt, b_dt, A_log, D, W_out):
        import jax, jax.numpy as jnp
        import numpy as np
        from jax import lax
        D_MODEL, D_STATE, D_CONV, D_INNER, DT_RANK = (256, 16, 4, 512, 64)
        B_SZ, L_SEQ = (2, 1024)

        def _silu(v):
            return v * jax.nn.sigmoid(v)

        def _layernorm(v, w, b, eps=1e-05):
            mu = jnp.mean(v, axis=-1, keepdims=True)
            var = jnp.var(v, axis=-1, keepdims=True)
            return (v - mu) * lax.rsqrt(var + eps) * w + b

        def _selective_scan(u, delta, A, Bm, Cm, Dp):
            Bb, L, d_inner = u.shape
            N = A.shape[1]

            def step(h, inp):
                dt_t, u_t, B_t, C_t = inp
                A_bar = jnp.exp(dt_t[..., None] * A)
                h = A_bar * h + dt_t[..., None] * B_t[:, None, :] * u_t[..., None]
                y = jnp.sum(h * C_t[:, None, :], axis=-1)
                return (h, y)
            h0 = jnp.zeros((Bb, d_inner, N), u.dtype)
            xs = (jnp.swapaxes(delta, 0, 1), jnp.swapaxes(u, 0, 1), jnp.swapaxes(Bm, 0, 1), jnp.swapaxes(Cm, 0, 1))
            _, ys = lax.scan(step, h0, xs)
            y = jnp.swapaxes(ys, 0, 1)
            return y + u * Dp[None, None, :]
        residual = x
        xn = _layernorm(x, norm_w, norm_b)
        xz = xn @ W_in
        x_ssm, z = jnp.split(xz, 2, axis=-1)
        xt = jnp.swapaxes(x_ssm, 1, 2)
        xt = jnp.pad(xt, ((0, 0), (0, 0), (D_CONV - 1, 0)))
        xc = lax.conv_general_dilated(xt, conv_w, window_strides=(1,), padding='VALID', feature_group_count=D_INNER, dimension_numbers=('NCH', 'OIH', 'NCH'))
        xc = xc + conv_b[None, :, None]
        x_conv = jnp.swapaxes(_silu(xc), 1, 2)
        x_dbl = x_conv @ W_x
        dt_low, B_mat, C_mat = jnp.split(x_dbl, [DT_RANK, DT_RANK + D_STATE], axis=-1)
        delta = jax.nn.softplus(dt_low @ W_dt + b_dt)
        A = -jnp.exp(A_log)
        y = _selective_scan(x_conv, delta, A, B_mat, C_mat, D)
        y = y * _silu(z)
        return residual + y @ W_out

    def _L0_ffn_ref(hidden_states, sim_matrix, gates, q_proj, k_proj, v_proj, o_proj):
        import jax, jax.numpy as jnp
        import numpy as np
        HIDDEN = 256
        HEAD_DIM = 64
        N_EXPERTS = 16
        MIN_EXPERTS = 2
        B, T = (4, 512)

        def _normalize(x, axis):
            n = jnp.sqrt(jnp.sum(x * x, axis=axis, keepdims=True))
            return x / jnp.maximum(n, 1e-12)

        def _ste(x):
            hard = jax.lax.stop_gradient((x > 0).astype(x.dtype))
            return hard + x - jax.lax.stop_gradient(x)

        def _gating(hidden_states, sim_matrix, gates):
            b, t, c = hidden_states.shape
            flat = hidden_states.reshape(b * t, c)
            logits = _normalize(flat, -1) @ _normalize(sim_matrix, 0) - jax.nn.sigmoid(gates)
            gated = jax.nn.relu(logits)
            mask = _ste(gated)
            inactive = jnp.sum(mask, axis=1) == 0
            _, fb_idx = jax.lax.top_k(logits, MIN_EXPERTS)
            fb = jnp.zeros_like(mask).at[jnp.arange(b * t)[:, None], fb_idx].set(1.0)
            fb_applied = inactive[:, None] & (fb > 0)
            mask = jnp.where(fb_applied, 1.0, mask)
            masked_logits = jnp.where(mask > 0, gated, -jnp.inf)
            return jax.nn.softmax(masked_logits, axis=-1).reshape(b, t, -1)
        b, t, c = hidden_states.shape
        rw = _gating(hidden_states, sim_matrix, gates)
        q = jnp.einsum('bte,bted->btd', rw, jnp.einsum('btc,ecd->bted', hidden_states, q_proj))
        k = jnp.einsum('bte,bted->btd', rw, jnp.einsum('btc,ecd->bted', hidden_states, k_proj))
        v = jnp.einsum('bte,bted->btd', rw, jnp.einsum('btc,ecd->bted', hidden_states, v_proj))
        scale = 1.0 / jnp.sqrt(jnp.asarray(HEAD_DIM, dtype=q.dtype))
        scores = jnp.einsum('bqd,bkd->bqk', q, k) * scale
        causal = jnp.tril(jnp.ones((t, t), dtype=bool))
        scores = jnp.where(causal, scores, -jnp.inf)
        attn = jnp.einsum('bqk,bkd->bqd', jax.nn.softmax(scores, axis=-1), v)
        mixed = attn[:, :, None, :] * rw[..., None]
        return jnp.einsum('bted,edc->btc', mixed, o_proj)

    def _L1_attn_ref(hidden_states, Wq, bq, Wk, bk, Wv, bv, Wo, bo):
        import jax, jax.numpy as jnp
        import numpy as np
        DIM, H, G = (256, 16, 4)
        HD = DIM // H
        HKV = H // G

        def rotate_half(x):
            return jnp.concatenate([-x[..., 1::2], x[..., ::2]], axis=-1)

        def rope_tables(seq_len, dim, dtype):
            inv_freq = 1.0 / 10000.0 ** (jnp.arange(0, dim, 2, dtype=jnp.float32) / dim)
            pos = jnp.arange(seq_len, dtype=jnp.float32)
            sinusoid = pos[:, None] * inv_freq[None, :]
            sin = jnp.concatenate([jnp.sin(sinusoid)] * 2, -1)
            cos = jnp.concatenate([jnp.cos(sinusoid)] * 2, -1)
            return (sin.astype(dtype)[None, :, None, :], cos.astype(dtype)[None, :, None, :])
        b, t, _ = hidden_states.shape
        q = (hidden_states @ Wq.T + bq).reshape(b, t, H, HD)
        k = (hidden_states @ Wk.T + bk).reshape(b, t, HKV, HD)
        v = (hidden_states @ Wv.T + bv).reshape(b, t, HKV, HD)
        sin, cos = rope_tables(t, HD, q.dtype)
        q = q * cos + rotate_half(q) * sin
        k = k * cos + rotate_half(k) * sin
        k = jnp.repeat(k, G, axis=2)
        v = jnp.repeat(v, G, axis=2)
        scale = 1.0 / jnp.sqrt(jnp.float32(HD)).astype(q.dtype)
        scores = jnp.einsum('bthd,bshd->btsh', q, k) * scale
        probs = jax.nn.softmax(scores, axis=2)
        context = jnp.einsum('btsh,bshd->bthd', probs, v).reshape(b, t, DIM)
        return context @ Wo.T + bo

    def _L1_ffn_ref(hidden_states, q_proj_w, router_w, aux_keys, aux_values, reliability_mask, unc_w1, unc_b1, unc_w2, unc_b2, gate_w1, gate_bias):
        import math
        import jax, jax.numpy as jnp
        import numpy as np
        B, S, H, BOT, RD, N, K = (4, 512, 256, 128, 48, 1024, 8)
        query = jnp.einsum('bsh,dh->bsd', hidden_states, q_proj_w)
        rq = jnp.einsum('bsd,rd->bsr', query, router_w)
        rk = jnp.einsum('nd,rd->nr', aux_keys, router_w)
        scores = jnp.einsum('bsr,nr->bsn', rq, rk) / math.sqrt(RD)
        scores = scores + reliability_mask[None, None, :]
        top_scores, top_idx = jax.lax.top_k(scores, K)
        mean = hidden_states.mean(axis=-1, keepdims=True)
        variance = ((hidden_states - mean) ** 2).mean(axis=-1)
        log_var = jnp.log1p(variance)
        normalized_var = log_var / (log_var.mean() + 1e-06)
        h1 = jax.nn.gelu(jnp.einsum('bsh,fh->bsf', hidden_states, unc_w1) + unc_b1, approximate=False)
        learned = (jnp.einsum('bsf,of->bso', h1, unc_w2) + unc_b2)[..., 0]
        uncertainty = jnp.clip(normalized_var * 0.5 + jax.nn.sigmoid(learned) * 2.5, 0.0, 5.0)
        gate = jax.nn.sigmoid(gate_w1 * uncertainty + gate_bias)
        w = jax.nn.softmax(top_scores, axis=-1)
        v = aux_values[top_idx]
        agg = jnp.einsum('bsk,bskh->bsh', w, v)
        out = hidden_states + gate[..., None] * agg
        return out
    x = L0_attn_x
    x = x + _L0_attn_ref(_layernorm(x, axis=-1), L0_attn_norm_w, L0_attn_norm_b, L0_attn_W_in, L0_attn_conv_w, L0_attn_conv_b, L0_attn_W_x, L0_attn_W_dt, L0_attn_b_dt, L0_attn_A_log, L0_attn_D, L0_attn_W_out)
    x = x + _L0_ffn_ref(_layernorm(x, axis=-1), L0_ffn_sim_matrix, L0_ffn_gates, L0_ffn_q_proj, L0_ffn_k_proj, L0_ffn_v_proj, L0_ffn_o_proj)
    x = x + _L1_attn_ref(_layernorm(x, axis=-1), L1_attn_Wq, L1_attn_bq, L1_attn_Wk, L1_attn_bk, L1_attn_Wv, L1_attn_bv, L1_attn_Wo, L1_attn_bo)
    x = x + _L1_ffn_ref(_layernorm(x, axis=-1), L1_ffn_q_proj_w, L1_ffn_router_w, L1_ffn_aux_keys, L1_ffn_aux_values, L1_ffn_reliability_mask, L1_ffn_unc_w1, L1_ffn_unc_b1, L1_ffn_unc_w2, L1_ffn_unc_b2, L1_ffn_gate_w1, L1_ffn_gate_bias)
    return x

_drawn_inputs = setup_inputs


def setup_inputs(seed=0):
    import zlib

    import numpy as np

    out = dict(_drawn_inputs(seed))
    spreads = {'L0_attn_norm_w': (1.0, 0.2),
     'L0_attn_norm_b': (0.0, 0.1),
     'L0_attn_conv_b': (0.0, 0.1),
     'L0_attn_D': (1.0, 0.2),
     'L0_ffn_gates': (0.0, 0.1),
     'L1_attn_bq': (0.0, 0.1),
     'L1_attn_bk': (0.0, 0.1),
     'L1_attn_bv': (0.0, 0.1),
     'L1_attn_bo': (0.0, 0.1),
     'L1_ffn_unc_b1': (0.0, 0.1)}
    factors = {}
    for name, (base, spread) in spreads.items():
        noise = np.random.default_rng([zlib.crc32(name.encode()), seed]).standard_normal(out[name].shape)
        drawn = base * np.exp(spread * noise) if base else spread * noise
        out[name] = jnp.asarray(drawn.astype(out[name].dtype))
    for name, factor in factors.items():
        out[name] = (out[name] * factor).astype(out[name].dtype)
    return out
```

```python
import numpy as np
import concourse.bass as bass
from concourse import mybir
from contextlib import ExitStack

FP32 = mybir.dt.float32
BF16 = mybir.dt.bfloat16
ALU = mybir.AluOpType
ACT = mybir.ActivationFunctionType
AXIS_X = mybir.AxisListType.X
ds = bass.ds

B, L, D = 2, 2048, 256
T = B * L
TILE = 128
NT = T // TILE
CH = 512
TPC = CH // TILE
NCH = T // CH
CPB = L // CH
KD = D // 128
DI, DTR, NS, KC = 512, 64, 16, 4
NDI = DI // 128
EPS = 1e-5


class Chain:

    def __init__(self, eng, sem, base=0):
        self.eng, self.sem, self.base, self.n = eng, sem, base, 0

    def mark(self, ins):
        ins.then_inc(self.sem, 1)
        self.n += 1

    def wait(self):
        self.eng.wait_ge(self.sem, self.base + self.n)

    def step(self, ins):
        self.mark(ins)
        self.wait()


class Scope(ExitStack):

    def __init__(self, nc, name):
        super().__init__()
        self.nc, self.name, self.sems = nc, name, []

    def sb(self, name, shape, dt=FP32):
        return self.enter_context(self.nc.sbuf_tensor(f"{self.name}_{name}", shape, dt))

    def ps(self, name, shape, dt=FP32):
        return self.enter_context(self.nc.psum_tensor(f"{self.name}_{name}", shape, dt))

    def sem(self, name):
        self.sems.append(self.nc.alloc_semaphore(f"{self.name}_{name}"))
        return self.sems[-1]

    def clear(self):
        self.nc.all_engine_barrier()
        self.nc.clear_and_free_semaphores(self.sems)
        self.nc.all_engine_barrier()


def layernorm_scales(nc, chain, stats, mean, rstd, tmp, var_ready, rstd_ready, nth):
    me, mo, ve, vo = (stats[:, :, k] for k in (1, 4, 2, 5))
    chain.mark(nc.vector.tensor_tensor(mean[:], me, mo, ALU.add))
    chain.mark(nc.vector.tensor_tensor(tmp[:], me, mo, ALU.subtract))
    chain.step(nc.vector.tensor_tensor(rstd[:], ve, vo, ALU.add))
    chain.mark(nc.vector.tensor_scalar(mean[:], mean[:], 0.5, None, ALU.mult))
    chain.mark(nc.vector.tensor_tensor(tmp[:], tmp[:], tmp[:], ALU.mult))
    chain.step(nc.vector.tensor_scalar(rstd[:], rstd[:], 1.0 / D, EPS, ALU.mult, ALU.add))
    nc.vector.scalar_tensor_tensor(rstd[:], tmp[:], 0.25, rstd[:], ALU.mult, ALU.add).then_inc(var_ready, 1)
    chain.eng.wait_ge(rstd_ready, nth)


def mamba_front(nc, a):
    with Scope(nc, "front") as s:
        x = s.sb("x", [128, NT, D])
        xr = s.sb("xr", [128, TPC, D])
        stats, mean, rstd, tmp = s.sb("stats", [128, NT, 6]), s.sb("mean", [128, NT]), s.sb("rstd", [128, NT]), s.sb("tmp", [128, NT])
        stats2, mean2, rstd2 = s.sb("stats2", [128, NT, 6]), s.sb("mean2", [128, NT]), s.sb("rstd2", [128, NT])
        mhalf = s.sb("mhalf", [128, NT])
        ident = s.sb("ident", [128, 128])
        w_in = s.sb("w_in", [128, KD, 2 * DI])
        w_x = s.sb("w_x", [128, NDI, DTR + 2 * NS])
        w_dt = s.sb("w_dt", [DTR, DI])
        norm_w, norm_b = s.sb("norm_w", [128, KD]), s.sb("norm_b", [128, KD])
        conv_w, conv_b, b_dt = s.sb("conv_w", [128, NDI, KC]), s.sb("conv_b", [128, NDI]), s.sb("b_dt", [128, NDI])
        xn = s.sb("xn", [128, TPC, D])
        xnT = s.sb("xnT", [128, KD, CH])
        xs = s.sb("xs", [128, NDI, KC - 1 + CH])
        xc = s.sb("xc", [128, NDI, CH])
        uT, gT, dT = s.sb("uT", [128, NDI, CH]), s.sb("gT", [128, NDI, CH]), s.sb("dT", [128, NDI, CH])
        xdbl = s.sb("xdbl", [DTR + 2 * NS, CH])
        sp_abs, sp_exp, sp_log, sp_relu = (s.sb(n, [128, NDI, CH]) for n in ("sp_abs", "sp_exp", "sp_log", "sp_relu"))

        pT = s.ps("pT", [128, KD, CH])
        pXZ = s.ps("pXZ", [128, 4, CH])
        pDBL = s.ps("pDBL", [128, CH])

        x_in, w_loaded, x_stored, out_u, out_g, out_d, out_bc = (s.sem(n) for n in (
            "x_in", "w_loaded", "x_stored", "out_u", "out_g", "out_d", "out_bc"))
        dve_chain, act_chain = s.sem("dve_chain"), s.sem("act_chain")
        half_ready, var_ready, rstd_ready, var2_ready, rstd2_ready = (s.sem(n) for n in (
            "half_ready", "var_ready", "rstd_ready", "var2_ready", "rstd2_ready"))
        xh_ready, xr_ready, xn_ready, xnT_psum, xnT_ready = (s.sem(n) for n in (
            "xh_ready", "xr_ready", "xn_ready", "xnT_psum", "xnT_ready"))
        x_proj, z_proj, x_evac, z_evac, conv_done, u_ready, g_ready = (s.sem(n) for n in (
            "x_proj", "z_proj", "x_evac", "z_evac", "conv_done", "u_ready", "g_ready"))
        dbl_psum, dbl_ready, dt_psum, dt_read, dt_relu, log_ready, d_ready = (s.sem(n) for n in (
            "dbl_psum", "dbl_ready", "dt_psum", "dt_read", "dt_relu", "log_ready", "d_ready"))

        x_view = a["x"].rearrange("(n p) d -> p n d", p=128)
        xr_view = a["xr"].rearrange("(n p) d -> p n d", p=128)
        uT_view, gT_view, dT_view = (a[n].rearrange("(m p) t -> p m t", p=128) for n in ("uT", "gT", "dT"))
        WLOADS = 11

        with nc.Block() as block:
            @block.sync
            def _(sp):
                for q in range(4):
                    n0 = q * NT // 4
                    sp.dma_start(x[:, n0:n0 + NT // 4, :], x_view[:, n0:n0 + NT // 4, :]).then_inc(x_in, 16)
                for dst, src in ((ident[:], a["ident"]), (w_in[:], a["W_in"].rearrange("(k p) n -> p k n", p=128)),
                                 (norm_w[:], a["norm_w"]),
                                 (norm_b[:], a["norm_b"]),
                                 (conv_w[:], a["conv_w"]),
                                 (conv_b[:], a["conv_b"]),
                                 (b_dt[:], a["b_dt"]),
                                 (w_x[:], a["W_x"].rearrange("(m p) n -> p m n", p=128)),
                                 (w_dt[:], a["W_dt"])):
                    sp.dma_start(dst, src).then_inc(w_loaded, 16)
                with sp.Fori(0, NCH) as c:
                    sp.wait_ge(xr_ready, c + 1)
                    sp.dma_start(xr_view[:, ds(c * TPC, TPC), :], xr[:]).then_inc(x_stored, 16)
                with sp.Fori(0, NCH) as c:
                    sp.wait_ge(u_ready, (c + 1) * NDI)
                    sp.dma_start(uT_view[:, :, ds(c * CH, CH)], uT[:]).then_inc(out_u, 16)
                    sp.wait_ge(g_ready, (c + 1) * NDI)
                    sp.dma_start(gT_view[:, :, ds(c * CH, CH)], gT[:]).then_inc(out_g, 16)
                    sp.wait_ge(dbl_ready, c + 1)
                    sp.dma_start(a["BC"][:, ds(c * CH, CH)], xdbl[DTR:DTR + 2 * NS, :]).then_inc(out_bc, 16)
                    sp.wait_ge(d_ready, c + 1)
                    sp.dma_start(dT_view[:, :, ds(c * CH, CH)], dT[:]).then_inc(out_d, 16)
                for sem in (x_stored, out_u, out_g, out_bc, out_d):
                    sp.wait_ge(sem, 16 * NCH)

            @block.gpsimd
            def _(pool):
                nc.gpsimd.memset(mhalf[:], -0.5).then_inc(half_ready, 1)
                pool.wait_ge(half_ready, 1)
                pool.wait_ge(var_ready, 1)
                nc.gpsimd.tensor_tensor(rstd[:], rstd[:], mhalf[:], ALU.pow).then_inc(rstd_ready, 1)
                pool.wait_ge(var2_ready, 1)
                nc.gpsimd.tensor_tensor(rstd2[:], rstd2[:], mhalf[:], ALU.pow).then_inc(rstd2_ready, 1)
                with pool.Fori(0, NCH) as c:
                    pool.wait_ge(log_ready, c + 1)
                    pool.wait_ge(dt_relu, (c + 1) * NDI)
                    pool.wait_ge(out_d, c * 16)
                    nc.gpsimd.tensor_tensor(dT[:], sp_relu[:], sp_log[:], ALU.add).then_inc(d_ready, 1)

            @block.vector
            def _(dve):
                ch = Chain(dve, dve_chain)
                for n in range(NT):
                    if n % (NT // 4) == 0:
                        dve.wait_ge(x_in, 16 * 4)
                    ch.mark(nc.vector.bn_stats(stats[:, n, :], x[:, n, :]))
                ch.wait()
                layernorm_scales(nc, ch, stats, mean, rstd, tmp, var_ready, rstd_ready, 1)
                front = ch.n
                with dve.Fori(0, NCH) as c:
                    lc = Chain(dve, dve_chain, front + c * 4 * TPC)
                    dve.wait_ge(x_stored, c * 16)
                    for j in range(TPC):
                        n = c * TPC + j
                        lc.mark(nc.vector.tensor_scalar(xn[:, j, :], x[:, ds(n, 1), :], mean[:, ds(n, 1)], rstd[:, ds(n, 1)], ALU.subtract, ALU.mult))
                    lc.wait()
                    for j in range(TPC):
                        n = c * TPC + j
                        lc.mark(nc.vector.bn_stats(stats2[:, ds(n, 1), :], xn[:, j, :]))
                        lc.mark(nc.vector.tensor_tensor(xr[:, j, :], x[:, ds(n, 1), :], xn[:, j, :], ALU.add))
                    lc.wait()
                    for j in range(TPC):
                        n = c * TPC + j
                        lc.mark(nc.vector.tensor_scalar(x[:, ds(n, 1), :], xn[:, j, :], 1.0, None, ALU.mult))
                    lc.wait()
                    dve.sem_inc(xr_ready, 1)
                ch = Chain(dve, dve_chain, front + NCH * 4 * TPC)
                layernorm_scales(nc, ch, stats2, mean2, rstd2, tmp, var2_ready, rstd2_ready, 1)
                dve.wait_ge(w_loaded, 16 * 9)
                before = front + NCH * 4 * TPC + ch.n
                PER = 1 + NDI * KC
                with dve.Fori(0, B) as b:
                    nc.vector.memset(xs[:, :, CH:CH + KC - 1], 0.0).then_inc(dve_chain, 1)
                    with dve.Fori(0, CPB) as j4:
                        c = b * CPB + j4
                        lc = Chain(dve, dve_chain, before + 1 + b * (1 + CPB * PER) + j4 * PER)
                        lc.wait()
                        dve.wait_ge(xnT_psum, c)
                        for j in range(TPC):
                            n = c * TPC + j
                            nc.vector.tensor_scalar(xn[:, j, :], x[:, ds(n, 1), :], mean2[:, ds(n, 1)], rstd2[:, ds(n, 1)], ALU.subtract, ALU.mult).then_inc(xn_ready, 1)
                        lc.step(nc.vector.tensor_copy(xs[:, :, 0:KC - 1], xs[:, :, CH:CH + KC - 1]))
                        for m in range(NDI):
                            dve.wait_ge(x_proj, c * NDI + m + 1)
                            nc.vector.tensor_copy(xs[:, m, KC - 1:], pXZ[:, m, :]).then_inc(x_evac, 1)
                            dve.wait_ge(x_evac, c * NDI + m + 1)
                            if m == 0:
                                dve.wait_ge(u_ready, c * NDI)
                            lc.step(nc.vector.tensor_scalar(xc[:, m, :], xs[:, m, 0:CH], conv_w[:, m, 0:1], conv_b[:, m:m + 1], ALU.mult, ALU.add))
                            for k in range(1, KC):
                                ins = nc.vector.scalar_tensor_tensor(xc[:, m, :], xs[:, m, k:k + CH], conv_w[:, m, k:k + 1], xc[:, m, :], ALU.mult, ALU.add)
                                lc.step(ins)
                            dve.sem_inc(conv_done, 1)
                        for m in range(NDI):
                            dve.wait_ge(dt_psum, c * NDI + m + 1)
                            if m == 0:
                                dve.wait_ge(d_ready, c)
                            nc.vector.tensor_scalar(sp_relu[:, m, :], pXZ[:, m, :], b_dt[:, m:m + 1], 0.0, ALU.add, ALU.max).then_inc(dt_relu, 1)
                        assert lc.n == PER

            @block.scalar
            def _(act):
                act.wait_ge(w_loaded, 16 * 9)
                with act.Fori(0, NCH) as c:
                    lc = Chain(act, act_chain, c * 2 * NDI)
                    act.wait_ge(xnT_psum, c + 1)
                    act.wait_ge(z_proj, c * NDI)
                    for k in range(KD):
                        nc.scalar.activation(xnT[:, k, :], pT[:, k, :], ACT.Identity, bias=norm_b[:, k:k + 1], scale=norm_w[:, k:k + 1]).then_inc(xnT_ready, 1)
                    act.wait_ge(out_u, c * 16)
                    for m in range(NDI):
                        act.wait_ge(conv_done, c * NDI + m + 1)
                        nc.scalar.activation(uT[:, m, :], xc[:, m, :], ACT.Silu).then_inc(u_ready, 1)
                    act.wait_ge(out_g, c * 16)
                    for m in range(NDI):
                        act.wait_ge(z_proj, c * NDI + m + 1)
                        nc.scalar.activation(gT[:, m, :], pXZ[:, m, :], ACT.Silu).then_inc(g_ready, 1)
                    act.wait_ge(dbl_psum, c + 1)
                    act.wait_ge(out_bc, c * 16)
                    nc.scalar.activation(xdbl[:], pDBL[0:DTR + 2 * NS, :], ACT.Identity).then_inc(dbl_ready, 1)
                    for m in range(NDI):
                        act.wait_ge(dt_relu, c * NDI + m + 1)
                        nc.scalar.activation(sp_abs[:, m, :], pXZ[:, m, :], ACT.Abs, bias=b_dt[:, m:m + 1]).then_inc(dt_read, 1)
                    act.wait_ge(dt_read, (c + 1) * NDI)
                    for m in range(NDI):
                        lc.mark(nc.scalar.activation(sp_exp[:, m, :], sp_abs[:, m, :], ACT.Exp, scale=-1.0))
                    lc.wait()
                    act.wait_ge(d_ready, c)
                    for m in range(NDI):
                        lc.mark(nc.scalar.activation(sp_log[:, m, :], sp_exp[:, m, :], ACT.Ln, bias=1.0))
                    lc.wait()
                    act.sem_inc(log_ready, 1)

            @block.tensor
            def _(pe):
                pe.wait_ge(w_loaded, 16 * 9)
                with pe.Fori(0, NCH) as c:
                    pe.wait_ge(xnT_ready, c * KD)
                    for j in range(TPC):
                        pe.wait_ge(xn_ready, c * TPC + j + 1)
                        for k in range(KD):
                            last = nc.tensor.transpose(pT[:, k, j * 128:(j + 1) * 128], xn[:, j, k * 128:(k + 1) * 128], ident[:])
                    last.then_inc(xnT_psum, 1)
                    pe.wait_ge(xnT_ready, (c + 1) * KD)
                    pe.wait_ge(dt_read, c * NDI)
                    pe.wait_ge(dt_relu, c * NDI)
                    for m in range(NDI):
                        for k in range(KD):
                            last = nc.tensor.matmul(pXZ[:, m, :], w_in[:, k, m * 128:(m + 1) * 128], xnT[:, k, :], start=(k == 0), stop=(k == KD - 1))
                        last.then_inc(x_proj, 1)
                    for m in range(NDI):
                        pe.wait_ge(x_evac, c * NDI + m + 1)
                        for k in range(KD):
                            last = nc.tensor.matmul(pXZ[:, m, :], w_in[:, k, DI + m * 128:DI + (m + 1) * 128], xnT[:, k, :], start=(k == 0), stop=(k == KD - 1))
                        last.then_inc(z_proj, 1)
                    pe.wait_ge(dbl_ready, c)
                    for m in range(NDI):
                        pe.wait_ge(u_ready, c * NDI + m + 1)
                        last = nc.tensor.matmul(pDBL[0:DTR + 2 * NS, :], w_x[:, m, :], uT[:, m, :], start=(m == 0), stop=(m == NDI - 1))
                    last.then_inc(dbl_psum, 1)
                    pe.wait_ge(dbl_ready, c + 1)
                    for m in range(NDI):
                        pe.wait_ge(g_ready, c * NDI + m + 1)
                        nc.tensor.matmul(pXZ[:, m, :], w_dt[:, m * 128:(m + 1) * 128], xdbl[0:DTR, :], start=True, stop=True).then_inc(dt_psum, 1)
        s.clear()

def selective_scan(nc, a):
    STEPS = NS * CPB
    ROUNDS = B * NDI
    SPLIT = 3
    NDBU = 4
    AHEAD = NDBU - 1
    with Scope(nc, "scan") as s:
        b_all = s.sb("b_all", [128, NS, L])
        delta, u = s.sb("delta", [128, 2, L]), s.sb("u", [128, 2, L])
        g, du = s.sb("g", [128, L]), s.sb("du", [128, L])
        a_log, decay = s.sb("a_log", [128, 2, NS + 1]), s.sb("decay", [128, 2, NS])
        c_parts = s.sb("c_parts", [96, L], BF16)
        pick = s.sb("pick", [96, NS, 128], BF16)
        part_of = s.sb("part_of", [96, NS])
        ident = s.sb("ident", [128, 128])
        dbu, h, hc = s.sb("dbu", [128, NDBU, CH]), s.sb("h", [128, 2, CH]), s.sb("hc", [128, 2, CH])
        y_acc = s.ps("y_acc", [128, CPB, CH])
        abar, c_all = s.ps("abar", [128, 2, CH]), s.ps("c_all", [128, 2, CH])

        c_raw, c_rest = h[:, 0, :], h[:, 1, :]
        c_split = dbu[:, 0:2, :].rearrange("p a c -> p (a c)").bitcast(BF16)[:, 0:SPLIT * CH].rearrange("p (i c) -> p i c", i=SPLIT)

        const_in, craw_in, split_done, split_out, cparts_in = (s.sem(n) for n in (
            "const_in", "craw_in", "split_done", "split_out", "cparts_in"))
        b_in = [s.sem(f"b_in{n}") for n in range(NS)]
        du_in = [s.sem("du_in_even"), s.sem("du_in_odd")]
        g_in, y_out = s.sem("g_in"), s.sem("y_out")
        du_ready, dbu_ready, decay_exp, decay_ready = (s.sem(n) for n in (
            "du_ready", "dbu_ready", "decay_exp", "decay_ready"))
        abar_ready, scan_done, c_ready, c_used, hc_added, acc_read, y_half, y_ready, zeroed = (s.sem(n) for n in (
            "abar_ready", "scan_done", "c_ready", "c_used", "hc_added", "acc_read", "y_half", "y_ready", "zeroed"))
        pick_made = s.sem("pick_made")

        dT_view, uT_view, gT_view, yT_view = (a[n].rearrange("(m p) t -> p m t", p=128) for n in ("dT", "uT", "gT", "yT"))
        BC = a["BC"]

        with nc.Block() as block:
            @block.sync
            def _(sp):
                sp.dma_start(c_raw, BC[NS:2 * NS, :].rearrange("n (c t) -> (n c) t", t=CH)).then_inc(craw_in, 16)
                sp.dma_start(part_of[:], a["part_of"]).then_inc(const_in, 16)
                sp.dma_start(ident[:], a["ident"]).then_inc(const_in, 16)
                sp.wait_ge(split_done, 5)
                for i in range(SPLIT):
                    sp.dma_start(a["c_split"][i].rearrange("n (c t) -> (n c) t", t=CH), c_split[:, i, :]).then_inc(split_out, 16)

                def load_round(q):
                    b, m = divmod(q, NDI)
                    sp.dma_start(a_log[:, q % 2, :], a["a_log_d"][:, m, :]).then_inc(du_in[q % 2], 16)
                    sp.dma_start(delta[:, q % 2, :], dT_view[:, m, b * L:(b + 1) * L]).then_inc(du_in[q % 2], 16)
                    sp.dma_start(u[:, q % 2, :], uT_view[:, m, b * L:(b + 1) * L]).then_inc(du_in[q % 2], 16)

                def load_gate(q):
                    b, m = divmod(q, NDI)
                    sp.dma_start(g[:], gT_view[:, m, b * L:(b + 1) * L]).then_inc(g_in, 16)

                def load_b(n, b):
                    sp.dma_start(b_all[:, n, :], BC[n:n + 1, b * L:(b + 1) * L].broadcast_to([128, L])).then_inc(b_in[n], 16)

                def load_c(b):
                    for i in range(SPLIT):
                        sp.dma_start(c_parts[32 * i:32 * i + NS, :], a["c_split"][i, :, b * L:(b + 1) * L]).then_inc(cparts_in, 16)

                load_round(0)
                load_b(0, 0)
                sp.wait_ge(split_out, 16 * SPLIT)
                sp.wait_ge(zeroed, 1)
                load_c(0)
                for n in range(1, NS):
                    load_b(n, 0)
                load_gate(0)
                load_round(1)
                for q in range(ROUNDS):
                    if (q + 1) % NDI == 0 and q + 1 < ROUNDS:
                        for n in range(NS):
                            sp.wait_ge(dbu_ready, q * STEPS + (n + 1) * CPB)
                            load_b(n, (q + 1) // NDI)
                        sp.wait_ge(c_ready, (q + 1) * STEPS)
                        load_c((q + 1) // NDI)
                    sp.wait_ge(y_ready, (q + 1) * CPB)
                    b, m = divmod(q, NDI)
                    sp.dma_start(yT_view[:, m, b * L:(b + 1) * L], u[:, q % 2, :]).then_inc(y_out, 16)
                    if q + 1 < ROUNDS:
                        load_gate(q + 1)
                    if q + 2 < ROUNDS:
                        sp.wait_ge(y_out, 16 * (q + 1))
                        load_round(q + 2)
                sp.wait_ge(y_out, 16 * ROUNDS)

            @block.gpsimd
            def _(pool):
                nc.gpsimd.memset(c_parts[:], 0.0).then_inc(zeroed, 1)
                with pool.Fori(0, ROUNDS // 2) as pair:
                    for par in range(2):
                        q = pair * 2 + par
                        pool.wait_ge(du_in[par], (pair + 1) * 48)
                        pool.wait_ge(dbu_ready, q * STEPS)
                        nc.gpsimd.tensor_tensor(du[:], delta[:, par, :], u[:, par, :], ALU.mult).then_inc(du_ready, 1)
                        pool.wait_ge(du_ready, q + 1)
                        for n in range(NS):
                            pool.wait_ge(b_in[n], (pair // (NDI // 2) + 1) * 16)
                            for j in range(CPB):
                                k = n * CPB + j
                                pool.wait_ge(scan_done, q * STEPS + k)
                                nc.gpsimd.tensor_tensor(dbu[:, k % NDBU, :], du[:, j * CH:(j + 1) * CH], b_all[:, n, j * CH:(j + 1) * CH], ALU.mult).then_inc(dbu_ready, 1)

            @block.scalar
            def _(act):
                with act.Fori(0, ROUNDS // 2) as pair:
                    for par in range(2):
                        q = pair * 2 + par
                        act.wait_ge(du_in[par], (pair + 1) * 48)
                        nc.scalar.activation(decay[:, par, :], a_log[:, par, 0:NS], ACT.Exp).then_inc(decay_exp, 1)
                        act.wait_ge(decay_exp, q + 1)
                        nc.scalar.activation(decay[:, par, :], decay[:, par, :], ACT.Copy, scale=-1.0).then_inc(decay_ready, 1)
                        act.wait_ge(decay_ready, q + 1)
                        for k in range(STEPS):
                            n, j = divmod(k, CPB)
                            act.wait_ge(scan_done, q * STEPS + k - 1 + AHEAD)
                            nc.scalar.activation(abar[:, k % 2, :], delta[:, par, j * CH:(j + 1) * CH], ACT.Exp, scale=decay[:, par, n:n + 1]).then_inc(abar_ready, 1)

            @block.vector
            def _(dve):
                dve.wait_ge(craw_in, 16)
                for i in range(SPLIT):
                    nc.vector.tensor_copy(c_split[:, i, :], c_raw if i % 2 == 0 else c_rest).then_inc(split_done, 1)
                    dve.wait_ge(split_done, 2 * i + 1)
                    if i < SPLIT - 1:
                        rest, new = (c_raw, c_rest) if i % 2 == 0 else (c_rest, c_raw)
                        nc.vector.tensor_tensor(new, rest, c_split[:, i, :], ALU.subtract).then_inc(split_done, 1)
                        dve.wait_ge(split_done, 2 * i + 2)
                dve.wait_ge(const_in, 32)
                nc.vector.tensor_copy(pick[:], part_of[:].unsqueeze(2).broadcast_to([96, NS, 128])).then_inc(pick_made, 1)
                dve.wait_ge(split_out, 16 * SPLIT)
                dve.sem_inc(scan_done, AHEAD)
                with dve.Fori(0, ROUNDS // 2) as pair:
                    for par in range(2):
                        q = pair * 2 + par
                        s0 = q * STEPS
                        for k in range(STEPS + 1):
                            n, j = divmod(k, CPB)
                            if k < STEPS:
                                dve.wait_ge(abar_ready, s0 + k + 1)
                                dve.wait_ge(dbu_ready, s0 + k + 1)
                                if j:
                                    dve.wait_ge(scan_done, s0 + k + AHEAD)
                                if k >= 2:
                                    dve.wait_ge(c_used, s0 + k - 1)
                                state = h[:, (k - 1) % 2, CH - 1:CH] if j else 0.0
                                ins = nc.vector.tensor_tensor_scan(h[:, k % 2, :], abar[:, k % 2, :], dbu[:, k % NDBU, :], state, ALU.mult, ALU.add)
                                ins.then_inc(scan_done, 1)
                            if k >= 1:
                                dve.wait_ge(scan_done, s0 + k + AHEAD)
                                dve.wait_ge(c_ready, s0 + k)
                                dve.wait_ge(hc_added, s0 + k)
                                nc.vector.tensor_tensor(hc[:, (k - 1) % 2, :], h[:, (k - 1) % 2, :], c_all[:, (k - 1) % 2, :], ALU.mult).then_inc(c_used, 1)
                        dve.wait_ge(hc_added, s0 + STEPS + 2)
                        dve.wait_ge(g_in, (q + 1) * 16)
                        dve.wait_ge(du_in[par], (pair + 1) * 48)
                        dve.wait_ge(dbu_ready, s0 + STEPS)
                        for j in range(CPB):
                            t = slice(j * CH, (j + 1) * CH)
                            nc.vector.scalar_tensor_tensor(u[:, par, t], u[:, par, t], a_log[:, par, NS:NS + 1], y_acc[:, j, :], ALU.mult, ALU.add).then_inc(acc_read, 1)
                        for j in range(CPB):
                            t = slice(j * CH, (j + 1) * CH)
                            dve.wait_ge(acc_read, q * CPB + j + 1)
                            nc.vector.tensor_tensor(u[:, par, t], u[:, par, t], g[:, t], ALU.mult).then_inc(y_ready, 1)

            @block.tensor
            def _(pe):
                pe.wait_ge(const_in, 32)
                pe.wait_ge(pick_made, 1)
                pe.sem_inc(hc_added, 2)

                with pe.Fori(0, ROUNDS // 2) as pair:
                    for par in range(2):
                        q = pair * 2 + par
                        s0 = q * STEPS
                        pe.wait_ge(cparts_in, (pair // (NDI // 2) + 1) * 16 * SPLIT)
                        for k in range(STEPS + 1):
                            n, j = divmod(k, CPB)
                            if k < STEPS:
                                if k >= 2:
                                    pe.wait_ge(c_used, s0 + k - 1)
                                else:
                                    pe.wait_ge(c_used, s0)
                                nc.tensor.matmul(c_all[:, k % 2, :], pick[:, n, :], c_parts[:, j * CH:(j + 1) * CH], start=True, stop=True).then_inc(c_ready, 1)
                            if k >= 1:
                                n1, j1 = divmod(k - 1, CPB)
                                pe.wait_ge(c_used, s0 + k)
                                if k - 1 < CPB:
                                    pe.wait_ge(acc_read, q * CPB)
                                nc.tensor.matmul(y_acc[:, j1, :], ident[:], hc[:, (k - 1) % 2, :], start=(n1 == 0), stop=(n1 == NS - 1)).then_inc(hc_added, 1)
        s.clear()

NE, HD = 16, 64
QKV = 3 * HD


def chunk_layernorm(nc, ch, xin, xout, st, pow_in, pow_out, var_ready, rstd_ready, nth):
    for j in range(TPC):
        ch.mark(nc.vector.bn_stats(st[:, j, 0:6], xin[:, j, :]))
    ch.wait()
    me, mo, ve, vo = (st[:, :, k] for k in (1, 4, 2, 5))
    mean, diff = st[:, :, 6], st[:, :, 7]
    ch.mark(nc.vector.tensor_tensor(mean, me, mo, ALU.add))
    ch.mark(nc.vector.tensor_tensor(diff, me, mo, ALU.subtract))
    ch.step(nc.vector.tensor_tensor(pow_in[:, 0:TPC], ve, vo, ALU.add))
    ch.mark(nc.vector.tensor_scalar(mean, mean, 0.5, None, ALU.mult))
    ch.mark(nc.vector.tensor_tensor(diff, diff, diff, ALU.mult))
    ch.step(nc.vector.tensor_scalar(pow_in[:, 0:TPC], pow_in[:, 0:TPC], 1.0 / D, EPS, ALU.mult, ALU.add))
    nc.vector.scalar_tensor_tensor(pow_in[:, 0:TPC], diff, 0.25, pow_in[:, 0:TPC], ALU.mult, ALU.add).then_inc(var_ready, 1)
    ch.eng.wait_ge(rstd_ready, nth)
    for j in range(TPC):
        ch.mark(nc.vector.tensor_scalar(xout[:, j, :], xin[:, j, :], st[:, j, 6:7], pow_out[:, j:j + 1], ALU.subtract, ALU.mult))


CHUNK_LN_MARKS = TPC + 6 + TPC


def expert_front(nc, a):
    with Scope(nc, "moe") as s:
        w_out = s.sb("w_out", [128, NDI, D])
        w_qkv = s.sb("w_qkv", [128, KD, NE * QKV])
        sim, sim_sq = s.sb("sim", [128, KD, NE]), s.sb("sim_sq", [128, KD, NE])
        sim_inv, sim_eps = s.sb("sim_inv", [128, NE]), s.sb("sim_eps", [128, NE])
        gate_sig = s.sb("gate_sig", [128, NE])
        expert_no = s.sb("expert_no", [128, NE])
        ident, ones, mhalf = s.sb("ident", [128, 128]), s.sb("ones", [128, 128]), s.sb("mhalf", [128, NE])
        yT, xr = s.sb("yT", [128, NDI, CH]), s.sb("xr", [128, TPC, D])
        x1, xh, sq = s.sb("x1", [128, TPC, D]), s.sb("xh", [128, TPC, D]), s.sb("sq", [128, D])
        st, var, rstd = s.sb("st", [128, TPC, 8]), s.sb("var", [128, TPC]), s.sb("rstd", [128, TPC])
        ssq, ssq_clamped, inv_norm = s.sb("ssq", [128, TPC]), s.sb("ssq_clamped", [128, TPC]), s.sb("inv_norm", [128, TPC])
        xT = s.sb("xT", [128, KD, CH])
        logit, gated, active, shifted, expd, rw = (s.sb(n, [128, TPC, NE]) for n in ("logit", "gated", "active", "shifted", "expd", "rw"))
        top, top_idx, top_f = s.sb("top", [128, TPC, 8]), s.sb("top_idx", [128, TPC, 8], mybir.dt.uint32), s.sb("top_f", [128, TPC, 8])
        fall, fall2 = s.sb("fall", [128, TPC, NE]), s.sb("fall2", [128, TPC, NE])
        gmax, idle, total = s.sb("gmax", [128, TPC]), s.sb("idle", [128, TPC]), s.sb("total", [128, TPC])
        acc = s.sb("acc", [128, TPC, 2, QKV])
        mixed = s.sb("mixed", [128, TPC, QKV])
        qkT = s.sb("qkT", [128, CH])

        NP = 4
        pP = s.ps("pP", [128, NP, CH])
        pT = s.ps("pT", [128, KD, CH])
        pX = s.ps("pX", [128, CH])
        pQK = s.ps("pQK", [128, CH])

        w_loaded, y_in, x1_out, rw_out, qk_out, v_out = (s.sem(n) for n in ("w_loaded", "y_in", "x1_out", "rw_out", "qk_out", "v_out"))
        dve_sem, const_set, sim_ready, ssq_ready = (s.sem(n) for n in ("dve_sem", "const_set", "sim_ready", "ssq_ready"))
        x1_psum, x1_ready, var_ready, rstd_ready, xh_ready, norm_ready, inv_ready = (s.sem(n) for n in (
            "x1_psum", "x1_ready", "var_ready", "rstd_ready", "xh_ready", "norm_ready", "inv_ready"))
        xT_psum, xT_ready, lg_psum, lg_read, shift_ready, exp_ready, rw_ready = (s.sem(n) for n in (
            "xT_psum", "xT_ready", "lg_psum", "lg_read", "shift_ready", "exp_ready", "rw_ready"))
        p_psum, p_read, mix_ready, qk_psum, qk_ready, sim_psum, simsq_ready, sig_ready, pow_sim, pow_sim_in = (s.sem(n) for n in (
            "p_psum", "p_read", "mix_ready", "qk_psum", "qk_ready", "sim_psum", "simsq_ready", "sig_ready", "pow_sim", "pow_sim_in"))

        yT_view = a["yT"].rearrange("(m p) t -> p m t", p=128)
        xr_view, x1_view, rw_view, v_view = (a[n].rearrange("(n p) d -> p n d", p=128) for n in ("xr", "x1", "rw", "v0"))
        PAIRS = NE // 2
        BANKS = TPC * PAIRS
        NW = 7

        with nc.Block() as block:
            @block.sync
            def _(sp):
                for dst, src in ((ident[:], a["ident"]), (w_out[:], a["W_out"].rearrange("(m p) n -> p m n", p=128)),
                                 (sim[:], a["sim"].rearrange("(k p) n -> p k n", p=128)),
                                 (gate_sig[:], a["gates"].broadcast_to([128, NE])),
                                 (expert_no[:], a["expert_no"]), (w_qkv[:, 0, :], a["w_qkv"][0:128, :]), (w_qkv[:, 1, :], a["w_qkv"][128:256, :])):
                    sp.dma_start(dst, src).then_inc(w_loaded, 16)
                sp.dma_start(yT[:], yT_view[:, :, 0:CH]).then_inc(y_in, 16)
                sp.dma_start(xr[:], xr_view[:, 0:TPC, :]).then_inc(y_in, 16)

                def stores(c, more):
                    sp.wait_ge(x1_ready, (c + 1) * TPC)
                    sp.dma_start(x1_view[:, ds(c * TPC, TPC), :], x1[:]).then_inc(x1_out, 16)
                    if more:
                        sp.dma_start(yT[:], yT_view[:, :, ds((c + 1) * CH, CH)]).then_inc(y_in, 16)
                        sp.dma_start(xr[:], xr_view[:, ds((c + 1) * TPC, TPC), :]).then_inc(y_in, 16)
                    sp.wait_ge(rw_ready, c + 1)
                    sp.dma_start(rw_view[:, ds(c * TPC, TPC), :], rw[:]).then_inc(rw_out, 16)

                def qkv_stores(c):
                    sp.wait_ge(mix_ready, (c + 1) * TPC)
                    sp.dma_start(v_view[:, ds(c * TPC, TPC), :], mixed[:, :, 2 * HD:QKV]).then_inc(v_out, 16)
                    sp.wait_ge(qk_ready, c + 1)
                    sp.dma_start(a["qkT"][:, ds(c * CH, CH)], qkT[:]).then_inc(qk_out, 16)

                stores(0, True)
                with sp.Fori(1, NCH - 1) as c:
                    sp.wait_ge(x1_ready, (c + 1) * TPC)
                    sp.dma_start(x1_view[:, ds(c * TPC, TPC), :], x1[:]).then_inc(x1_out, 16)
                    sp.dma_start(yT[:], yT_view[:, :, ds((c + 1) * CH, CH)]).then_inc(y_in, 16)
                    sp.dma_start(xr[:], xr_view[:, ds((c + 1) * TPC, TPC), :]).then_inc(y_in, 16)
                    qkv_stores(c - 1)
                    sp.wait_ge(rw_ready, c + 1)
                    sp.dma_start(rw_view[:, ds(c * TPC, TPC), :], rw[:]).then_inc(rw_out, 16)
                c = NCH - 1
                sp.wait_ge(x1_ready, (c + 1) * TPC)
                sp.dma_start(x1_view[:, ds(c * TPC, TPC), :], x1[:]).then_inc(x1_out, 16)
                qkv_stores(c - 1)
                sp.wait_ge(rw_ready, c + 1)
                sp.dma_start(rw_view[:, ds(c * TPC, TPC), :], rw[:]).then_inc(rw_out, 16)
                qkv_stores(c)
                for sem in (x1_out, rw_out, v_out, qk_out):
                    sp.wait_ge(sem, 16 * NCH)

            @block.gpsimd
            def _(pool):
                nc.gpsimd.memset(mhalf[:], -0.5).then_inc(const_set, 1)
                nc.gpsimd.memset(ones[:], 1.0).then_inc(const_set, 1)
                pool.wait_ge(const_set, 2)
                pool.wait_ge(pow_sim_in, 1)
                nc.gpsimd.tensor_tensor(sim_inv[:], sim_eps[:], mhalf[:], ALU.pow).then_inc(pow_sim, 1)
                with pool.Fori(0, NCH) as c:
                    pool.wait_ge(var_ready, c + 1)
                    nc.gpsimd.tensor_tensor(rstd[:], var[:], mhalf[:, 0:TPC], ALU.pow).then_inc(rstd_ready, 1)
                    pool.wait_ge(ssq_ready, c + 1)
                    pool.wait_ge(lg_read, c * TPC)
                    nc.gpsimd.tensor_tensor(inv_norm[:], ssq_clamped[:], mhalf[:, 0:TPC], ALU.pow).then_inc(inv_ready, 1)

            HEAD = CHUNK_LN_MARKS
            GATE = 10 + 4 * TPC
            MIX = 2 * PAIRS * TPC

            @block.vector
            def _(dve):
                def head(c, base):
                    ch = Chain(dve, dve_sem, base)
                    dve.wait_ge(y_in, (c + 1) * 32)
                    dve.wait_ge(x1_out, c * 16)
                    for j in range(TPC):
                        dve.wait_ge(x1_psum, c * TPC + j + 1)
                        nc.vector.tensor_tensor(x1[:, j, :], pX[:, (j % 2) * D:(j % 2 + 1) * D], xr[:, j, :], ALU.add).then_inc(x1_ready, 1)
                    dve.wait_ge(x1_ready, (c + 1) * TPC)
                    dve.wait_ge(xT_psum, c)
                    dve.wait_ge(norm_ready, c * TPC)
                    chunk_layernorm(nc, ch, x1, xh, st, var, rstd, var_ready, rstd_ready, c + 1)
                    ch.wait()
                    dve.sem_inc(xh_ready, 1)
                    assert ch.n == HEAD, ch.n

                def clamp(c):
                    dve.wait_ge(norm_ready, (c + 1) * TPC)
                    dve.wait_ge(inv_ready, c)
                    nc.vector.tensor_scalar(ssq_clamped[:], ssq[:], 1e-24, None, ALU.max).then_inc(ssq_ready, 1)

                def gate(c, base):
                    ch = Chain(dve, dve_sem, base)
                    dve.wait_ge(lg_psum, c + 1)
                    dve.wait_ge(inv_ready, c + 1)
                    for j in range(TPC):
                        nc.vector.scalar_tensor_tensor(logit[:, j, :], pX[:, j * NE:(j + 1) * NE], inv_norm[:, j:j + 1], gate_sig[:], ALU.mult, ALU.subtract).then_inc(lg_read, 1)
                    dve.wait_ge(lg_read, (c + 1) * TPC)
                    ch.mark(nc.vector.tensor_scalar(gated[:], logit[:], 0.0, None, ALU.max))
                    for j in range(TPC):
                        ch.mark(nc.vector.max(top[:, j, :], logit[:, j, :]))
                    ch.wait()
                    ch.mark(nc.vector.tensor_scalar(active[:], gated[:], 0.0, None, ALU.is_gt))
                    ch.mark(nc.vector.reduce_max(gmax[:], gated[:], AXIS_X))
                    for j in range(TPC):
                        ch.mark(nc.vector.max_index(top_idx[:, j, :], top[:, j, :], logit[:, j, :]))
                    ch.wait()
                    dve.wait_ge(exp_ready, c)
                    nc.vector.tensor_tensor(shifted[:], gated[:], gmax[:, :].unsqueeze(2).broadcast_to([128, TPC, NE]), ALU.subtract).then_inc(shift_ready, 1)
                    ch.mark(nc.vector.tensor_scalar(idle[:], gmax[:], 0.0, None, ALU.is_le))
                    ch.step(nc.vector.tensor_copy(top_f[:], top_idx[:]))
                    for j in range(TPC):
                        ch.mark(nc.vector.tensor_scalar(fall[:, j, :], expert_no[:], top_f[:, j, 0:1], idle[:, j:j + 1], ALU.is_equal, ALU.mult))
                    for j in range(TPC):
                        ch.mark(nc.vector.tensor_scalar(fall2[:, j, :], expert_no[:], top_f[:, j, 1:2], idle[:, j:j + 1], ALU.is_equal, ALU.mult))
                    ch.wait()
                    ch.step(nc.vector.tensor_tensor(active[:], active[:], fall[:], ALU.add))
                    ch.step(nc.vector.tensor_tensor(active[:], active[:], fall2[:], ALU.add))
                    dve.wait_ge(exp_ready, c + 1)
                    ch.step(nc.vector.tensor_tensor(expd[:], expd[:], active[:], ALU.mult))
                    ch.step(nc.vector.reduce_sum(total[:], expd[:], AXIS_X))
                    ch.step(nc.vector.reciprocal(total[:], total[:]))
                    dve.wait_ge(rw_out, c * 16)
                    nc.vector.tensor_tensor(rw[:], expd[:], total[:, :].unsqueeze(2).broadcast_to([128, TPC, NE]), ALU.mult).then_inc(rw_ready, 1)
                    dve.wait_ge(rw_ready, c + 1)
                    assert ch.n == GATE, ch.n

                def mix(c, j, base):
                    ch = Chain(dve, dve_sem, base + j * 2 * PAIRS)
                    for e in range(NE):
                        bank = (j * PAIRS + e // 2) % NP
                        src = pP[:, bank, (e % 2) * QKV:(e % 2 + 1) * QKV]
                        dst = acc[:, j, e % 2, :]
                        if e % 2 == 0:
                            dve.wait_ge(p_psum, c * BANKS + j * PAIRS + e // 2 + 1)
                        if e < 2:
                            ins = nc.vector.tensor_scalar(dst, src, rw[:, j, e:e + 1], None, ALU.mult)
                        else:
                            dve.wait_ge(dve_sem, ch.base + e - 1)
                            ins = nc.vector.scalar_tensor_tensor(dst, src, rw[:, j, e:e + 1], dst, ALU.mult, ALU.add)
                        ch.mark(ins)
                    ch.wait()
                    if j == 0:
                        dve.wait_ge(qk_psum, c)
                        dve.wait_ge(v_out, c * 16)
                    nc.vector.tensor_tensor(mixed[:, j, :], acc[:, j, 0, :], acc[:, j, 1, :], ALU.add).then_inc(mix_ready, 1)

                dve.wait_ge(w_loaded, 16 * NW)
                nc.vector.tensor_tensor(sim_sq[:], sim[:], sim[:], ALU.mult).then_inc(simsq_ready, 1)
                dve.wait_ge(sim_psum, 1)
                nc.vector.tensor_scalar(sim_eps[:], pX[:, 0:NE], 1e-24, None, ALU.max).then_inc(pow_sim_in, 1)
                dve.wait_ge(pow_sim, 1)
                for k in range(KD):
                    ins = nc.vector.tensor_tensor(sim[:, k, :], sim[:, k, :], sim_inv[:], ALU.mult)
                    ins.then_inc(sim_ready, 1)
                head(0, 0)
                clamp(0)
                dve.wait_ge(sig_ready, 1)
                PER = GATE + MIX + HEAD
                with dve.Fori(0, NCH - 1) as c:
                    base = HEAD + c * PER
                    gate(c, base)
                    mix(c, 0, base + GATE)
                    mix(c, 1, base + GATE)
                    head(c + 1, base + GATE + 2 * PAIRS * 2)
                    mix(c, 2, base + GATE + HEAD)
                    clamp(c + 1)
                    mix(c, 3, base + GATE + HEAD)
                c, base = NCH - 1, HEAD + (NCH - 1) * PER
                gate(c, base)
                for j in range(TPC):
                    mix(c, j, base + GATE)

            @block.scalar
            def _(act):
                def head(c):
                    act.wait_ge(xh_ready, c + 1)
                    act.wait_ge(ssq_ready, c)
                    for j in range(TPC):
                        if j:
                            act.wait_ge(norm_ready, c * TPC + j)
                        nc.scalar.activation(sq[:], xh[:, j, :], ACT.Square, accum_out=ssq[:, j:j + 1]).then_inc(norm_ready, 1)

                def move_in(c):
                    act.wait_ge(xT_psum, c + 1)
                    act.wait_ge(p_psum, c * BANKS)
                    for k in range(KD):
                        nc.scalar.activation(xT[:, k, :], pT[:, k, :], ACT.Copy).then_inc(xT_ready, 1)

                def gate(c):
                    act.wait_ge(shift_ready, c + 1)
                    act.wait_ge(rw_ready, c)
                    nc.scalar.activation(expd[:], shifted[:], ACT.Exp).then_inc(exp_ready, 1)

                def qk(c):
                    act.wait_ge(qk_psum, c + 1)
                    act.wait_ge(qk_out, c * 16)
                    nc.scalar.activation(qkT[:], pQK[:], ACT.Copy).then_inc(qk_ready, 1)

                act.wait_ge(w_loaded, 16 * NW)
                nc.scalar.activation(gate_sig[:], gate_sig[:], ACT.Sigmoid).then_inc(sig_ready, 1)
                head(0)
                with act.Fori(0, NCH - 1) as c:
                    move_in(c)
                    gate(c)
                    head(c + 1)
                    qk(c)
                move_in(NCH - 1)
                gate(NCH - 1)
                qk(NCH - 1)

            @block.tensor
            def _(pe):
                def head_x(c):
                    pe.wait_ge(y_in, (c + 1) * 32)
                    pe.wait_ge(lg_read, c * TPC)
                    for j in range(TPC):
                        if j == 2:
                            pe.wait_ge(x1_ready, c * TPC + 2)
                        for m in range(NDI):
                            last = nc.tensor.matmul(pX[:, (j % 2) * D:(j % 2 + 1) * D], yT[:, m, j * 128:(j + 1) * 128], w_out[:, m, :], start=(m == 0), stop=(m == NDI - 1))
                        if j % 2:
                            last.then_inc(x1_psum, 2)

                def head_t(c):
                    pe.wait_ge(xh_ready, c + 1)
                    pe.wait_ge(xT_ready, c * KD)
                    for j in range(TPC):
                        for k in range(KD):
                            last = nc.tensor.transpose(pT[:, k, j * 128:(j + 1) * 128], xh[:, j, k * 128:(k + 1) * 128], ident[:])
                    last.then_inc(xT_psum, 1)

                def logits(c):
                    pe.wait_ge(xT_ready, (c + 1) * KD)
                    pe.wait_ge(x1_ready, (c + 1) * TPC)
                    for j in range(TPC):
                        for k in range(KD):
                            last = nc.tensor.matmul(pX[:, j * NE:(j + 1) * NE], xT[:, k, j * 128:(j + 1) * 128], sim[:, k, :], start=(k == 0), stop=(k == KD - 1))
                    last.then_inc(lg_psum, 1)

                def products(c, j):
                    for pr in range(PAIRS):
                        n = j * PAIRS + pr
                        bank_free(c, n)
                        for k in range(KD):
                            last = nc.tensor.matmul(pP[:, n % NP, 0:2 * QKV], xT[:, k, j * 128:(j + 1) * 128], w_qkv[:, k, pr * 2 * QKV:(pr + 1) * 2 * QKV], start=(k == 0), stop=(k == KD - 1))
                        last.then_inc(p_psum, 1)

                def bank_free(c, n):
                    PER = GATE + MIX + HEAD
                    if n >= NP:
                        j, pr = divmod(n - NP, PAIRS)
                        past_head = HEAD if (j >= 2) else 0
                        if isinstance(c, int) and c == NCH - 1:
                            past_head = 0
                        pe.wait_ge(dve_sem, HEAD + c * PER + GATE + past_head + j * 2 * PAIRS + 2 * pr + 2)
                    else:
                        pe.wait_ge(mix_ready, c * TPC)

                def qk(c):
                    pe.wait_ge(mix_ready, (c + 1) * TPC)
                    pe.wait_ge(qk_ready, c)
                    for j in range(TPC):
                        last = nc.tensor.transpose(pQK[:, j * 128:(j + 1) * 128], mixed[:, j, 0:128], ident[:])
                    last.then_inc(qk_psum, 1)

                pe.wait_ge(w_loaded, 16 * NW)
                pe.wait_ge(const_set, 2)
                pe.wait_ge(simsq_ready, 1)
                for k in range(KD):
                    last = nc.tensor.matmul(pX[:, 0:NE], ones[:], sim_sq[:, k, :], start=(k == 0), stop=(k == KD - 1))
                last.then_inc(sim_psum, 1)
                pe.wait_ge(sim_ready, KD)
                head_x(0)
                head_t(0)
                with pe.Fori(0, NCH - 1) as c:
                    logits(c)
                    products(c, 0)
                    products(c, 1)
                    head_x(c + 1)
                    products(c, 2)
                    head_t(c + 1)
                    products(c, 3)
                    qk(c)
                c = NCH - 1
                logits(c)
                for j in range(TPC):
                    products(c, j)
                qk(c)
        s.clear()

def causal_attention(nc, a):
    QT = L // TILE
    GRP = CH // TILE
    SCALE = float(HD) ** -0.5
    KO = NE * HD // 128
    with Scope(nc, "causal") as s:
        ident, above = s.sb("ident", [128, 128]), s.sb("above", [128, 128])
        w_o = s.sb("w_o", [128, KO, D])
        qT, kT = s.sb("qT", [HD, L]), s.sb("kT", [HD, L])
        v, rw, x = s.sb("v", [128, QT, HD]), s.sb("rw", [128, QT, NE]), s.sb("x", [128, QT, D])
        probs = s.sb("probs", [128, 2, L])
        probsT = s.sb("probsT", [128, 2, CH])
        smax, nmax, ssum, rsum = (s.sb(n, [128, QT]) for n in ("smax", "nmax", "ssum", "rsum"))
        attn, mixed = s.sb("attn", [128, 2, HD]), s.sb("mixed", [128, 2, NE, HD])
        mixedT = s.sb("mixedT", [128, KO, TILE])
        pS = s.ps("pS", [128, L])
        pT = s.ps("pT", [128, 2, CH])
        pA, pO = s.ps("pA", [128, CH]), s.ps("pO", [128, CH])

        w_in, b_in, x_out = s.sem("w_in"), s.sem("b_in"), s.sem("x_out")
        (s_psum, masked, max_ready, nmax_ready, exp_done, pT_psum, pT_moved, attn_psum, rsum_ready, attn_ready,
         mix_ready, o_psum, x_ready) = (s.sem(n) for n in (
             "s_psum", "masked", "max_ready", "nmax_ready", "exp_done", "pT_psum", "pT_moved", "attn_psum", "rsum_ready",
             "attn_ready", "mix_ready", "o_psum", "x_ready"))

        rw_view, v_view, x1_view, x2_view = (a[n].rearrange("(n p) d -> p n d", p=128) for n in ("rw", "v0", "x1", "x2"))
        GRPS = [qt // GRP + 1 for qt in range(QT)]
        PER_B = sum(GRPS) + 2 * QT

        uses = {}
        for qt in range(QT + 2):
            if 2 <= qt:
                for hlf in range(2):
                    uses["m", qt - 2, hlf] = len(uses)
            if 1 <= qt <= QT:
                for g in range(GRPS[qt - 1]):
                    uses["p", qt - 1, g] = len(uses)
        assert len(uses) == PER_B and PER_B % 2 == 0

        with nc.Block() as block:
            @block.sync
            def _(sp):
                for dst, src in ((ident[:], a["ident"]), (above[:], a["above"]), (w_o[:], a["w_o"].rearrange("(m p) n -> p m n", p=128))):
                    sp.dma_start(dst, src).then_inc(w_in, 16)
                with sp.Fori(0, B) as b:
                    sp.wait_ge(s_psum, b * QT)
                    sp.wait_ge(x_out, b * 16)
                    sp.dma_start(qT[:], a["qkT"][0:HD, ds(b * L, L)]).then_inc(b_in, 16)
                    sp.dma_start(kT[:], a["qkT"][HD:2 * HD, ds(b * L, L)]).then_inc(b_in, 16)
                    sp.dma_start(v[:], v_view[:, ds(b * QT, QT), :]).then_inc(b_in, 16)
                    sp.dma_start(rw[:], rw_view[:, ds(b * QT, QT), :]).then_inc(b_in, 16)
                    sp.dma_start(x[:], x1_view[:, ds(b * QT, QT), :]).then_inc(b_in, 16)
                    sp.wait_ge(x_ready, (b + 1) * QT)
                    sp.dma_start(x2_view[:, ds(b * QT, QT), :], x[:]).then_inc(x_out, 16)
                sp.wait_ge(x_out, 16 * B)

            @block.vector
            def _(dve):
                with dve.Fori(0, B) as b:
                    def peak(qt):
                        dve.wait_ge(s_psum, b * QT + qt + 1)
                        diag = pS[:, qt * 128:(qt + 1) * 128]
                        nc.vector.tensor_tensor(diag, diag, above[:], ALU.add).then_inc(masked, 1)
                        dve.wait_ge(masked, b * QT + qt + 1)
                        nc.vector.reduce_max(smax[:, qt:qt + 1], pS[:, 0:(qt + 1) * 128], AXIS_X).then_inc(max_ready, 1)
                        dve.wait_ge(max_ready, b * QT + qt + 1)
                        nc.vector.tensor_scalar(nmax[:, qt:qt + 1], smax[:, qt:qt + 1], -SCALE, None, ALU.mult).then_inc(nmax_ready, 1)

                    def spread(qt):
                        dve.wait_ge(exp_done, b * QT + qt + 1)
                        nc.vector.reciprocal(rsum[:, qt:qt + 1], ssum[:, qt:qt + 1]).then_inc(rsum_ready, 1)
                        dve.wait_ge(rsum_ready, b * QT + qt + 1)
                        dve.wait_ge(attn_psum, b * QT + qt + 1)
                        nc.vector.tensor_scalar(attn[:, qt % 2, :], pA[:, 0:HD], rsum[:, qt:qt + 1], None, ALU.mult).then_inc(attn_ready, 1)
                        dve.wait_ge(attn_ready, b * QT + qt + 1)
                        if qt >= 2:
                            dve.wait_ge(pT_psum, b * PER_B + uses["m", qt - 2, 1] + 1)
                        nc.vector.tensor_tensor(mixed[:, qt % 2, :, :], attn[:, qt % 2, :].unsqueeze(1).broadcast_to([128, NE, HD]),
                                                rw[:, qt, :].unsqueeze(2).broadcast_to([128, NE, HD]), ALU.mult).then_inc(mix_ready, 1)

                    def add(qt):
                        dve.wait_ge(o_psum, b * QT + qt + 1)
                        nc.vector.tensor_tensor(x[:, qt, :], pO[:, 0:D], x[:, qt, :], ALU.add).then_inc(x_ready, 1)

                    dve.wait_ge(w_in, 48)
                    dve.wait_ge(b_in, (b + 1) * 80)
                    for qt in range(QT + 2):
                        if qt < QT:
                            peak(qt)
                        if 2 <= qt:
                            add(qt - 2)
                        if 1 <= qt <= QT:
                            spread(qt - 1)

            @block.scalar
            def _(act):
                with act.Fori(0, B) as b:
                    for qt in range(QT + 2):
                        if 2 <= qt:
                            for hlf in range(2):
                                act.wait_ge(pT_psum, b * PER_B + uses["m", qt - 2, hlf] + 1)
                                if hlf == 0:
                                    act.wait_ge(o_psum, b * QT + qt - 2)
                                nc.scalar.activation(mixedT[:, 4 * hlf:4 * hlf + 4, :], pT[:, uses["m", qt - 2, hlf] % 2, :], ACT.Copy).then_inc(pT_moved, 1)
                        if qt < QT:
                            act.wait_ge(nmax_ready, b * QT + qt + 1)
                            if qt >= 2:
                                act.wait_ge(attn_psum, b * QT + qt - 1)
                            else:
                                act.wait_ge(attn_psum, b * QT)
                            n = (qt + 1) * 128
                            nc.scalar.activation(probs[:, qt % 2, 0:n], pS[:, 0:n], ACT.Exp, bias=nmax[:, qt:qt + 1], scale=SCALE, accum_out=ssum[:, qt:qt + 1]).then_inc(exp_done, 1)
                        if 1 <= qt <= QT:
                            for g in range(GRPS[qt - 1]):
                                n = uses["p", qt - 1, g]
                                w = min(GRP, qt - g * GRP) * 128
                                act.wait_ge(pT_psum, b * PER_B + n + 1)
                                nc.scalar.activation(probsT[:, n % 2, 0:w], pT[:, n % 2, 0:w], ACT.Copy).then_inc(pT_moved, 1)

            @block.tensor
            def _(pe):
                pe.wait_ge(w_in, 48)
                with pe.Fori(0, B) as b:
                    pe.wait_ge(b_in, (b + 1) * 80)
                    for qt in range(QT + 2):
                        if qt < QT:
                            pe.wait_ge(exp_done, b * QT + qt)
                            n = (qt + 1) * 128
                            for k0 in range(0, n, CH):
                                w = min(CH, n - k0)
                                last = nc.tensor.matmul(pS[:, k0:k0 + w], qT[:, qt * 128:(qt + 1) * 128], kT[:, k0:k0 + w], start=True, stop=True)
                            last.then_inc(s_psum, 1)
                        if 2 <= qt:
                            t = qt - 2
                            pe.wait_ge(mix_ready, b * QT + t + 1)
                            for hlf in range(2):
                                n = uses["m", t, hlf]
                                pe.wait_ge(pT_moved, b * PER_B + max(0, n - 1))
                                src = mixed[:, t % 2, :, :].rearrange("p e d -> p (e d)")
                                for i in range(4):
                                    m = 4 * hlf + i
                                    last = nc.tensor.transpose(pT[:, n % 2, i * 128:(i + 1) * 128], src[:, m * 128:(m + 1) * 128], ident[:])
                                last.then_inc(pT_psum, 1)
                        if 1 <= qt <= QT:
                            t = qt - 1
                            pe.wait_ge(exp_done, b * QT + t + 1)
                            groups = GRPS[t]
                            for g in range(groups + 1):
                                if g < groups:
                                    n = uses["p", t, g]
                                    pe.wait_ge(pT_moved, b * PER_B + max(0, n - 1))
                                    for i in range(min(GRP, t + 1 - g * GRP)):
                                        kt = g * GRP + i
                                        last = nc.tensor.transpose(pT[:, n % 2, i * 128:(i + 1) * 128], probs[:, t % 2, kt * 128:(kt + 1) * 128], ident[:])
                                    last.then_inc(pT_psum, 1)
                                if g >= 1:
                                    n = uses["p", t, g - 1]
                                    pe.wait_ge(pT_moved, b * PER_B + n + 1)
                                    if g == 1:
                                        pe.wait_ge(attn_ready, b * QT + t)
                                    for i in range(min(GRP, t + 1 - (g - 1) * GRP)):
                                        kt = (g - 1) * GRP + i
                                        last = nc.tensor.matmul(pA[:, 0:HD], probsT[:, n % 2, i * 128:(i + 1) * 128], v[:, kt, :], start=(kt == 0), stop=(kt == t))
                            last.then_inc(attn_psum, 1)
                        if 2 <= qt:
                            t = qt - 2
                            pe.wait_ge(pT_moved, b * PER_B + uses["m", t, 1] + 1)
                            pe.wait_ge(x_ready, b * QT + t)
                            for m in range(KO):
                                last = nc.tensor.matmul(pO[:, 0:D], mixedT[:, m, :], w_o[:, m, :], start=(m == 0), stop=(m == KO - 1))
                            last.then_inc(o_psum, 1)
        s.clear()

NH, NKV, HW = 16, 4, 16
KVD = NKV * HW


def rotary_front(nc, a):
    with Scope(nc, "rot") as s:
        NQ = D // 128
        ROWS = [128] * NQ + [KVD]
        NPC = len(ROWS)
        ident, mhalf = s.sb("ident", [128, 128]), s.sb("mhalf", [128, TPC])
        w_qk = s.sb("w_qk", [128, KD, 2 * (D + KVD)])
        w_v, b_v = s.sb("w_v", [128, KD, KVD]), s.sb("b_v", [128, KVD])
        b_qk = s.sb("b_qk", [128, 2 * NPC])
        cos, sin = s.sb("cos", [128, L]), s.sb("sin", [128, L])
        x, xh = s.sb("x", [128, 2, TPC, D]), s.sb("xh", [128, TPC, D])
        st, var, rstd = s.sb("st", [128, TPC, 8]), s.sb("var", [128, TPC]), s.sb("rstd", [128, TPC])
        xT = s.sb("xT", [128, KD, CH])
        straight, crossed, q, rest = (s.sb(n, [128, NPC, CH]) for n in ("straight", "crossed", "q", "rest"))
        part = [s.sb(f"part{i}", [128, NPC, CH], BF16) for i in range(3)]
        v = s.sb("v", [128, TPC, KVD])
        pP = s.ps("pP", [128, 4, CH])
        pT = s.ps("pT", [128, KD, CH])
        pV = s.ps("pV", [128, CH])

        w_in = s.sem("w_in")
        x_in = [s.sem("x_in_even"), s.sem("x_in_odd")]
        (dve_sem, half_set, var_ready, rstd_ready, xh_ready, xT_psum, xT_ready, p_psum, straight_ready, crossed_ready,
         q_ready, part0, part1, rest_ready, part2, v_psum, v_ready, parts_out, v_out) = (s.sem(n) for n in (
             "dve_sem", "half_set", "var_ready", "rstd_ready", "xh_ready", "xT_psum", "xT_ready", "p_psum", "straight_ready",
             "crossed_ready", "q_ready", "part0", "part1", "rest_ready", "part2", "v_psum", "v_ready", "parts_out", "v_out"))
        x_view, v_view = (a[n].rearrange("(n p) d -> p n d", p=128) for n in ("x2", "v1"))
        W = D + KVD
        NW = 9
        NOUT = 3 * (NQ + 1)

        with nc.Block() as block:
            @block.sync
            def _(sp):
                sp.dma_start(x[:, 0, :, :], x_view[:, 0:TPC, :]).then_inc(x_in[0], 16)
                for dst, src in ((ident[:], a["ident"]), (w_qk[:, 0, :], a["w_qk"][0:128, :]), (w_qk[:, 1, :], a["w_qk"][128:256, :]),
                                 (w_v[:, 0, :], a["w_v"][0:128, :]), (w_v[:, 1, :], a["w_v"][128:256, :]),
                                 (b_v[:], a["b_v"].broadcast_to([128, KVD])), (b_qk[:], a["b_qk"]), (cos[:], a["cos"]), (sin[:], a["sin"])):
                    sp.dma_start(dst, src).then_inc(w_in, 16)
                with sp.Fori(0, NCH // 2) as pair:
                    for par in range(2):
                        c = pair * 2 + par
                        if par == 0:
                            sp.wait_ge(xh_ready, c)
                            sp.dma_start(x[:, 1, :, :], x_view[:, ds((c + 1) * TPC, TPC), :]).then_inc(x_in[1], 16)
                        else:
                            sp.wait_ge(xh_ready, c)
                            sp.dma_start(x[:, 0, :, :], x_view[:, ds(((c + 1) % NCH) * TPC, TPC), :]).then_inc(x_in[0], 16)
                        sp.wait_ge(v_ready, (c + 1) * TPC)
                        sp.dma_start(v_view[:, ds(c * TPC, TPC), :], v[:]).then_inc(v_out, 16)
                        sp.wait_ge(part0, (c + 1) * NPC)
                        sp.wait_ge(part1, (c + 1) * NPC)
                        sp.wait_ge(part2, (c + 1) * NPC)
                        for i in range(3):
                            for m in range(NQ):
                                sp.dma_start(a["q_parts"][i, m * 128:(m + 1) * 128, ds(c * CH, CH)], part[i][:, m, :]).then_inc(parts_out, 16)
                            sp.dma_start(a["k_parts"][i, :, ds(c * CH, CH)], part[i][0:KVD, NQ, :]).then_inc(parts_out, 16)
                sp.wait_ge(x_in[0], 16 * (NCH // 2 + 1))
                sp.wait_ge(v_out, 16 * NCH)
                sp.wait_ge(parts_out, 16 * NOUT * NCH)

            @block.gpsimd
            def _(pool):
                nc.gpsimd.memset(mhalf[:], -0.5).then_inc(half_set, 1)
                pool.wait_ge(half_set, 1)

                def root(c):
                    pool.wait_ge(var_ready, c + 1)
                    nc.gpsimd.tensor_tensor(rstd[:], var[:], mhalf[:], ALU.pow).then_inc(rstd_ready, 1)

                def add(c):
                    for m, r in enumerate(ROWS):
                        pool.wait_ge(crossed_ready, c * NPC + m + 1)
                        pool.wait_ge(rest_ready, c * NPC)
                        nc.gpsimd.tensor_tensor(q[0:r, m, :], straight[0:r, m, :], crossed[0:r, m, :], ALU.add).then_inc(q_ready, 1)

                with pool.Fori(0, NCH) as c:
                    root(c)
                    add(c)

            @block.vector
            def _(dve):
                LN = CHUNK_LN_MARKS
                dve.wait_ge(w_in, 16 * NW)
                with dve.Fori(0, NCH // 2) as pair:
                    for par in range(2):
                        c = pair * 2 + par
                        ch = Chain(dve, dve_sem, c * LN)
                        dve.wait_ge(x_in[par], (pair + 1) * 16)
                        dve.wait_ge(xT_psum, c)
                        chunk_layernorm(nc, ch, x[:, par, :, :], xh, st, var, rstd, var_ready, rstd_ready, c + 1)
                        ch.wait()
                        dve.sem_inc(xh_ready, 1)
                        t0 = (pair % (CPB // 2)) * 2 * CH + par * CH
                        dve.wait_ge(q_ready, c * NPC)
                        for m, r in enumerate(ROWS):
                            for w, (dst, table, done) in enumerate(((straight, cos, straight_ready), (crossed, sin, crossed_ready))):
                                n = 2 * m + w
                                dve.wait_ge(p_psum, c * 2 * NPC + n + 1)
                                nc.vector.scalar_tensor_tensor(dst[0:r, m, :], pP[0:r, n % 4, :], b_qk[0:r, w * NPC + m:w * NPC + m + 1],
                                                               table[0:r, ds(t0, CH)], ALU.add, ALU.mult).then_inc(done, 1)
                        dve.wait_ge(v_psum, c + 1)
                        dve.wait_ge(v_out, c * 16)
                        for j in range(TPC):
                            nc.vector.tensor_tensor(v[:, j, :], pV[:, j * KVD:(j + 1) * KVD], b_v[:], ALU.add).then_inc(v_ready, 1)
                        dve.wait_ge(parts_out, c * 16 * NOUT)
                        for m, r in enumerate(ROWS):
                            dve.wait_ge(part0, c * NPC + m + 1)
                            nc.vector.tensor_tensor(rest[0:r, m, :], q[0:r, m, :], part[0][0:r, m, :], ALU.subtract).then_inc(rest_ready, 1)
                        for m, r in enumerate(ROWS):
                            dve.wait_ge(part1, c * NPC + m + 1)
                            nc.vector.tensor_tensor(part[2][0:r, m, :], rest[0:r, m, :], part[1][0:r, m, :], ALU.subtract).then_inc(part2, 1)

            @block.scalar
            def _(act):
                with act.Fori(0, NCH // 2) as pair:
                    for par in range(2):
                        c = pair * 2 + par
                        act.wait_ge(xT_psum, c + 1)
                        act.wait_ge(v_psum, c)
                        for k in range(KD):
                            nc.scalar.activation(xT[:, k, :], pT[:, k, :], ACT.Copy).then_inc(xT_ready, 1)
                        act.wait_ge(parts_out, c * 16 * NOUT)
                        for m, r in enumerate(ROWS):
                            act.wait_ge(q_ready, c * NPC + m + 1)
                            nc.scalar.activation(part[0][0:r, m, :], q[0:r, m, :], ACT.Copy).then_inc(part0, 1)
                        for m, r in enumerate(ROWS):
                            act.wait_ge(rest_ready, c * NPC + m + 1)
                            nc.scalar.activation(part[1][0:r, m, :], rest[0:r, m, :], ACT.Copy).then_inc(part1, 1)

            @block.tensor
            def _(pe):
                pe.wait_ge(w_in, 16 * NW)
                with pe.Fori(0, NCH) as c:
                    pe.wait_ge(xh_ready, c + 1)
                    pe.wait_ge(xT_ready, c * KD)
                    for j in range(TPC):
                        for k in range(KD):
                            last = nc.tensor.transpose(pT[:, k, j * 128:(j + 1) * 128], xh[:, j, k * 128:(k + 1) * 128], ident[:])
                    last.then_inc(xT_psum, 1)
                    pe.wait_ge(xT_ready, (c + 1) * KD)
                    for m, r in enumerate(ROWS):
                        for w, done in enumerate((straight_ready, crossed_ready)):
                            n = 2 * m + w
                            if n < 4:
                                pe.wait_ge(done, c * NPC)
                            else:
                                pe.wait_ge(done, c * NPC + m - 1)
                            for k in range(KD):
                                last = nc.tensor.matmul(pP[0:r, n % 4, :], w_qk[:, k, w * W + m * 128:w * W + m * 128 + r], xT[:, k, :], start=(k == 0), stop=(k == KD - 1))
                            last.then_inc(p_psum, 1)
                    pe.wait_ge(v_ready, c * TPC)
                    for j in range(TPC):
                        for k in range(KD):
                            last = nc.tensor.matmul(pV[:, j * KVD:(j + 1) * KVD], xT[:, k, j * 128:(j + 1) * 128], w_v[:, k, :], start=(k == 0), stop=(k == KD - 1))
                    last.then_inc(v_psum, 1)
        s.clear()

def full_attention(nc, a):
    G = NH // NKV
    QC = L // CH
    KT = L // TILE
    NB = B * NKV
    RUNS = ((0, 3), (1, 2), (2, 1))
    COMBOS = [(qp, kp) for qp, n in RUNS for kp in range(n)]
    ROWS = len(COMBOS) * HW
    PARTS = 3
    SCALE = float(HW) ** -0.5
    NM = 3

    next_pass = []
    for h in range(G):
        for n in range(16):
            if n == 8 and h:
                next_pass.append(("row", h - 1))
            next_pass.append(("max", h, n // 4, n % 4))
    NP = len(next_pass)
    OUT_AT = 7
    ROW_AT = [next_pass.index(("row", h)) for h in range(G - 1)]
    PER_UNIT = NP + 2
    assert (2 * NP + 1) % NM == 0 and PER_UNIT % NM == 0 and OUT_AT < ROW_AT[0]

    def unit_items(first, last):
        items = [("row", G - 1)]
        if not last:
            items += next_pass
        if not first:
            items.insert(1 if last else OUT_AT, ("out",))
        return items

    def items_before(u):
        if isinstance(u, int):
            return NP if u == 0 else 2 * NP + 1 + PER_UNIT * (u - 1)
        return u * PER_UNIT + (2 * NP + 1 - PER_UNIT)

    with Scope(nc, "attn") as s:
        ident, ident_bf = s.sb("ident", [128, 128]), s.sb("ident_bf", [128, 128], BF16)
        k_max, k_exp = s.sb("k_max", [ROWS, 2, L], BF16), s.sb("k_exp", [ROWS + PARTS, 2, L], BF16)
        v = s.sb("v", [128, 2, KT, 32])
        q = s.sb("q", [ROWS + PARTS, QC, G, CH], BF16)
        probs = s.sb("probs", [128, 2, G, CH])
        part_max = s.sb("part_max", [128, G, 4, 4])
        peak, rest = s.sb("peak", [128, G, 4]), s.sb("rest", [128, G, 4])
        peak_parts = s.sb("peak_parts", [128, G, 4, PARTS], BF16)
        o_rows = s.sb("o_rows", [128, CH])
        inv = s.sb("inv", [128, 4, G])
        ctx = s.sb("ctx", [128, 4, G, HW])
        pE = s.ps("pE", [128, G, CH])
        pM = s.ps("pM", [128, NM, CH])
        pA = s.ps("pA", [128, CH])

        ident_made = s.sem("ident_made")
        const_in, ones_set, ctx_out = (s.sem(n) for n in ("const_in", "ones_set", "ctx_out"))
        kmax_in, kexp_in, v_in = ([s.sem(f"{n}_{par}") for par in ("even", "odd")] for n in ("kmax_in", "kexp_in", "v_in"))
        q_in = [s.sem(f"q_in{qc}") for qc in range(QC)]
        e_psum, exp_done, pv_done, o_moved, m_psum, m_free, parts_ready, split_sem, inv_ready, ctx_ready = (s.sem(n) for n in (
            "e_psum", "exp_done", "pv_done", "o_moved", "m_psum", "m_free", "parts_ready", "split_sem", "inv_ready", "ctx_ready"))
        v_view = a["v1"].rearrange("(n p) d -> p n d", p=128)
        ctx_view = a["ctx"].rearrange("(n p) d -> p n d", p=128)

        def at_least(eng, sem, value):
            if not isinstance(value, int) or value > 0:
                eng.wait_ge(sem, value)

        def every_bg(eng, body):
            def both(pair, first, last):
                for par in range(2):
                    body(pair * 2 + par, pair, par, first and par == 0, last and par == 1)
            both(0, True, False)
            with eng.Fori(1, NB // 2 - 1) as pair:
                both(pair, False, False)
            both(NB // 2 - 1, False, True)

        with nc.Block() as block:
            @block.sync
            def _(sp):
                def load_k(dst, sem, bg, par):
                    b, g = bg // NKV, bg % NKV
                    row = 0
                    for _, n in RUNS:
                        src = a["k_parts"][0:n, ds(g * HW, HW), ds(b * L, L)]
                        sp.dma_start(dst[row:row + n * HW, par, :], src).then_inc(sem[par], 16)
                        row += n * HW

                def load_v(bg, par):
                    b, g = bg // NKV, bg % NKV
                    sp.dma_start(v[:, par, :, 0:HW], v_view[:, ds(b * KT, KT), ds(g * HW, HW)]).then_inc(v_in[par], 16)

                def load_q(bg, qc):
                    b, g = bg // NKV, bg % NKV
                    for i, (qp, _) in enumerate(COMBOS):
                        src = a["q_parts"][qp, ds(g * G * HW, G * HW), ds(b * L + qc * CH, CH)].rearrange("(h r) t -> r h t", h=G)
                        sp.dma_start(q[i * HW:(i + 1) * HW, qc, :, :], src).then_inc(q_in[qc], 16)

                def store(u_end, bg, qc):
                    b, g = bg // NKV, bg % NKV
                    sp.wait_ge(ctx_ready, u_end)
                    sp.dma_start(ctx_view[:, ds(b * KT + qc * 4, 4), ds(g * G * HW, G * HW)], ctx[:].rearrange("p j h d -> p j (h d)")).then_inc(ctx_out, 16)

                load_q(0, 0)
                load_k(k_max, kmax_in, 0, 0)
                sp.dma_start(ident[:], a["ident"]).then_inc(const_in, 16)
                load_k(k_exp, kexp_in, 0, 0)
                load_q(0, 1)
                sp.wait_ge(ones_set, 2)
                load_v(0, 0)

                def body(bg, pair, par, first, last):
                    for qc in range(QC):
                        u = bg * QC + qc
                        if not (first and qc == 0):
                            sp.wait_ge(e_psum, u * 2 * KT)
                        if not (last and qc >= QC - 2):
                            load_q(bg if qc < QC - 2 else bg + 1, (qc + 2) % QC)
                        if qc == 0 and not last:
                            at_least(sp, m_psum, items_before(u) - NP)
                            load_k(k_max, kmax_in, bg + 1, 1 - par)
                            load_k(k_exp, kexp_in, bg + 1, 1 - par)
                            at_least(sp, pv_done, u * KT)
                            load_v(bg + 1, 1 - par)
                        if not (first and qc == 0):
                            store(u, bg if qc else bg - 1, qc - 1 if qc else QC - 1)
                    if last:
                        store(NB * QC, bg, QC - 1)

                every_bg(sp, body)
                sp.wait_ge(ctx_out, 16 * NB * QC)

            @block.gpsimd
            def _(pool):
                nc.gpsimd.memset(v[:], 0.0).then_inc(ones_set, 1)
                pool.wait_ge(ones_set, 1)
                nc.gpsimd.memset(v[:, :, :, HW:HW + 1], 1.0).then_inc(ones_set, 1)
                pool.wait_ge(ones_set, 2)
                nc.gpsimd.memset(k_exp[ROWS:ROWS + PARTS, :, :], 1.0).then_inc(ones_set, 1)

            @block.scalar
            def _(act):
                def body(bg, pair, par, first, last):
                    for qc in range(QC):
                        u = bg * QC + qc
                        for kt in range(KT):
                            for hp in range(2):
                                act.wait_ge(e_psum, u * 2 * KT + 2 * kt + hp + 1)
                                if hp == 0:
                                    at_least(act, pv_done, u * KT + kt - 1)
                                nc.scalar.activation(probs[:, kt % 2, 2 * hp:2 * hp + 2, :], pE[:, 2 * hp:2 * hp + 2, :], ACT.Exp, scale=SCALE).then_inc(exp_done, 1)
                            if kt == 0 and not (first and qc == 0):
                                move_out(u - 1, first and qc == 1, False)
                    if last:
                        move_out(NB * QC - 1, False, True)

                def move_out(u, first, last):
                    act.wait_ge(pv_done, (u + 1) * KT)
                    if not first:
                        act.wait_ge(m_psum, items_before(u) + (1 if last else OUT_AT) + 1)
                    nc.scalar.activation(o_rows[:], pA[:], ACT.Copy).then_inc(o_moved, 1)

                every_bg(act, body)

            @block.vector
            def _(dve):
                SPLITS = 4

                def split_step(i, h, u, n):
                    if i == 0:
                        dve.wait_ge(m_free, n + 1)
                        ins = nc.vector.reduce_max(peak[:, h, :], part_max[:, h, :, :], AXIS_X)
                    else:
                        dve.wait_ge(split_sem, (u * G + h) * SPLITS + i)
                        if i == 1:
                            ins = nc.vector.tensor_scalar(peak_parts[:, h, :, 0], peak[:, h, :], -1.0, None, ALU.mult)
                        elif i == 2:
                            ins = nc.vector.scalar_tensor_tensor(rest[:, h, :], peak[:, h, :], -1.0, peak_parts[:, h, :, 0], ALU.mult, ALU.subtract)
                        elif i == 3:
                            ins = nc.vector.tensor_scalar(peak_parts[:, h, :, 1], rest[:, h, :], 1.0, None, ALU.mult)
                        else:
                            ins = nc.vector.tensor_tensor(peak_parts[:, h, :, 2], rest[:, h, :], peak_parts[:, h, :, 1], ALU.subtract)
                    ins.then_inc(split_sem if i < SPLITS else parts_ready, 1)

                def take(item, slot, n, u, par):
                    dve.wait_ge(m_psum, n + 1)
                    if item[0] == "max":
                        _, h, j, kc = item
                        nc.vector.reduce_max(part_max[:, h, j, kc:kc + 1], pM[:, slot, :], AXIS_X).then_inc(m_free, 1)
                        step = 4 * j + kc
                        if h and step <= SPLITS:
                            split_step(step, h - 1, u, n - 1 - step)
                        if h == G - 1 and step == 15:
                            for i in range(SPLITS + 1):
                                split_step(i, h, u, n)
                    elif item[0] == "row":
                        nc.vector.tensor_copy(q[ROWS:ROWS + PARTS, par, item[1], :], pM[ROWS:ROWS + PARTS, slot, :]).then_inc(m_free, 1)
                    else:
                        out(slot, u)

                def out(slot, u):
                    heads = pM[:, slot, :].rearrange("p (j h d) -> p j h d", j=4, h=G)
                    nc.vector.reciprocal(inv[:], heads[:, :, :, HW]).then_inc(inv_ready, 1)
                    dve.wait_ge(inv_ready, u + 1)
                    at_least(dve, ctx_out, u * 16)
                    nc.vector.tensor_tensor(ctx[:], heads[:, :, :, 0:HW], inv[:].unsqueeze(3).broadcast_to([128, 4, G, HW]), ALU.mult).then_inc(ctx_ready, 1)
                    dve.wait_ge(ctx_ready, u + 1)
                    dve.sem_inc(m_free, 1)

                dve.wait_ge(const_in, 16)
                nc.vector.tensor_copy(ident_bf[:], ident[:]).then_inc(ident_made, 1)
                for n, item in enumerate(next_pass):
                    take(item, n % NM, n, 0, 0)

                def body(bg, pair, par, first, last):
                    for qc in range(QC):
                        u = bg * QC + qc
                        start, end = first and qc == 0, last and qc == QC - 1
                        slot0 = NP % NM if start else 0
                        for i, item in enumerate(unit_items(start, end)):
                            of = u if i == 0 else u - 1 if item[0] == "out" else u + 1
                            take(item, (slot0 + i) % NM, items_before(u) + i, of, qc if i == 0 else (qc + 1) % QC)
                        if end:
                            take(("out",), 2, items_before(u) + 2, u, 0)

                every_bg(dve, body)

            @block.tensor
            def _(pe):
                def give(item, slot, n, u, par, qc):
                    at_least(pe, m_free, n - NM + 1)
                    if item[0] == "max":
                        _, h, j, kc = item
                        nc.tensor.matmul(pM[:, slot, :], q[0:ROWS, qc, h, j * 128:(j + 1) * 128], k_max[0:ROWS, par, kc * CH:(kc + 1) * CH], start=True, stop=True).then_inc(m_psum, 1)
                    elif item[0] == "row":
                        h = item[1]
                        pe.wait_ge(parts_ready, u * G + h + 1)
                        for j in range(4):
                            last = nc.tensor.matmul(pM[ROWS:ROWS + PARTS, slot, j * 128:(j + 1) * 128], peak_parts[:, h, j, :], ident_bf[:], start=True, stop=True)
                        last.then_inc(m_psum, 1)
                    else:
                        pe.wait_ge(o_moved, u + 1)
                        for j in range(4):
                            last = nc.tensor.transpose(pM[:, slot, j * 128:(j + 1) * 128], o_rows[:, j * 128:(j + 1) * 128], ident[:])
                        last.then_inc(m_psum, 1)

                def sums(u, kt, par):
                    pe.wait_ge(exp_done, u * 2 * KT + 2 * kt + 2)
                    if kt == 0:
                        at_least(pe, o_moved, u)
                    for h in range(G):
                        last = nc.tensor.matmul(pA[32 * h:32 * h + 32, :], v[:, par, kt, :], probs[:, kt % 2, h, :], start=(kt == 0), stop=(kt == KT - 1))
                    last.then_inc(pv_done, 1)

                pe.wait_ge(const_in, 16)
                pe.wait_ge(ident_made, 1)
                pe.wait_ge(q_in[0], 16 * len(COMBOS))
                pe.wait_ge(kmax_in[0], 16 * len(RUNS))
                for n, item in enumerate(next_pass):
                    give(item, n % NM, n, 0, 0, 0)
                pe.wait_ge(ones_set, 3)

                def body(bg, pair, par, first, last):
                    for qc in range(QC):
                        u = bg * QC + qc
                        start, end = first and qc == 0, last and qc == QC - 1
                        n0, slot0 = items_before(u), NP % NM if start else 0
                        items = list(enumerate(unit_items(start, end)))
                        nbg = par if qc < QC - 1 else 1 - par

                        def give_next(count):
                            for i, item in items[:count]:
                                of = u if i == 0 else u - 1 if item[0] == "out" else u + 1
                                if i == 1 and item[0] == "max":
                                    pe.wait_ge(q_in[(qc + 1) % QC], (bg + (1 if qc < QC - 1 else 2)) * 16 * len(COMBOS))
                                    if qc == QC - 1:
                                        pe.wait_ge(kmax_in[nbg], (pair + (1 if par == 0 else 2)) * 16 * len(RUNS))
                                give(item, (slot0 + i) % NM, n0 + i, of, nbg, qc if i == 0 else (qc + 1) % QC)
                            del items[:count]

                        def scores(kt, hp):
                            at_least(pe, exp_done, u * 2 * KT + 2 * kt + hp - 1)
                            for h in (2 * hp, 2 * hp + 1):
                                last_mm = nc.tensor.matmul(pE[:, h, :], k_exp[:, par, kt * 128:(kt + 1) * 128], q[:, qc, h, :], start=True, stop=True)
                            last_mm.then_inc(e_psum, 1)

                        for kt in range(KT):
                            if kt == 0:
                                pe.wait_ge(m_free, n0 - NP + ROW_AT[1] + 1)
                                pe.wait_ge(kexp_in[par], (pair + 1) * 16 * len(RUNS))
                            scores(kt, 0)
                            give_next(1 if end else 2)
                            if kt == 0:
                                if not start:
                                    sums(u - 1, KT - 1, par if qc else 1 - par)
                                pe.wait_ge(v_in[par], (pair + 1) * 16)
                                pe.wait_ge(m_free, n0 + 1)
                            scores(kt, 1)
                            give_next(0 if end else 1)
                            if kt:
                                sums(u, kt - 1, par)
                            give_next(0 if end else 2 if kt <= 5 else 1)
                        assert not items
                    if last:
                        sums(u, KT - 1, par)
                        give(("out",), 2, n0 + 2, u, 0, 0)

                every_bg(pe, body)
        s.clear()

BOT, RD, NK, TOP, UH = 128, 48, 1024, 8, 64


def key_lookup(nc, a):
    KV = NK // 128
    GONE = -3.0e38
    with Scope(nc, "look") as s:
        ident, ones, mhalf = s.sb("ident", [128, 128]), s.sb("ones", [128, 128]), s.sb("mhalf", [128, TPC])
        w_o, b_o = s.sb("w_o", [128, KD, D]), s.sb("b_o", [128, D])
        w_q, w_r = s.sb("w_q", [128, KD, BOT]), s.sb("w_r", [128, RD])
        keysT, values = s.sb("keysT", [128, NK]), s.sb("values", [128, KV, D])
        w_u1, b_u1, w_u2 = s.sb("w_u1", [128, KD, UH]), s.sb("b_u1", [UH, 1]), s.sb("w_u2", [UH, 1])
        scalars = s.sb("scalars", [128, 3])
        rk, rq = s.sb("rk", [RD + 1, NK]), s.sb("rq", [64, CH])
        ctx, x2 = s.sb("ctx", [128, TPC, D]), s.sb("x2", [128, TPC, D])
        ctxT, xT = s.sb("ctxT", [128, KD, CH]), s.sb("xT", [128, KD, CH])
        x3, xh = s.sb("x3", [128, TPC, D]), s.sb("xh", [128, TPC, D])
        st, var, rstd, st_h = s.sb("st", [128, TPC, 8]), s.sb("var", [128, TPC]), s.sb("rstd", [128, TPC]), s.sb("st_h", [128, TPC, 6])
        query, h1 = s.sb("query", [BOT, CH]), s.sb("h1", [UH, CH])
        top, ntop = s.sb("top", [128, 2, TOP]), s.sb("ntop", [128, 2])
        left, expd, weight = s.sb("left", [128, NK]), s.sb("expd", [128, 2, NK]), s.sb("weight", [128, 2, NK])
        wsum, winv = s.sb("wsum", [128, 2]), s.sb("winv", [128, 2])
        weightT = s.sb("weightT", [128, KV, TILE])
        sum_all, look_all = s.sb("sum_all", [128, NT, D]), s.sb("look_all", [128, NT, D])
        stats_all, learned_all = s.sb("stats_all", [128, NT, 6]), s.sb("learned_all", [128, NT])
        mean_v, var_v, tmp_v, logv, gate = (s.sb(n, [128, NT]) for n in ("mean_v", "var_v", "tmp_v", "logv", "gate"))
        logsum = s.sb("logsum", [128, 1])
        result = s.sb("result", [128, 2, TPC, D])

        pS = s.ps("pS", [128, 2, NK])
        pT = s.ps("pT", [128, 2, CH])
        pL, pX = s.ps("pL", [128, CH]), s.ps("pX", [128, CH])

        w_in = s.sem("w_in")
        c_in = s.sem("c_in")
        (dve_sem, const_set, biased, var_ready, rstd_ready, xh_ready, t_psum, t_moved, x_psum, x_read, x3_ready,
         query_ready, rq_ready, h1_ready, s_psum, ntop_ready, exp_ready, weight_ready, look_psum, look_ready, s_free) = (s.sem(n) for n in (
             "dve_sem", "const_set", "biased", "var_ready", "rstd_ready", "xh_ready", "t_psum", "t_moved", "x_psum", "x_read", "x3_ready",
             "query_ready", "rq_ready", "h1_ready", "s_psum", "ntop_ready", "exp_ready", "weight_ready", "look_psum", "look_ready", "s_free"))
        rk_psum, rk_moved, logv_ready, lsum_ready, lsum_psum, learn_ready, unc_ready, gate_ready, var_all = (s.sem(n) for n in (
            "rk_psum", "rk_moved", "logv_ready", "lsum_ready", "lsum_psum", "learn_ready", "unc_ready", "gate_ready", "var_all"))
        out_ready, winv_ready = s.sem("out_ready"), s.sem("winv_ready")
        out_done = [s.sem("out_even"), s.sem("out_odd")]

        ctx_view, x2_view, out_view = (a[n].rearrange("(n p) d -> p n d", p=128) for n in ("ctx", "x2", "out"))
        NW = 14
        TPER = TPC + 2
        XPER = 6

        def t_use(c, what):
            if isinstance(c, int) and c == 0 and what in ("ctx", "xh"):
                return 0 if what == "ctx" else 1
            if what in ("ctx", "xh"):
                body = (c - 1) * TPER + 2
                return body + (0 if what == "ctx" else 3)
            body = c * TPER + 2
            if isinstance(c, int) and c == NCH - 1:
                return body + what
            return body + (1, 2, 4, 5)[what]

        with nc.Block() as block:
            @block.sync
            def _(sp):
                two = lambda n: a[n].rearrange("(k p) n -> p k n", p=128)
                for dst, src in ((ident[:], a["ident"]), (w_r[:], a["w_r"]), (keysT[:], a["keysT"]), (rk[RD:RD + 1, :], a["reliability"]),
                                 (w_o[:], two("w_ho")), (b_o[:], a["b_ho"].broadcast_to([128, D])), (w_q[:], two("w_fq")),
                                 (w_u1[:], two("w_u1")), (b_u1[:], a["b_u1"]), (w_u2[:], a["w_u2"]),
                                 (scalars[:, 0:1], a["unc_b2"].broadcast_to([128, 1])), (scalars[:, 1:2], a["gate_w1"].broadcast_to([128, 1])),
                                 (scalars[:, 2:3], a["gate_bias"].broadcast_to([128, 1])), (values[:], two("values"))):
                    sp.dma_start(dst, src).then_inc(w_in, 16)
                with sp.Fori(0, NCH) as c:
                    sp.wait_ge(x3_ready, c * TPC)
                    sp.dma_start(ctx[:], ctx_view[:, ds(c * TPC, TPC), :]).then_inc(c_in, 16)
                    sp.dma_start(x2[:], x2_view[:, ds(c * TPC, TPC), :]).then_inc(c_in, 16)
                with sp.Fori(0, NCH // 2) as pair:
                    for par in range(2):
                        c = pair * 2 + par
                        sp.wait_ge(out_ready, (c + 1) * TPC)
                        sp.dma_start(out_view[:, ds(c * TPC, TPC), :], result[:, par, :, :]).then_inc(out_done[par], 16)
                for par in range(2):
                    sp.wait_ge(out_done[par], 16 * (NCH // 2))

            @block.gpsimd
            def _(pool):
                nc.gpsimd.memset(mhalf[:], -0.5).then_inc(const_set, 1)
                nc.gpsimd.memset(ones[:], 1.0).then_inc(const_set, 1)
                nc.gpsimd.memset(rq[:], 1.0).then_inc(const_set, 1)
                pool.wait_ge(const_set, 3)
                pool.wait_ge(w_in, 16 * NW)
                with pool.Fori(0, NCH) as c:
                    pool.wait_ge(c_in, (c + 1) * 32)
                    nc.gpsimd.tensor_tensor(x2[:], x2[:], b_o[:].unsqueeze(1).broadcast_to([128, TPC, D]), ALU.add).then_inc(biased, 1)
                    pool.wait_ge(var_ready, c + 1)
                    nc.gpsimd.tensor_tensor(rstd[:], var[:], mhalf[:], ALU.pow).then_inc(rstd_ready, 1)

            HEAD = CHUNK_LN_MARKS + TPC + 2
            TILE_MARKS = 3

            @block.vector
            def _(dve):
                def head(c, base):
                    ch = Chain(dve, dve_sem, base)
                    dve.wait_ge(biased, c + 1)
                    for j in range(TPC):
                        dve.wait_ge(x_psum, c * XPER + j // 2 + 1)
                        nc.vector.tensor_tensor(x3[:, j, :], pX[:, (j % 2) * D:(j % 2 + 1) * D], x2[:, j, :], ALU.add).then_inc(x3_ready, 1)
                    dve.wait_ge(x3_ready, (c + 1) * TPC)
                    dve.wait_ge(t_psum, t_use(c, "ctx") + 1)
                    chunk_layernorm(nc, ch, x3, xh, st, var, rstd, var_ready, rstd_ready, c + 1)
                    ch.wait()
                    dve.sem_inc(xh_ready, 1)
                    ch.mark(nc.vector.tensor_tensor(sum_all[:, ds(c * TPC, TPC), :], x3[:], xh[:], ALU.add))
                    for j in range(TPC):
                        ch.mark(nc.vector.bn_stats(st_h[:, j, :], xh[:, j, :]))
                    ch.wait()
                    ch.step(nc.vector.tensor_scalar(stats_all[:, ds(c * TPC, TPC), :], st_h[:], 1.0, None, ALU.mult))
                    assert ch.n == HEAD, ch.n

                def learned(c):
                    dve.wait_ge(x_psum, (c + 1) * XPER)
                    nc.vector.tensor_scalar(learned_all[:, ds(c * TPC, TPC)], pX[:, 0:TPC], 1.0, None, ALU.mult).then_inc(learn_ready, 1)

                def choose(c, j, base):
                    ch = Chain(dve, dve_sem, base)
                    n, b = c * TPC + j, j % 2
                    dve.wait_ge(s_psum, n + 1)
                    nc.vector.memset(wsum[:, b:b + 1], 0.0).then_inc(dve_sem, 1)
                    ch.n += 1
                    ch.step(nc.vector.max(top[:, b, :], pS[:, b, :]))
                    nc.vector.tensor_scalar(ntop[:, b:b + 1], top[:, b, 0:1], -1.0, None, ALU.mult).then_inc(ntop_ready, 1)
                    ch.mark(nc.vector.match_replace(out=left[:], in_to_replace=top[:, b, :], in_values=pS[:, b, :], imm_value=GONE))
                    ch.wait()
                    dve.sem_inc(s_free, 1)
                    dve.wait_ge(exp_ready, n + 1)
                    nc.vector.scalar_tensor_tensor(weight[:, b, :], left[:], GONE, expd[:, b, :], ALU.is_equal, ALU.mult, accum_out=wsum[:, b:b + 1]).then_inc(weight_ready, 1)
                    assert ch.n == TILE_MARKS

                def finish(c, j):
                    n, b = c * TPC + j, j % 2
                    dve.wait_ge(weight_ready, n + 1)
                    nc.vector.reciprocal(winv[:, b:b + 1], wsum[:, b:b + 1]).then_inc(winv_ready, 1)
                    dve.wait_ge(winv_ready, n + 1)
                    dve.wait_ge(look_psum, n + 1)
                    nc.vector.tensor_scalar(look_all[:, ds(n, 1), :], pL[:, 0:D], winv[:, b:b + 1], None, ALU.mult).then_inc(look_ready, 1)

                dve.wait_ge(w_in, 16 * NW)
                for i in range(2):
                    dve.wait_ge(rk_psum, i + 1)
                    nc.vector.tensor_copy(rk[0:RD, i * CH:(i + 1) * CH], (pX, pL)[i][0:RD, :]).then_inc(rk_moved, 1)
                head(0, 0)
                learned(0)
                PER = HEAD + TPC * TILE_MARKS

                def body(c, more, base):
                    choose(c, 0, base)
                    choose(c, 1, base + TILE_MARKS)
                    finish(c, 0)
                    if more:
                        head(c + 1, base + 2 * TILE_MARKS)
                        base = base + HEAD
                    choose(c, 2, base + 2 * TILE_MARKS)
                    finish(c, 1)
                    choose(c, 3, base + 3 * TILE_MARKS)
                    finish(c, 2)
                    finish(c, 3)
                    if more:
                        learned(c + 1)

                with dve.Fori(0, NCH - 1) as c:
                    body(c, True, HEAD + c * PER)
                body(NCH - 1, False, HEAD + (NCH - 1) * PER)
                ch = Chain(dve, dve_sem, HEAD + (NCH - 1) * PER + TPC * TILE_MARKS)
                ch.wait()
                me, mo, ve, vo = (stats_all[:, :, k] for k in (1, 4, 2, 5))
                ch.mark(nc.vector.tensor_tensor(tmp_v[:], me, mo, ALU.subtract))
                ch.step(nc.vector.tensor_tensor(var_v[:], ve, vo, ALU.add))
                ch.mark(nc.vector.tensor_tensor(tmp_v[:], tmp_v[:], tmp_v[:], ALU.mult))
                ch.step(nc.vector.tensor_scalar(var_v[:], var_v[:], 1.0 / D, None, ALU.mult))
                nc.vector.scalar_tensor_tensor(var_v[:], tmp_v[:], 0.25, var_v[:], ALU.mult, ALU.add).then_inc(var_all, 1)
                dve.wait_ge(lsum_psum, 1)
                ch.step(nc.vector.tensor_scalar(logsum[:], pX[:, 0:1], 1.0 / T, 1e-6, ALU.mult, ALU.add))
                ch.step(nc.vector.reciprocal(logsum[:], logsum[:]))
                ch.step(nc.vector.tensor_scalar(logv[:], logv[:], logsum[:, 0:1], 0.5, ALU.mult, ALU.mult))
                dve.wait_ge(unc_ready, 1)
                ch.step(nc.vector.scalar_tensor_tensor(gate[:], gate[:], 2.5, logv[:], ALU.mult, ALU.add))
                nc.vector.tensor_scalar(gate[:], gate[:], 0.0, 5.0, ALU.max, ALU.min).then_inc(unc_ready, 1)
                dve.wait_ge(gate_ready, 1)
                dve.wait_ge(look_ready, NT)
                with dve.Fori(0, NCH // 2) as pair:
                    for par in range(2):
                        c = pair * 2 + par
                        dve.wait_ge(out_done[par], pair * 16)
                        for j in range(TPC):
                            n = c * TPC + j
                            nc.vector.scalar_tensor_tensor(result[:, par, j, :], look_all[:, ds(n, 1), :], gate[:, ds(n, 1)], sum_all[:, ds(n, 1), :], ALU.mult, ALU.add).then_inc(out_ready, 1)

            @block.scalar
            def _(act):
                def move(c, what, dst):
                    n = t_use(c, what)
                    act.wait_ge(t_psum, n + 1)
                    for k in range(2):
                        ins = nc.scalar.activation(dst(k), pT[:, k, :], ACT.Copy)
                    ins.then_inc(t_moved, 1)

                def head(c):
                    act.wait_ge(x_psum, c * XPER + 3)
                    nc.scalar.activation(query[:], pX[:], ACT.Copy).then_inc(query_ready, 1)

                def tail(c):
                    act.wait_ge(x_psum, c * XPER + 4)
                    nc.scalar.activation(rq[0:RD, :], pX[0:RD, :], ACT.Copy, scale=float(RD) ** -0.5).then_inc(rq_ready, 1)
                    act.wait_ge(x_psum, c * XPER + 5)
                    nc.scalar.activation(h1[:], pX[0:UH, :], ACT.Gelu, bias=b_u1[:, 0:1]).then_inc(h1_ready, 1)

                def expo(c, j):
                    n, b = c * TPC + j, j % 2
                    act.wait_ge(ntop_ready, n + 1)
                    act.wait_ge(dve_done_scores, n + 1)
                    nc.scalar.activation(expd[:, b, :], pS[:, b, :], ACT.Exp, bias=ntop[:, b:b + 1]).then_inc(exp_ready, 1)

                dve_done_scores = s_free
                act.wait_ge(w_in, 16 * NW)
                act.wait_ge(const_set, 3)
                move(0, "ctx", lambda k: ctxT[:, k, :])
                move(0, "xh", lambda k: xT[:, k, :])
                head(0)
                tail(0)
                wT = lambda k: weightT[:, 4 * k:4 * k + 4, :]

                def body(c, more):
                    expo(c, 0)
                    if more:
                        move(c + 1, "ctx", lambda k: ctxT[:, k, :])
                    expo(c, 1)
                    move(c, 0, wT)
                    move(c, 1, wT)
                    expo(c, 2)
                    if more:
                        move(c + 1, "xh", lambda k: xT[:, k, :])
                        head(c + 1)
                    expo(c, 3)
                    move(c, 2, wT)
                    move(c, 3, wT)
                    if more:
                        tail(c + 1)

                with act.Fori(0, NCH - 1) as c:
                    body(c, True)
                body(NCH - 1, False)
                act.wait_ge(var_all, 1)
                nc.scalar.activation(logv[:], var_v[:], ACT.Ln, bias=1.0, accum_out=tmp_v[:, 0:1]).then_inc(lsum_ready, 1)
                act.wait_ge(learn_ready, NCH)
                nc.scalar.activation(gate[:], learned_all[:], ACT.Sigmoid, bias=scalars[:, 0:1]).then_inc(unc_ready, 1)
                act.wait_ge(unc_ready, 2)
                nc.scalar.activation(gate[:], gate[:], ACT.Sigmoid, bias=scalars[:, 2:3], scale=scalars[:, 1:2]).then_inc(gate_ready, 1)

            @block.tensor
            def _(pe):
                def flip(c, what, src):
                    n = t_use(c, what)
                    pe.wait_ge(t_moved, n)
                    for i in range(8):
                        last = nc.tensor.transpose(pT[:, i // 4, (i % 4) * 128:(i % 4 + 1) * 128], src(i // 4, i % 4), ident[:])
                    last.then_inc(t_psum, 1)

                def flip_ctx(c):
                    pe.wait_ge(c_in, (c + 1) * 32)
                    flip(c, "ctx", lambda k, j: ctx[:, j, k * 128:(k + 1) * 128])

                def x3_pair(c, hlf):
                    if hlf == 0:
                        pe.wait_ge(t_moved, t_use(c, "ctx") + 1)
                        pe.wait_ge(learn_ready, c)
                    else:
                        pe.wait_ge(x3_ready, c * TPC + 2)
                    for j in (2 * hlf, 2 * hlf + 1):
                        for k in range(KD):
                            last = nc.tensor.matmul(pX[:, (j % 2) * D:(j % 2 + 1) * D], ctxT[:, k, j * 128:(j + 1) * 128], w_o[:, k, :], start=(k == 0), stop=(k == KD - 1))
                    last.then_inc(x_psum, 1)

                def flip_xh(c):
                    pe.wait_ge(xh_ready, c + 1)
                    flip(c, "xh", lambda k, j: xh[:, j, k * 128:(k + 1) * 128])

                def project(c):
                    pe.wait_ge(t_moved, t_use(c, "xh") + 1)
                    pe.wait_ge(x3_ready, (c + 1) * TPC)
                    for k in range(KD):
                        last = nc.tensor.matmul(pX[:], w_q[:, k, :], xT[:, k, :], start=(k == 0), stop=(k == KD - 1))
                    last.then_inc(x_psum, 1)

                def route(c):
                    pe.wait_ge(query_ready, c + 1)
                    nc.tensor.matmul(pX[0:RD, :], w_r[:], query[:], start=True, stop=True).then_inc(x_psum, 1)
                    pe.wait_ge(rq_ready, c + 1)
                    for k in range(KD):
                        last = nc.tensor.matmul(pX[0:UH, :], w_u1[:, k, :], xT[:, k, :], start=(k == 0), stop=(k == KD - 1))
                    last.then_inc(x_psum, 1)

                def learn(c):
                    pe.wait_ge(h1_ready, c + 1)
                    for j in range(TPC):
                        last = nc.tensor.matmul(pX[:, j:j + 1], h1[:, j * 128:(j + 1) * 128], w_u2[:], start=True, stop=True)
                    last.then_inc(x_psum, 1)

                def scores(c, j):
                    n, b = c * TPC + j, j % 2
                    if j >= 2:
                        pe.wait_ge(exp_ready, n - 1)
                    else:
                        pe.wait_ge(exp_ready, c * TPC)
                        pe.wait_ge(rq_ready, c + 1)
                    for i in range(NK // CH):
                        last = nc.tensor.matmul(pS[:, b, i * CH:(i + 1) * CH], rq[0:RD + 1, j * 128:(j + 1) * 128], rk[:, i * CH:(i + 1) * CH], start=True, stop=True)
                    last.then_inc(s_psum, 1)

                def flip_weights(c, j):
                    n, b = c * TPC + j, j % 2
                    pe.wait_ge(weight_ready, n + 1)
                    pe.wait_ge(look_psum, n)
                    flip(c, j, lambda k, i: weight[:, b, (4 * k + i) * 128:(4 * k + i + 1) * 128])

                def lookup(c, j):
                    n = c * TPC + j
                    pe.wait_ge(t_moved, t_use(c, j) + 1)
                    pe.wait_ge(look_ready, n)
                    for k in range(KV):
                        last = nc.tensor.matmul(pL[:, 0:D], weightT[:, k, :], values[:, k, :], start=(k == 0), stop=(k == KV - 1))
                    last.then_inc(look_psum, 1)

                pe.wait_ge(w_in, 16 * NW)
                pe.wait_ge(const_set, 3)
                for i in range(2):
                    nc.tensor.matmul((pX, pL)[i][0:RD, :], w_r[:], keysT[:, i * CH:(i + 1) * CH], start=True, stop=True).then_inc(rk_psum, 1)
                flip_ctx(0)
                pe.wait_ge(rk_moved, 2)
                x3_pair(0, 0)
                x3_pair(0, 1)
                flip_xh(0)
                project(0)
                route(0)
                learn(0)

                def body(c, more):
                    scores(c, 0)
                    scores(c, 1)
                    if more:
                        flip_ctx(c + 1)
                        x3_pair(c + 1, 0)
                    flip_weights(c, 0)
                    lookup(c, 0)
                    scores(c, 2)
                    if more:
                        x3_pair(c + 1, 1)
                    flip_weights(c, 1)
                    lookup(c, 1)
                    scores(c, 3)
                    if more:
                        flip_xh(c + 1)
                        project(c + 1)
                    flip_weights(c, 2)
                    lookup(c, 2)
                    flip_weights(c, 3)
                    lookup(c, 3)
                    if more:
                        route(c + 1)
                        learn(c + 1)

                with pe.Fori(0, NCH - 1) as c:
                    body(c, True)
                body(NCH - 1, False)
                pe.wait_ge(lsum_ready, 1)
                nc.tensor.matmul(pX[:, 0:1], ones[:], tmp_v[:, 0:1], start=True, stop=True).then_inc(lsum_psum, 1)
        s.clear()


def build_program(nc, inputs, out):
    a = dict(inputs)
    a["out"] = out
    for name, shape, dt in (("xr", (T, D), FP32), ("uT", (DI, T), FP32), ("gT", (DI, T), FP32), ("dT", (DI, T), FP32),
                            ("BC", (2 * NS, T), FP32), ("c_split", (3, NS, T), BF16), ("yT", (DI, T), FP32),
                            ("x1", (T, D), FP32), ("rw", (T, NE), FP32), ("qkT", (2 * HD, T), FP32), ("v0", (T, HD), FP32),
                            ("x2", (T, D), FP32), ("q_parts", (3, D, T), BF16), ("k_parts", (3, KVD, T), BF16), ("v1", (T, KVD), FP32),
                            ("ctx", (T, D), FP32)):
        a[name] = nc.dram_tensor(f"mid_{name}", shape, dt, kind="Internal").ap()
    for stage in (mamba_front, selective_scan, expert_front, causal_attention, rotary_front, full_attention, key_lookup):
        stage(nc, a)


def columns(v, parts=128):
    v = np.asarray(v)
    return np.ascontiguousarray(np.swapaxes(v.reshape((-1, parts) + v.shape[1:]), 0, 1))


def lay_out(i):
    g = {k.replace('L0_attn_', 'm_').replace('L0_ffn_', 'e_').replace('L1_attn_', 'h_').replace('L1_ffn_', 'f_'): np.ascontiguousarray(np.asarray(v)) for k, v in i.items()}
    a = {'x': g['m_x'].reshape(-1, 256), 'ident': np.eye(128, dtype=np.float32)}
    a['W_in'], a['W_x'], a['W_dt'], a['W_out'] = g['m_W_in'], g['m_W_x'], g['m_W_dt'], g['m_W_out']
    for n in ('norm_w', 'norm_b', 'conv_b', 'b_dt', 'A_log', 'D'):
        a[n] = columns(g['m_' + n])
    a['conv_w'] = columns(g['m_conv_w'].reshape(512, 4))
    a['part_of'] = np.tile(np.eye(32, 16, dtype=np.float32), (3, 1))
    a['a_log_d'] = np.ascontiguousarray(np.concatenate([columns(g['m_A_log']), columns(g['m_D'])[:, :, None]], axis=2))
    a['sim'] = g['e_sim_matrix']
    a['gates'] = g['e_gates'].reshape(1, 16)
    a['expert_no'] = np.tile(np.arange(16, dtype=np.float32), (128, 1))
    qkv = np.concatenate([g['e_q_proj'], g['e_k_proj'], g['e_v_proj']], axis=2)
    a['w_qkv'] = np.ascontiguousarray(qkv.transpose(1, 0, 2).reshape(256, -1))
    a['w_o'] = g['e_o_proj'].reshape(1024, 256)
    a['above'] = np.triu(np.full((128, 128), -1e30, np.float32), 1)
    place = np.arange(16)
    partner = np.where(place < 8, 2 * place + 1, 2 * (place - 8))
    rows = lambda n: (np.arange(n) // 16) * 16 + partner[np.arange(n) % 16]
    w = [g['h_Wq'], g['h_Wk'], g['h_Wq'][rows(256)], g['h_Wk'][rows(64)]]
    a['w_qk'] = np.ascontiguousarray(np.concatenate(w, axis=0).T)
    a['w_v'] = np.ascontiguousarray(g['h_Wv'].T)
    a['b_v'] = g['h_bv'].reshape(1, 64)
    b_qk = np.zeros((128, 6), np.float32)
    for i, v in enumerate((g['h_bq'][:128], g['h_bq'][128:], g['h_bk'], g['h_bq'][rows(256)][:128], g['h_bq'][rows(256)][128:], g['h_bk'][rows(64)])):
        b_qk[:len(v), i] = v
    a['b_qk'] = b_qk
    freq = (1.0 / np.float32(10000.0) ** (np.arange(0, 16, 2, dtype=np.float32) / np.float32(16))).astype(np.float32)
    turn = (np.arange(2048, dtype=np.float32)[None, :] * freq[np.arange(128) % 8][:, None]).astype(np.float32)
    a['cos'] = np.cos(turn).astype(np.float32)
    a['sin'] = np.sin(turn).astype(np.float32) * np.where(np.arange(128) % 16 < 8, -1, 1).astype(np.float32)[:, None]
    t = lambda v: np.ascontiguousarray(v.T)
    a['w_ho'], a['b_ho'] = t(g['h_Wo']), g['h_bo'].reshape(1, 256)
    a['w_fq'], a['w_r'], a['keysT'] = t(g['f_q_proj_w']), t(g['f_router_w']), t(g['f_aux_keys'])
    a['reliability'], a['values'] = g['f_reliability_mask'].reshape(1, 1024), g['f_aux_values']
    a['w_u1'], a['b_u1'], a['w_u2'] = t(g['f_unc_w1']), g['f_unc_b1'].reshape(64, 1), t(g['f_unc_w2'])
    for n in ('unc_b2', 'gate_w1', 'gate_bias'):
        a[n] = g['f_' + n].reshape(1, 1)
    return a


def kernel(**inputs):
    import concourse.bacc as bacc
    from concourse.bass_utils import run_bass_kernel_spmd

    nc = bacc.Bacc("TRN2", target_bir_lowering=False, num_devices=1)
    arrays = lay_out(inputs)
    tensors = {n: nc.dram_tensor(f"in_{n}", v.shape, mybir.dt.from_np(v.dtype), kind="ExternalInput").ap() for n, v in arrays.items()}
    out = nc.dram_tensor("out_0", (T, D), FP32, kind="ExternalOutput").ap()
    build_program(nc, tensors, out)
    r = run_bass_kernel_spmd(nc, [{f"in_{n}": v for n, v in arrays.items()}], core_ids=[0])
    return r.results[0]["out_0"].reshape(B, L, D)
```

```python
import numpy as np
import concourse.bass as bass
from concourse import mybir
from contextlib import ExitStack

FP32 = mybir.dt.float32
BF16 = mybir.dt.bfloat16
ALU = mybir.AluOpType
ACT = mybir.ActivationFunctionType
AXIS_X = mybir.AxisListType.X
ds = bass.ds

B, L, D = 2, 2048, 256
T = B * L
TILE = 128
NT = T // TILE
CH = 512
TPC = CH // TILE
NCH = T // CH
CPB = L // CH
KD = D // 128
DI, DTR, NS, KC = 512, 64, 16, 4
NDI = DI // 128
EPS = 1e-5


class Chain:

    def __init__(self, eng, sem, base=0):
        self.eng, self.sem, self.base, self.n = eng, sem, base, 0

    def mark(self, ins):
        ins.then_inc(self.sem, 1)
        self.n += 1

    def wait(self):
        self.eng.wait_ge(self.sem, self.base + self.n)

    def step(self, ins):
        self.mark(ins)
        self.wait()


class Scope(ExitStack):

    def __init__(self, nc, name):
        super().__init__()
        self.nc, self.name, self.sems = nc, name, []

    def sb(self, name, shape, dt=FP32):
        return self.enter_context(self.nc.sbuf_tensor(f"{self.name}_{name}", shape, dt))

    def ps(self, name, shape, dt=FP32):
        return self.enter_context(self.nc.psum_tensor(f"{self.name}_{name}", shape, dt))

    def sem(self, name):
        self.sems.append(self.nc.alloc_semaphore(f"{self.name}_{name}"))
        return self.sems[-1]

    def clear(self):
        self.nc.all_engine_barrier()
        self.nc.clear_and_free_semaphores(self.sems)
        self.nc.all_engine_barrier()


def chunk_layernorm(nc, ch, xin, xout, st, pow_in, pow_out, var_ready, rstd_ready, nth):
    for j in range(TPC):
        ch.mark(nc.vector.bn_stats(st[:, j, 0:6], xin[:, j, :]))
    ch.wait()
    me, mo, ve, vo = (st[:, :, k] for k in (1, 4, 2, 5))
    mean, diff = st[:, :, 6], st[:, :, 7]
    ch.mark(nc.vector.tensor_tensor(mean, me, mo, ALU.add))
    ch.mark(nc.vector.tensor_tensor(diff, me, mo, ALU.subtract))
    ch.step(nc.vector.tensor_tensor(pow_in[:, 0:TPC], ve, vo, ALU.add))
    ch.mark(nc.vector.tensor_scalar(mean, mean, 0.5, None, ALU.mult))
    ch.mark(nc.vector.tensor_tensor(diff, diff, diff, ALU.mult))
    ch.step(nc.vector.tensor_scalar(pow_in[:, 0:TPC], pow_in[:, 0:TPC], 1.0 / D, EPS, ALU.mult, ALU.add))
    nc.vector.scalar_tensor_tensor(pow_in[:, 0:TPC], diff, 0.25, pow_in[:, 0:TPC], ALU.mult, ALU.add).then_inc(var_ready, 1)
    ch.eng.wait_ge(rstd_ready, nth)
    for j in range(TPC):
        ch.mark(nc.vector.tensor_scalar(xout[:, j, :], xin[:, j, :], st[:, j, 6:7], pow_out[:, j:j + 1], ALU.subtract, ALU.mult))


CHUNK_LN_MARKS = TPC + 6 + TPC


def at_least(eng, sem, value):
    if not isinstance(value, int) or value > 0:
        eng.wait_ge(sem, value)


def mamba_front(nc, a):
    with Scope(nc, "front") as s:
        x, xh, xr = (s.sb(n, [128, TPC, D]) for n in ("x", "xh", "xr"))
        st = s.sb("st", [128, TPC, 8])
        st2 = s.sb("st2", [128, TPC, 8])
        var, rstd, mhalf = s.sb("var", [128, TPC]), s.sb("rstd", [128, TPC]), s.sb("mhalf", [128, TPC])
        ident = s.sb("ident", [128, 128])
        w_in = s.sb("w_in", [128, KD, 2 * DI])
        w_x = s.sb("w_x", [128, NDI, DTR + 2 * NS])
        w_dt = s.sb("w_dt", [DTR, DI])
        norm_w, norm_b = s.sb("norm_w", [128, KD]), s.sb("norm_b", [128, KD])
        conv_w, conv_b, b_dt = s.sb("conv_w", [128, NDI, KC]), s.sb("conv_b", [128, NDI]), s.sb("b_dt", [128, NDI])
        xn = s.sb("xn", [128, TPC, D])
        xnT = s.sb("xnT", [128, KD, CH])
        xs = s.sb("xs", [128, NDI, KC - 1 + CH])
        xc = s.sb("xc", [128, NDI, CH])
        uT, gT, dT = s.sb("uT", [128, NDI, CH]), s.sb("gT", [128, NDI, CH]), s.sb("dT", [128, NDI, CH])
        xdbl = s.sb("xdbl", [DTR + 2 * NS, CH])
        sp_abs, sp_exp, sp_log, sp_relu = (s.sb(n, [128, NDI, CH]) for n in ("sp_abs", "sp_exp", "sp_log", "sp_relu"))

        pT = s.ps("pT", [128, KD, CH])
        pXZ = s.ps("pXZ", [128, NDI, CH])
        pDBL = s.ps("pDBL", [128, CH])

        x_in, w_loaded, x_stored, out_u, out_g, out_d, out_bc = (s.sem(n) for n in (
            "x_in", "w_loaded", "x_stored", "out_u", "out_g", "out_d", "out_bc"))
        dve_chain, act_chain, tail_ready = s.sem("dve_chain"), s.sem("act_chain"), s.sem("tail_ready")
        half_ready, var_ready, rstd_ready = s.sem("half_ready"), s.sem("var_ready"), s.sem("rstd_ready")
        xh_ready, xr_ready, xn_ready, xnT_psum, xnT_ready = (s.sem(n) for n in (
            "xh_ready", "xr_ready", "xn_ready", "xnT_psum", "xnT_ready"))
        x_proj, z_proj, x_evac, conv_done, u_ready, g_ready = (s.sem(n) for n in (
            "x_proj", "z_proj", "x_evac", "conv_done", "u_ready", "g_ready"))
        dbl_psum, dbl_ready, dt_psum, dt_read, dt_relu, log_ready, d_ready = (s.sem(n) for n in (
            "dbl_psum", "dbl_ready", "dt_psum", "dt_read", "dt_relu", "log_ready", "d_ready"))

        x_view = a["x"].rearrange("(n p) d -> p n d", p=128)
        xr_view = a["xr"].rearrange("(n p) d -> p n d", p=128)
        uT_view, gT_view, dT_view = (a[n].rearrange("(m p) t -> p m t", p=128) for n in ("uT", "gT", "dT"))
        WLOADS = 9

        def every_chunk(eng, body):
            for b in range(B):
                body(b * CPB, True, False)
                with eng.Fori(b * CPB + 1, (b + 1) * CPB - (b == B - 1)) as c:
                    body(c, False, False)
            body(NCH - 1, False, True)

        with nc.Block() as block:
            @block.sync
            def _(sp):
                def load_x(c):
                    sp.dma_start(x[:], x_view[:, ds(c * TPC, TPC), :]).then_inc(x_in, 16)

                def next_x(c, last=False):
                    sp.wait_ge(xr_ready, c + 1)
                    sp.dma_start(xr_view[:, ds(c * TPC, TPC), :], xr[:]).then_inc(x_stored, 16)
                    if not last:
                        load_x(c + 1)

                def store_u(c):
                    sp.wait_ge(u_ready, (c + 1) * NDI)
                    sp.dma_start(uT_view[:, :, ds(c * CH, CH)], uT[:]).then_inc(out_u, 16)
                    sp.wait_ge(g_ready, (c + 1) * NDI)
                    sp.dma_start(gT_view[:, :, ds(c * CH, CH)], gT[:]).then_inc(out_g, 16)
                    sp.wait_ge(dbl_ready, c + 1)
                    sp.dma_start(a["BC"][:, ds(c * CH, CH)], xdbl[DTR:DTR + 2 * NS, :]).then_inc(out_bc, 16)

                def store_d(c):
                    sp.wait_ge(d_ready, c + 1)
                    sp.dma_start(dT_view[:, :, ds(c * CH, CH)], dT[:]).then_inc(out_d, 16)

                load_x(0)
                for dst, src in ((ident[:], a["ident"]), (w_in[:], a["W_in"].rearrange("(k p) n -> p k n", p=128)),
                                 (norm_w[:], a["norm_w"]),
                                 (norm_b[:], a["norm_b"]),
                                 (conv_w[:], a["conv_w"]),
                                 (conv_b[:], a["conv_b"]),
                                 (b_dt[:], a["b_dt"]),
                                 (w_x[:], a["W_x"].rearrange("(m p) n -> p m n", p=128)),
                                 (w_dt[:], a["W_dt"])):
                    sp.dma_start(dst, src).then_inc(w_loaded, 16)
                next_x(0)
                next_x(1)
                store_u(0)
                with sp.Fori(2, NCH - 1) as c:
                    next_x(c)
                    store_d(c - 2)
                    store_u(c - 1)
                next_x(NCH - 1, last=True)
                store_d(NCH - 3)
                store_u(NCH - 2)
                store_d(NCH - 2)
                store_u(NCH - 1)
                store_d(NCH - 1)
                for sem in (x_stored, out_u, out_g, out_bc, out_d):
                    sp.wait_ge(sem, 16 * NCH)

            @block.gpsimd
            def _(pool):
                def first_root(c):
                    pool.wait_ge(var_ready, 2 * c + 1)
                    nc.gpsimd.tensor_tensor(rstd[:], var[:], mhalf[:], ALU.pow).then_inc(rstd_ready, 1)
                    pool.wait_ge(xh_ready, c + 1)
                    at_least(pool, x_stored, c * 16)
                    nc.gpsimd.tensor_tensor(xr[:], x[:], xh[:], ALU.add).then_inc(xr_ready, 1)

                def second_root(c):
                    pool.wait_ge(var_ready, 2 * c + 2)
                    nc.gpsimd.tensor_tensor(rstd[:], var[:], mhalf[:], ALU.pow).then_inc(rstd_ready, 1)

                def delta(c):
                    pool.wait_ge(log_ready, c + 1)
                    pool.wait_ge(dt_relu, (c + 1) * NDI)
                    at_least(pool, out_d, c * 16)
                    nc.gpsimd.tensor_tensor(dT[:], sp_relu[:], sp_log[:], ALU.add).then_inc(d_ready, 1)

                nc.gpsimd.memset(mhalf[:], -0.5).then_inc(half_ready, 1)
                pool.wait_ge(half_ready, 1)
                for c in range(2):
                    first_root(c)
                    second_root(c)
                with pool.Fori(1, NCH - 1) as c:
                    first_root(c + 1)
                    delta(c - 1)
                    second_root(c + 1)
                delta(NCH - 2)
                delta(NCH - 1)

            @block.vector
            def _(dve):
                LN = CHUNK_LN_MARKS
                PER = 2 * LN + NDI * (KC - 1)

                def first_norm(c, base):
                    ch = Chain(dve, dve_chain, base)
                    dve.wait_ge(x_in, (c + 1) * 16)
                    at_least(dve, xr_ready, c)
                    chunk_layernorm(nc, ch, x, xh, st, var, rstd, var_ready, rstd_ready, 2 * c + 1)
                    ch.wait()
                    dve.sem_inc(xh_ready, 1)
                    assert ch.n == LN

                def second_norm(c, base):
                    ch = Chain(dve, dve_chain, base)
                    at_least(dve, xnT_psum, c)
                    chunk_layernorm(nc, ch, xh, xn, st2, var, rstd, var_ready, rstd_ready, 2 * c + 2)
                    ch.wait()
                    dve.sem_inc(xn_ready, 1)

                def convolution(c, base):
                    ch = Chain(dve, dve_chain, base)
                    at_least(dve, u_ready, c * NDI)
                    for m0 in range(0, NDI, 2):
                        for k in range(KC):
                            for m in (m0, m0 + 1):
                                if k == 0:
                                    dve.wait_ge(x_evac, c * NDI + m + 1)
                                    ch.mark(nc.vector.tensor_scalar(xc[:, m, :], xs[:, m, 0:CH], conv_w[:, m, 0:1], conv_b[:, m:m + 1], ALU.mult, ALU.add))
                                else:
                                    dve.wait_ge(dve_chain, ch.base + (m0 // 2) * 2 * (KC - 1) + 2 * (k - 1) + (m - m0) + 1)
                                    ins = nc.vector.scalar_tensor_tensor(xc[:, m, :], xs[:, m, k:k + CH], conv_w[:, m, k:k + 1], xc[:, m, :], ALU.mult, ALU.add)
                                    if k < KC - 1:
                                        ch.mark(ins)
                                    else:
                                        ins.then_inc(conv_done, 1)
                    assert ch.n == NDI * (KC - 1)

                first_norm(0, 0)
                second_norm(0, LN)
                dve.wait_ge(w_loaded, 16 * WLOADS)

                def body(c, start, last):
                    base = 2 * LN + c * PER
                    if start:
                        at_least(dve, conv_done, c * NDI)
                        nc.vector.memset(xs[:, :, 0:KC - 1], 0.0).then_inc(tail_ready, 1)
                    else:
                        dve.wait_ge(conv_done, c * NDI)
                        nc.vector.tensor_copy(xs[:, :, 0:KC - 1], xs[:, :, CH:CH + KC - 1]).then_inc(tail_ready, 1)
                    if not last:
                        first_norm(c + 1, base)
                    else:
                        base = base - LN
                    convolution(c, base + LN)
                    if not last:
                        second_norm(c + 1, base + LN + NDI * (KC - 1))
                    for m in range(NDI):
                        dve.wait_ge(dt_psum, c * NDI + m + 1)
                        if m == 0:
                            at_least(dve, d_ready, c)
                        nc.vector.tensor_scalar(sp_relu[:, m, :], pXZ[:, m, :], b_dt[:, m:m + 1], 0.0, ALU.add, ALU.max).then_inc(dt_relu, 1)

                every_chunk(dve, body)

            @block.scalar
            def _(act):
                def move_in(c):
                    act.wait_ge(xnT_psum, c + 1)
                    at_least(act, z_proj, c * NDI)
                    for k in range(KD):
                        nc.scalar.activation(xnT[:, k, :], pT[:, k, :], ACT.Identity, bias=norm_b[:, k:k + 1], scale=norm_w[:, k:k + 1]).then_inc(xnT_ready, 1)

                def softplus(c):
                    lc = Chain(act, act_chain, c * 2 * NDI)
                    act.wait_ge(dt_read, (c + 1) * NDI)
                    for m in range(NDI):
                        lc.mark(nc.scalar.activation(sp_exp[:, m, :], sp_abs[:, m, :], ACT.Exp, scale=-1.0))
                    lc.wait()
                    at_least(act, d_ready, c)
                    for m in range(NDI):
                        lc.mark(nc.scalar.activation(sp_log[:, m, :], sp_exp[:, m, :], ACT.Ln, bias=1.0))
                    lc.wait()
                    act.sem_inc(log_ready, 1)

                def silu_u(c, m):
                    act.wait_ge(conv_done, c * NDI + m + 1)
                    if m == 0:
                        at_least(act, out_u, c * 16)
                    nc.scalar.activation(uT[:, m, :], xc[:, m, :], ACT.Silu).then_inc(u_ready, 1)

                def silu_z(c, m):
                    act.wait_ge(z_proj, c * NDI + m + 1)
                    if m == 0:
                        at_least(act, out_g, c * 16)
                    nc.scalar.activation(gT[:, m, :], pXZ[:, m, :], ACT.Silu).then_inc(g_ready, 1)

                act.wait_ge(w_loaded, 16 * WLOADS)
                move_in(0)

                def body(c, start, last):
                    for m in range(NDI):
                        act.wait_ge(x_proj, c * NDI + m + 1)
                        if m == 0:
                            act.wait_ge(tail_ready, c + 1)
                        nc.scalar.activation(xs[:, m, KC - 1:], pXZ[:, m, :], ACT.Identity).then_inc(x_evac, 1)
                    if not (isinstance(c, int) and c == 0):
                        softplus(c - 1)
                    for m in range(0, NDI, 2):
                        silu_u(c, m)
                        silu_u(c, m + 1)
                        silu_z(c, m)
                        silu_z(c, m + 1)
                    act.wait_ge(dbl_psum, c + 1)
                    at_least(act, out_bc, c * 16)
                    nc.scalar.activation(xdbl[:], pDBL[0:DTR + 2 * NS, :], ACT.Identity).then_inc(dbl_ready, 1)
                    if not last:
                        move_in(c + 1)
                    for m in range(NDI):
                        act.wait_ge(dt_relu, c * NDI + m + 1)
                        nc.scalar.activation(sp_abs[:, m, :], pXZ[:, m, :], ACT.Abs, bias=b_dt[:, m:m + 1]).then_inc(dt_read, 1)
                    if last:
                        softplus(c)

                every_chunk(act, body)

            @block.tensor
            def _(pe):
                def transposes(c):
                    at_least(pe, xnT_ready, c * KD)
                    pe.wait_ge(xn_ready, c + 1)
                    for j in range(TPC):
                        for k in range(KD):
                            last = nc.tensor.transpose(pT[:, k, j * 128:(j + 1) * 128], xn[:, j, k * 128:(k + 1) * 128], ident[:])
                    last.then_inc(xnT_psum, 1)

                pe.wait_ge(w_loaded, 16 * WLOADS)
                transposes(0)

                def body(c, start, last):
                    pe.wait_ge(xnT_ready, (c + 1) * KD)
                    for m in range(NDI):
                        at_least(pe, dt_read, (c - 1) * NDI + m + 1)
                        for k in range(KD):
                            ins = nc.tensor.matmul(pXZ[:, m, :], w_in[:, k, m * 128:(m + 1) * 128], xnT[:, k, :], start=(k == 0), stop=(k == KD - 1))
                        ins.then_inc(x_proj, 1)
                    for m in range(NDI):
                        pe.wait_ge(x_evac, c * NDI + m + 1)
                        for k in range(KD):
                            ins = nc.tensor.matmul(pXZ[:, m, :], w_in[:, k, DI + m * 128:DI + (m + 1) * 128], xnT[:, k, :], start=(k == 0), stop=(k == KD - 1))
                        ins.then_inc(z_proj, 1)
                    at_least(pe, dbl_ready, c)
                    for m in range(NDI):
                        pe.wait_ge(u_ready, c * NDI + m + 1)
                        ins = nc.tensor.matmul(pDBL[0:DTR + 2 * NS, :], w_x[:, m, :], uT[:, m, :], start=(m == 0), stop=(m == NDI - 1))
                    ins.then_inc(dbl_psum, 1)
                    if not last:
                        transposes(c + 1)
                    pe.wait_ge(dbl_ready, c + 1)
                    for m in range(NDI):
                        pe.wait_ge(g_ready, c * NDI + m + 1)
                        nc.tensor.matmul(pXZ[:, m, :], w_dt[:, m * 128:(m + 1) * 128], xdbl[0:DTR, :], start=True, stop=True).then_inc(dt_psum, 1)

                every_chunk(pe, body)
        s.clear()

def selective_scan(nc, a):
    STEPS = NS * CPB
    ROUNDS = B * NDI
    SPLIT = 3
    NSTATE = 3
    NDBU = 4
    AHEAD = NDBU - 1
    with Scope(nc, "scan") as s:
        b_all = s.sb("b_all", [128, NS, L])
        delta, u = s.sb("delta", [128, 2, L]), s.sb("u", [128, 2, L])
        g, du = s.sb("g", [128, L]), s.sb("du", [128, L])
        a_log, decay = s.sb("a_log", [128, 2, NS + 1]), s.sb("decay", [128, 2, NS])
        c_parts = s.sb("c_parts", [96, L], BF16)
        pick = s.sb("pick", [96, NS, 128], BF16)
        part_of = s.sb("part_of", [96, NS])
        ident = s.sb("ident", [128, 128])
        dbu, h, hc = s.sb("dbu", [128, NDBU, CH]), s.sb("h", [128, NSTATE, CH]), s.sb("hc", [128, 2, CH])
        y_acc = s.ps("y_acc", [128, CPB, CH])
        abar, c_all = s.ps("abar", [128, 2, CH]), s.ps("c_all", [128, 2, CH])

        c_raw, c_rest = h[:, 0, :], h[:, 1, :]
        c_split = dbu[:, 0:2, :].rearrange("p a c -> p (a c)").bitcast(BF16)[:, 0:SPLIT * CH].rearrange("p (i c) -> p i c", i=SPLIT)

        const_in, craw_in, split_done, split_out, cparts_in = (s.sem(n) for n in (
            "const_in", "craw_in", "split_done", "split_out", "cparts_in"))
        b_in = [s.sem(f"b_in{n}") for n in range(NS)]
        du_in = [s.sem("du_in_even"), s.sem("du_in_odd")]
        g_in, y_out = s.sem("g_in"), s.sem("y_out")
        du_ready, dbu_ready, decay_exp, decay_ready = (s.sem(n) for n in (
            "du_ready", "dbu_ready", "decay_exp", "decay_ready"))
        abar_ready, scan_done, c_ready, c_used, hc_added, acc_read, y_half, y_ready, zeroed = (s.sem(n) for n in (
            "abar_ready", "scan_done", "c_ready", "c_used", "hc_added", "acc_read", "y_half", "y_ready", "zeroed"))
        pick_made = s.sem("pick_made")

        dT_view, uT_view, gT_view, yT_view = (a[n].rearrange("(m p) t -> p m t", p=128) for n in ("dT", "uT", "gT", "yT"))
        BC = a["BC"]

        with nc.Block() as block:
            @block.sync
            def _(sp):
                sp.dma_start(c_raw, BC[NS:2 * NS, :].rearrange("n (c t) -> (n c) t", t=CH)).then_inc(craw_in, 16)
                sp.dma_start(part_of[:], a["part_of"]).then_inc(const_in, 16)
                sp.dma_start(ident[:], a["ident"]).then_inc(const_in, 16)
                sp.wait_ge(split_done, 5)
                for i in range(SPLIT):
                    sp.dma_start(a["c_split"][i].rearrange("n (c t) -> (n c) t", t=CH), c_split[:, i, :]).then_inc(split_out, 16)

                def load_round(q):
                    b, m = divmod(q, NDI)
                    sp.dma_start(a_log[:, q % 2, :], a["a_log_d"][:, m, :]).then_inc(du_in[q % 2], 16)
                    sp.dma_start(delta[:, q % 2, :], dT_view[:, m, b * L:(b + 1) * L]).then_inc(du_in[q % 2], 16)
                    sp.dma_start(u[:, q % 2, :], uT_view[:, m, b * L:(b + 1) * L]).then_inc(du_in[q % 2], 16)

                def load_gate(q):
                    b, m = divmod(q, NDI)
                    sp.dma_start(g[:], gT_view[:, m, b * L:(b + 1) * L]).then_inc(g_in, 16)

                def load_b(n, b):
                    sp.dma_start(b_all[:, n, :], BC[n:n + 1, b * L:(b + 1) * L].broadcast_to([128, L])).then_inc(b_in[n], 16)

                def load_c(b):
                    for i in range(SPLIT):
                        sp.dma_start(c_parts[32 * i:32 * i + NS, :], a["c_split"][i, :, b * L:(b + 1) * L]).then_inc(cparts_in, 16)

                load_round(0)
                load_b(0, 0)
                sp.wait_ge(split_out, 16 * SPLIT)
                sp.wait_ge(zeroed, 1)
                load_c(0)
                for n in range(1, NS):
                    load_b(n, 0)
                load_gate(0)
                load_round(1)
                for q in range(ROUNDS):
                    if (q + 1) % NDI == 0 and q + 1 < ROUNDS:
                        for n in range(NS):
                            sp.wait_ge(dbu_ready, q * STEPS + (n + 1) * CPB)
                            load_b(n, (q + 1) // NDI)
                        sp.wait_ge(c_ready, (q + 1) * STEPS)
                        load_c((q + 1) // NDI)
                    sp.wait_ge(y_ready, (q + 1) * CPB)
                    b, m = divmod(q, NDI)
                    sp.dma_start(yT_view[:, m, b * L:(b + 1) * L], u[:, q % 2, :]).then_inc(y_out, 16)
                    if q + 1 < ROUNDS:
                        load_gate(q + 1)
                    if q + 2 < ROUNDS:
                        sp.wait_ge(y_out, 16 * (q + 1))
                        load_round(q + 2)
                sp.wait_ge(y_out, 16 * ROUNDS)

            @block.gpsimd
            def _(pool):
                nc.gpsimd.memset(c_parts[:], 0.0).then_inc(zeroed, 1)
                with pool.Fori(0, ROUNDS // 2) as pair:
                    for par in range(2):
                        q = pair * 2 + par
                        pool.wait_ge(du_in[par], (pair + 1) * 48)
                        pool.wait_ge(dbu_ready, q * STEPS)
                        nc.gpsimd.tensor_tensor(du[:], delta[:, par, :], u[:, par, :], ALU.mult).then_inc(du_ready, 1)
                        pool.wait_ge(du_ready, q + 1)
                        for n in range(NS):
                            pool.wait_ge(b_in[n], (pair // (NDI // 2) + 1) * 16)
                            for j in range(CPB):
                                k = n * CPB + j
                                pool.wait_ge(scan_done, q * STEPS + k)
                                nc.gpsimd.tensor_tensor(dbu[:, k % NDBU, :], du[:, j * CH:(j + 1) * CH], b_all[:, n, j * CH:(j + 1) * CH], ALU.mult).then_inc(dbu_ready, 1)

            @block.scalar
            def _(act):
                with act.Fori(0, ROUNDS // 2) as pair:
                    for par in range(2):
                        q = pair * 2 + par
                        act.wait_ge(du_in[par], (pair + 1) * 48)
                        nc.scalar.activation(decay[:, par, :], a_log[:, par, 0:NS], ACT.Exp).then_inc(decay_exp, 1)
                        act.wait_ge(decay_exp, q + 1)
                        nc.scalar.activation(decay[:, par, :], decay[:, par, :], ACT.Copy, scale=-1.0).then_inc(decay_ready, 1)
                        act.wait_ge(decay_ready, q + 1)
                        for k in range(STEPS):
                            n, j = divmod(k, CPB)
                            act.wait_ge(scan_done, q * STEPS + k - 1 + AHEAD)
                            nc.scalar.activation(abar[:, k % 2, :], delta[:, par, j * CH:(j + 1) * CH], ACT.Exp, scale=decay[:, par, n:n + 1]).then_inc(abar_ready, 1)

            @block.vector
            def _(dve):
                dve.wait_ge(craw_in, 16)
                for i in range(SPLIT):
                    nc.vector.tensor_copy(c_split[:, i, :], c_raw if i % 2 == 0 else c_rest).then_inc(split_done, 1)
                    dve.wait_ge(split_done, 2 * i + 1)
                    if i < SPLIT - 1:
                        rest, new = (c_raw, c_rest) if i % 2 == 0 else (c_rest, c_raw)
                        nc.vector.tensor_tensor(new, rest, c_split[:, i, :], ALU.subtract).then_inc(split_done, 1)
                        dve.wait_ge(split_done, 2 * i + 2)
                dve.wait_ge(const_in, 32)
                nc.vector.tensor_copy(pick[:], part_of[:].unsqueeze(2).broadcast_to([96, NS, 128])).then_inc(pick_made, 1)
                dve.wait_ge(split_out, 16 * SPLIT)
                dve.sem_inc(scan_done, AHEAD)
                with dve.Fori(0, ROUNDS // 2) as pair:
                    for par in range(2):
                        q = pair * 2 + par
                        s0 = q * STEPS
                        for k in range(STEPS + 1):
                            n, j = divmod(k, CPB)
                            if k < STEPS:
                                dve.wait_ge(abar_ready, s0 + k + 1)
                                dve.wait_ge(dbu_ready, s0 + k + 1)
                                if j:
                                    dve.wait_ge(scan_done, s0 + k + AHEAD)
                                if k >= NSTATE:
                                    dve.wait_ge(c_used, s0 + k - NSTATE + 1)
                                state = h[:, (k - 1) % NSTATE, CH - 1:CH] if j else 0.0
                                ins = nc.vector.tensor_tensor_scan(h[:, k % NSTATE, :], abar[:, k % 2, :], dbu[:, k % NDBU, :], state, ALU.mult, ALU.add)
                                ins.then_inc(scan_done, 1)
                            if k >= 1:
                                dve.wait_ge(scan_done, s0 + k + AHEAD)
                                dve.wait_ge(c_ready, s0 + k)
                                dve.wait_ge(hc_added, s0 + k)
                                nc.vector.tensor_tensor(hc[:, (k - 1) % 2, :], h[:, (k - 1) % NSTATE, :], c_all[:, (k - 1) % 2, :], ALU.mult).then_inc(c_used, 1)
                        dve.wait_ge(hc_added, s0 + STEPS + 2)
                        dve.wait_ge(g_in, (q + 1) * 16)
                        dve.wait_ge(du_in[par], (pair + 1) * 48)
                        dve.wait_ge(dbu_ready, s0 + STEPS)
                        for j in range(CPB):
                            t = slice(j * CH, (j + 1) * CH)
                            nc.vector.scalar_tensor_tensor(u[:, par, t], u[:, par, t], a_log[:, par, NS:NS + 1], y_acc[:, j, :], ALU.mult, ALU.add).then_inc(acc_read, 1)
                        for j in range(CPB):
                            t = slice(j * CH, (j + 1) * CH)
                            dve.wait_ge(acc_read, q * CPB + j + 1)
                            nc.vector.tensor_tensor(u[:, par, t], u[:, par, t], g[:, t], ALU.mult).then_inc(y_ready, 1)

            @block.tensor
            def _(pe):
                pe.wait_ge(const_in, 32)
                pe.wait_ge(pick_made, 1)
                pe.sem_inc(hc_added, 2)

                with pe.Fori(0, ROUNDS // 2) as pair:
                    for par in range(2):
                        q = pair * 2 + par
                        s0 = q * STEPS
                        pe.wait_ge(cparts_in, (pair // (NDI // 2) + 1) * 16 * SPLIT)
                        for k in range(STEPS + 1):
                            n, j = divmod(k, CPB)
                            if k < STEPS:
                                if k >= 2:
                                    pe.wait_ge(c_used, s0 + k - 1)
                                else:
                                    pe.wait_ge(c_used, s0)
                                nc.tensor.matmul(c_all[:, k % 2, :], pick[:, n, :], c_parts[:, j * CH:(j + 1) * CH], start=True, stop=True).then_inc(c_ready, 1)
                            if k >= 1:
                                n1, j1 = divmod(k - 1, CPB)
                                pe.wait_ge(c_used, s0 + k)
                                if k - 1 < CPB:
                                    pe.wait_ge(acc_read, q * CPB)
                                nc.tensor.matmul(y_acc[:, j1, :], ident[:], hc[:, (k - 1) % 2, :], start=(n1 == 0), stop=(n1 == NS - 1)).then_inc(hc_added, 1)
        s.clear()

NE, HD = 16, 64
QKV = 3 * HD


def expert_front(nc, a):
    with Scope(nc, "moe") as s:
        w_out = s.sb("w_out", [128, NDI, D])
        w_qkv = s.sb("w_qkv", [128, KD, NE * QKV])
        sim, sim_sq = s.sb("sim", [128, KD, NE]), s.sb("sim_sq", [128, KD, NE])
        sim_inv, sim_eps = s.sb("sim_inv", [128, NE]), s.sb("sim_eps", [128, NE])
        gate_sig = s.sb("gate_sig", [128, NE])
        expert_no = s.sb("expert_no", [128, NE])
        ident, ones, mhalf = s.sb("ident", [128, 128]), s.sb("ones", [128, 128]), s.sb("mhalf", [128, NE])
        yT, xr = s.sb("yT", [128, NDI, CH]), s.sb("xr", [128, TPC, D])
        x1, xh, sq = s.sb("x1", [128, TPC, D]), s.sb("xh", [128, TPC, D]), s.sb("sq", [128, D])
        st, var, rstd = s.sb("st", [128, TPC, 8]), s.sb("var", [128, TPC]), s.sb("rstd", [128, TPC])
        ssq, ssq_clamped, inv_norm = s.sb("ssq", [128, TPC]), s.sb("ssq_clamped", [128, TPC]), s.sb("inv_norm", [128, TPC])
        xT = s.sb("xT", [128, KD, CH])
        logit, gated, active, shifted, expd, rw = (s.sb(n, [128, TPC, NE]) for n in ("logit", "gated", "active", "shifted", "expd", "rw"))
        top, top_idx, top_f = s.sb("top", [128, TPC, 8]), s.sb("top_idx", [128, TPC, 8], mybir.dt.uint32), s.sb("top_f", [128, TPC, 8])
        fall, fall2 = s.sb("fall", [128, TPC, NE]), s.sb("fall2", [128, TPC, NE])
        gmax, idle, total = s.sb("gmax", [128, TPC]), s.sb("idle", [128, TPC]), s.sb("total", [128, TPC])
        acc = s.sb("acc", [128, TPC, 2, QKV])
        mixed = s.sb("mixed", [128, TPC, QKV])
        qkT = s.sb("qkT", [128, CH])

        NP = 4
        pP = s.ps("pP", [128, NP, CH])
        pT = s.ps("pT", [128, KD, CH])
        pX = s.ps("pX", [128, CH])
        pQK = s.ps("pQK", [128, CH])

        w_loaded, y_in, x1_out, rw_out, qk_out, v_out = (s.sem(n) for n in ("w_loaded", "y_in", "x1_out", "rw_out", "qk_out", "v_out"))
        dve_sem, const_set, sim_ready, ssq_ready = (s.sem(n) for n in ("dve_sem", "const_set", "sim_ready", "ssq_ready"))
        x1_psum, x1_ready, var_ready, rstd_ready, xh_ready, norm_ready, inv_ready = (s.sem(n) for n in (
            "x1_psum", "x1_ready", "var_ready", "rstd_ready", "xh_ready", "norm_ready", "inv_ready"))
        xT_psum, xT_ready, lg_psum, lg_read, shift_ready, exp_ready, rw_ready = (s.sem(n) for n in (
            "xT_psum", "xT_ready", "lg_psum", "lg_read", "shift_ready", "exp_ready", "rw_ready"))
        p_psum, p_read, mix_ready, qk_psum, qk_ready, sim_psum, simsq_ready, sig_ready, pow_sim, pow_sim_in = (s.sem(n) for n in (
            "p_psum", "p_read", "mix_ready", "qk_psum", "qk_ready", "sim_psum", "simsq_ready", "sig_ready", "pow_sim", "pow_sim_in"))

        yT_view = a["yT"].rearrange("(m p) t -> p m t", p=128)
        xr_view, x1_view, rw_view, v_view = (a[n].rearrange("(n p) d -> p n d", p=128) for n in ("xr", "x1", "rw", "v0"))
        PAIRS = NE // 2
        BANKS = TPC * PAIRS
        NW = 7

        with nc.Block() as block:
            @block.sync
            def _(sp):
                for dst, src in ((ident[:], a["ident"]), (w_out[:], a["W_out"].rearrange("(m p) n -> p m n", p=128)),
                                 (sim[:], a["sim"].rearrange("(k p) n -> p k n", p=128)),
                                 (gate_sig[:], a["gates"].broadcast_to([128, NE])),
                                 (expert_no[:], a["expert_no"]), (w_qkv[:, 0, :], a["w_qkv"][0:128, :]), (w_qkv[:, 1, :], a["w_qkv"][128:256, :])):
                    sp.dma_start(dst, src).then_inc(w_loaded, 16)
                sp.dma_start(yT[:], yT_view[:, :, 0:CH]).then_inc(y_in, 16)
                sp.dma_start(xr[:], xr_view[:, 0:TPC, :]).then_inc(y_in, 16)

                def stores(c, more):
                    sp.wait_ge(x1_ready, (c + 1) * TPC)
                    sp.dma_start(x1_view[:, ds(c * TPC, TPC), :], x1[:]).then_inc(x1_out, 16)
                    if more:
                        sp.dma_start(yT[:], yT_view[:, :, ds((c + 1) * CH, CH)]).then_inc(y_in, 16)
                        sp.dma_start(xr[:], xr_view[:, ds((c + 1) * TPC, TPC), :]).then_inc(y_in, 16)
                    sp.wait_ge(rw_ready, c + 1)
                    sp.dma_start(rw_view[:, ds(c * TPC, TPC), :], rw[:]).then_inc(rw_out, 16)

                def qkv_stores(c):
                    sp.wait_ge(mix_ready, (c + 1) * TPC)
                    sp.dma_start(v_view[:, ds(c * TPC, TPC), :], mixed[:, :, 2 * HD:QKV]).then_inc(v_out, 16)
                    sp.wait_ge(qk_ready, c + 1)
                    sp.dma_start(a["qkT"][:, ds(c * CH, CH)], qkT[:]).then_inc(qk_out, 16)

                stores(0, True)
                with sp.Fori(1, NCH - 1) as c:
                    sp.wait_ge(x1_ready, (c + 1) * TPC)
                    sp.dma_start(x1_view[:, ds(c * TPC, TPC), :], x1[:]).then_inc(x1_out, 16)
                    sp.dma_start(yT[:], yT_view[:, :, ds((c + 1) * CH, CH)]).then_inc(y_in, 16)
                    sp.dma_start(xr[:], xr_view[:, ds((c + 1) * TPC, TPC), :]).then_inc(y_in, 16)
                    qkv_stores(c - 1)
                    sp.wait_ge(rw_ready, c + 1)
                    sp.dma_start(rw_view[:, ds(c * TPC, TPC), :], rw[:]).then_inc(rw_out, 16)
                c = NCH - 1
                sp.wait_ge(x1_ready, (c + 1) * TPC)
                sp.dma_start(x1_view[:, ds(c * TPC, TPC), :], x1[:]).then_inc(x1_out, 16)
                qkv_stores(c - 1)
                sp.wait_ge(rw_ready, c + 1)
                sp.dma_start(rw_view[:, ds(c * TPC, TPC), :], rw[:]).then_inc(rw_out, 16)
                qkv_stores(c)
                for sem in (x1_out, rw_out, v_out, qk_out):
                    sp.wait_ge(sem, 16 * NCH)

            @block.gpsimd
            def _(pool):
                nc.gpsimd.memset(mhalf[:], -0.5).then_inc(const_set, 1)
                nc.gpsimd.memset(ones[:], 1.0).then_inc(const_set, 1)
                pool.wait_ge(const_set, 2)
                pool.wait_ge(pow_sim_in, 1)
                nc.gpsimd.tensor_tensor(sim_inv[:], sim_eps[:], mhalf[:], ALU.pow).then_inc(pow_sim, 1)
                with pool.Fori(0, NCH) as c:
                    pool.wait_ge(var_ready, c + 1)
                    nc.gpsimd.tensor_tensor(rstd[:], var[:], mhalf[:, 0:TPC], ALU.pow).then_inc(rstd_ready, 1)
                    pool.wait_ge(ssq_ready, c + 1)
                    pool.wait_ge(lg_read, c * TPC)
                    nc.gpsimd.tensor_tensor(inv_norm[:], ssq_clamped[:], mhalf[:, 0:TPC], ALU.pow).then_inc(inv_ready, 1)

            HEAD = CHUNK_LN_MARKS
            GATE = 10 + 4 * TPC
            MIX = 2 * PAIRS * TPC

            @block.vector
            def _(dve):
                def head(c, base):
                    ch = Chain(dve, dve_sem, base)
                    dve.wait_ge(y_in, (c + 1) * 32)
                    dve.wait_ge(x1_out, c * 16)
                    for j in range(TPC):
                        dve.wait_ge(x1_psum, c * TPC + j + 1)
                        nc.vector.tensor_tensor(x1[:, j, :], pX[:, (j % 2) * D:(j % 2 + 1) * D], xr[:, j, :], ALU.add).then_inc(x1_ready, 1)
                    dve.wait_ge(x1_ready, (c + 1) * TPC)
                    dve.wait_ge(xT_psum, c)
                    dve.wait_ge(norm_ready, c * TPC)
                    chunk_layernorm(nc, ch, x1, xh, st, var, rstd, var_ready, rstd_ready, c + 1)
                    ch.wait()
                    dve.sem_inc(xh_ready, 1)
                    assert ch.n == HEAD, ch.n

                def clamp(c):
                    dve.wait_ge(norm_ready, (c + 1) * TPC)
                    dve.wait_ge(inv_ready, c)
                    nc.vector.tensor_scalar(ssq_clamped[:], ssq[:], 1e-24, None, ALU.max).then_inc(ssq_ready, 1)

                def gate(c, base):
                    ch = Chain(dve, dve_sem, base)
                    dve.wait_ge(lg_psum, c + 1)
                    dve.wait_ge(inv_ready, c + 1)
                    for j in range(TPC):
                        nc.vector.scalar_tensor_tensor(logit[:, j, :], pX[:, j * NE:(j + 1) * NE], inv_norm[:, j:j + 1], gate_sig[:], ALU.mult, ALU.subtract).then_inc(lg_read, 1)
                    dve.wait_ge(lg_read, (c + 1) * TPC)
                    ch.mark(nc.vector.tensor_scalar(gated[:], logit[:], 0.0, None, ALU.max))
                    for j in range(TPC):
                        ch.mark(nc.vector.max(top[:, j, :], logit[:, j, :]))
                    ch.wait()
                    ch.mark(nc.vector.tensor_scalar(active[:], gated[:], 0.0, None, ALU.is_gt))
                    ch.mark(nc.vector.reduce_max(gmax[:], gated[:], AXIS_X))
                    for j in range(TPC):
                        ch.mark(nc.vector.max_index(top_idx[:, j, :], top[:, j, :], logit[:, j, :]))
                    ch.wait()
                    dve.wait_ge(exp_ready, c)
                    nc.vector.tensor_tensor(shifted[:], gated[:], gmax[:, :].unsqueeze(2).broadcast_to([128, TPC, NE]), ALU.subtract).then_inc(shift_ready, 1)
                    ch.mark(nc.vector.tensor_scalar(idle[:], gmax[:], 0.0, None, ALU.is_le))
                    ch.step(nc.vector.tensor_copy(top_f[:], top_idx[:]))
                    for j in range(TPC):
                        ch.mark(nc.vector.tensor_scalar(fall[:, j, :], expert_no[:], top_f[:, j, 0:1], idle[:, j:j + 1], ALU.is_equal, ALU.mult))
                    for j in range(TPC):
                        ch.mark(nc.vector.tensor_scalar(fall2[:, j, :], expert_no[:], top_f[:, j, 1:2], idle[:, j:j + 1], ALU.is_equal, ALU.mult))
                    ch.wait()
                    ch.step(nc.vector.tensor_tensor(active[:], active[:], fall[:], ALU.add))
                    ch.step(nc.vector.tensor_tensor(active[:], active[:], fall2[:], ALU.add))
                    dve.wait_ge(exp_ready, c + 1)
                    ch.step(nc.vector.tensor_tensor(expd[:], expd[:], active[:], ALU.mult))
                    ch.step(nc.vector.reduce_sum(total[:], expd[:], AXIS_X))
                    ch.step(nc.vector.reciprocal(total[:], total[:]))
                    dve.wait_ge(rw_out, c * 16)
                    nc.vector.tensor_tensor(rw[:], expd[:], total[:, :].unsqueeze(2).broadcast_to([128, TPC, NE]), ALU.mult).then_inc(rw_ready, 1)
                    dve.wait_ge(rw_ready, c + 1)
                    assert ch.n == GATE, ch.n

                def mix(c, j, base):
                    ch = Chain(dve, dve_sem, base + j * 2 * PAIRS)
                    for e in range(NE):
                        bank = (j * PAIRS + e // 2) % NP
                        src = pP[:, bank, (e % 2) * QKV:(e % 2 + 1) * QKV]
                        dst = acc[:, j, e % 2, :]
                        if e % 2 == 0:
                            dve.wait_ge(p_psum, c * BANKS + j * PAIRS + e // 2 + 1)
                        if e < 2:
                            ins = nc.vector.tensor_scalar(dst, src, rw[:, j, e:e + 1], None, ALU.mult)
                        else:
                            dve.wait_ge(dve_sem, ch.base + e - 1)
                            ins = nc.vector.scalar_tensor_tensor(dst, src, rw[:, j, e:e + 1], dst, ALU.mult, ALU.add)
                        ch.mark(ins)
                    ch.wait()
                    if j == 0:
                        dve.wait_ge(qk_psum, c)
                        dve.wait_ge(v_out, c * 16)
                    nc.vector.tensor_tensor(mixed[:, j, :], acc[:, j, 0, :], acc[:, j, 1, :], ALU.add).then_inc(mix_ready, 1)

                dve.wait_ge(w_loaded, 16 * NW)
                nc.vector.tensor_tensor(sim_sq[:], sim[:], sim[:], ALU.mult).then_inc(simsq_ready, 1)
                dve.wait_ge(sim_psum, 1)
                nc.vector.tensor_scalar(sim_eps[:], pX[:, 0:NE], 1e-24, None, ALU.max).then_inc(pow_sim_in, 1)
                dve.wait_ge(pow_sim, 1)
                for k in range(KD):
                    ins = nc.vector.tensor_tensor(sim[:, k, :], sim[:, k, :], sim_inv[:], ALU.mult)
                    ins.then_inc(sim_ready, 1)
                head(0, 0)
                clamp(0)
                dve.wait_ge(sig_ready, 1)
                PER = GATE + MIX + HEAD
                with dve.Fori(0, NCH - 1) as c:
                    base = HEAD + c * PER
                    gate(c, base)
                    mix(c, 0, base + GATE)
                    mix(c, 1, base + GATE)
                    head(c + 1, base + GATE + 2 * PAIRS * 2)
                    mix(c, 2, base + GATE + HEAD)
                    clamp(c + 1)
                    mix(c, 3, base + GATE + HEAD)
                c, base = NCH - 1, HEAD + (NCH - 1) * PER
                gate(c, base)
                for j in range(TPC):
                    mix(c, j, base + GATE)

            @block.scalar
            def _(act):
                def head(c):
                    act.wait_ge(xh_ready, c + 1)
                    act.wait_ge(ssq_ready, c)
                    for j in range(TPC):
                        if j:
                            act.wait_ge(norm_ready, c * TPC + j)
                        nc.scalar.activation(sq[:], xh[:, j, :], ACT.Square, accum_out=ssq[:, j:j + 1]).then_inc(norm_ready, 1)

                def move_in(c):
                    act.wait_ge(xT_psum, c + 1)
                    act.wait_ge(p_psum, c * BANKS)
                    for k in range(KD):
                        nc.scalar.activation(xT[:, k, :], pT[:, k, :], ACT.Copy).then_inc(xT_ready, 1)

                def gate(c):
                    act.wait_ge(shift_ready, c + 1)
                    act.wait_ge(rw_ready, c)
                    nc.scalar.activation(expd[:], shifted[:], ACT.Exp).then_inc(exp_ready, 1)

                def qk(c):
                    act.wait_ge(qk_psum, c + 1)
                    act.wait_ge(qk_out, c * 16)
                    nc.scalar.activation(qkT[:], pQK[:], ACT.Copy).then_inc(qk_ready, 1)

                act.wait_ge(w_loaded, 16 * NW)
                nc.scalar.activation(gate_sig[:], gate_sig[:], ACT.Sigmoid).then_inc(sig_ready, 1)
                head(0)
                with act.Fori(0, NCH - 1) as c:
                    move_in(c)
                    gate(c)
                    head(c + 1)
                    qk(c)
                move_in(NCH - 1)
                gate(NCH - 1)
                qk(NCH - 1)

            @block.tensor
            def _(pe):
                def head_x(c):
                    pe.wait_ge(y_in, (c + 1) * 32)
                    pe.wait_ge(lg_read, c * TPC)
                    for j in range(TPC):
                        if j == 2:
                            pe.wait_ge(x1_ready, c * TPC + 2)
                        for m in range(NDI):
                            last = nc.tensor.matmul(pX[:, (j % 2) * D:(j % 2 + 1) * D], yT[:, m, j * 128:(j + 1) * 128], w_out[:, m, :], start=(m == 0), stop=(m == NDI - 1))
                        if j % 2:
                            last.then_inc(x1_psum, 2)

                def head_t(c):
                    pe.wait_ge(xh_ready, c + 1)
                    pe.wait_ge(xT_ready, c * KD)
                    for j in range(TPC):
                        for k in range(KD):
                            last = nc.tensor.transpose(pT[:, k, j * 128:(j + 1) * 128], xh[:, j, k * 128:(k + 1) * 128], ident[:])
                    last.then_inc(xT_psum, 1)

                def logits(c):
                    pe.wait_ge(xT_ready, (c + 1) * KD)
                    pe.wait_ge(x1_ready, (c + 1) * TPC)
                    for j in range(TPC):
                        for k in range(KD):
                            last = nc.tensor.matmul(pX[:, j * NE:(j + 1) * NE], xT[:, k, j * 128:(j + 1) * 128], sim[:, k, :], start=(k == 0), stop=(k == KD - 1))
                    last.then_inc(lg_psum, 1)

                def products(c, j):
                    for pr in range(PAIRS):
                        n = j * PAIRS + pr
                        bank_free(c, n)
                        for k in range(KD):
                            last = nc.tensor.matmul(pP[:, n % NP, 0:2 * QKV], xT[:, k, j * 128:(j + 1) * 128], w_qkv[:, k, pr * 2 * QKV:(pr + 1) * 2 * QKV], start=(k == 0), stop=(k == KD - 1))
                        last.then_inc(p_psum, 1)

                def bank_free(c, n):
                    PER = GATE + MIX + HEAD
                    if n >= NP:
                        j, pr = divmod(n - NP, PAIRS)
                        past_head = HEAD if (j >= 2) else 0
                        if isinstance(c, int) and c == NCH - 1:
                            past_head = 0
                        pe.wait_ge(dve_sem, HEAD + c * PER + GATE + past_head + j * 2 * PAIRS + 2 * pr + 2)
                    else:
                        pe.wait_ge(mix_ready, c * TPC)

                def qk(c):
                    pe.wait_ge(mix_ready, (c + 1) * TPC)
                    pe.wait_ge(qk_ready, c)
                    for j in range(TPC):
                        last = nc.tensor.transpose(pQK[:, j * 128:(j + 1) * 128], mixed[:, j, 0:128], ident[:])
                    last.then_inc(qk_psum, 1)

                pe.wait_ge(w_loaded, 16 * NW)
                pe.wait_ge(const_set, 2)
                pe.wait_ge(simsq_ready, 1)
                for k in range(KD):
                    last = nc.tensor.matmul(pX[:, 0:NE], ones[:], sim_sq[:, k, :], start=(k == 0), stop=(k == KD - 1))
                last.then_inc(sim_psum, 1)
                pe.wait_ge(sim_ready, KD)
                head_x(0)
                head_t(0)
                with pe.Fori(0, NCH - 1) as c:
                    logits(c)
                    products(c, 0)
                    products(c, 1)
                    head_x(c + 1)
                    products(c, 2)
                    head_t(c + 1)
                    products(c, 3)
                    qk(c)
                c = NCH - 1
                logits(c)
                for j in range(TPC):
                    products(c, j)
                qk(c)
        s.clear()

def causal_attention(nc, a):
    QT = L // TILE
    GRP = CH // TILE
    SCALE = float(HD) ** -0.5
    KO = NE * HD // 128
    with Scope(nc, "causal") as s:
        ident, above = s.sb("ident", [128, 128]), s.sb("above", [128, 128])
        w_o = s.sb("w_o", [128, KO, D])
        qT, kT = s.sb("qT", [HD, L]), s.sb("kT", [HD, L])
        v, rw, x = s.sb("v", [128, QT, HD]), s.sb("rw", [128, QT, NE]), s.sb("x", [128, QT, D])
        probs = s.sb("probs", [128, 2, L])
        probsT = s.sb("probsT", [128, 2, CH])
        smax, nmax, ssum, rsum = (s.sb(n, [128, QT]) for n in ("smax", "nmax", "ssum", "rsum"))
        attn, mixed = s.sb("attn", [128, 2, HD]), s.sb("mixed", [128, 2, NE, HD])
        mixedT = s.sb("mixedT", [128, KO, TILE])
        pS = s.ps("pS", [128, L])
        pT = s.ps("pT", [128, 2, CH])
        pA, pO = s.ps("pA", [128, CH]), s.ps("pO", [128, CH])

        w_in, qk_in, v_in, rw_in, x_in, x_out = (s.sem(n) for n in ("w_in", "qk_in", "v_in", "rw_in", "x_in", "x_out"))
        (s_psum, masked, max_ready, nmax_ready, exp_done, mT_psum, mT_moved, pT_psum, pT_moved, attn_psum, rsum_ready, attn_ready,
         mix_ready, o_psum, x_ready) = (s.sem(n) for n in (
             "s_psum", "masked", "max_ready", "nmax_ready", "exp_done", "mT_psum", "mT_moved", "pT_psum", "pT_moved", "attn_psum", "rsum_ready",
             "attn_ready", "mix_ready", "o_psum", "x_ready"))

        rw_view, v_view, x1_view, x2_view = (a[n].rearrange("(n p) d -> p n d", p=128) for n in ("rw", "v0", "x1", "x2"))
        GRPS = [qt // GRP + 1 for qt in range(QT)]
        PER_B = sum(GRPS)
        FIRST = [sum(GRPS[:t]) for t in range(QT)]
        QUARTERS = 4

        uses = []
        for qt in range(QT + 2):
            if 2 <= qt:
                uses += [("m", 2 * (qt - 2)), ("m", 2 * (qt - 2) + 1)]
            if 1 <= qt <= QT:
                uses += [("p", FIRST[qt - 1] + g) for g in range(GRPS[qt - 1])]
        assert len(uses) % 2 == 0

        def bank(kind, n):
            return uses.index((kind, n)) % 2

        with nc.Block() as block:
            @block.sync
            def _(sp):
                def load_qk(b):
                    sp.dma_start(qT[:], a["qkT"][0:HD, ds(b * L, L)]).then_inc(qk_in, 16)
                    sp.dma_start(kT[:], a["qkT"][HD:2 * HD, ds(b * L, L)]).then_inc(qk_in, 16)

                def load_v(b):
                    sp.dma_start(v[:], v_view[:, ds(b * QT, QT), :]).then_inc(v_in, 16)

                def load_rw(b):
                    sp.dma_start(rw[:], rw_view[:, ds(b * QT, QT), :]).then_inc(rw_in, 16)

                def load_x(b):
                    sp.dma_start(x[:], x1_view[:, ds(b * QT, QT), :]).then_inc(x_in, 16)

                def store_x(b):
                    n = QT // QUARTERS
                    for i in range(QUARTERS):
                        sp.wait_ge(x_ready, b * QT + (i + 1) * n)
                        sp.dma_start(x2_view[:, ds(b * QT + i * n, n), :], x[:, i * n:(i + 1) * n, :]).then_inc(x_out, 16)

                load_qk(0)
                sp.dma_start(above[:], a["above"]).then_inc(w_in, 16)
                sp.dma_start(ident[:], a["ident"]).then_inc(w_in, 16)
                load_v(0)
                load_rw(0)
                sp.dma_start(w_o[:], a["w_o"].rearrange("(m p) n -> p m n", p=128)).then_inc(w_in, 16)
                load_x(0)
                with sp.Fori(0, B - 1) as b:
                    sp.wait_ge(s_psum, (b + 1) * QT)
                    load_qk(b + 1)
                    sp.wait_ge(attn_psum, (b + 1) * QT)
                    load_v(b + 1)
                    sp.wait_ge(mix_ready, (b + 1) * QT)
                    load_rw(b + 1)
                    store_x(b)
                    sp.wait_ge(x_out, (b + 1) * 16 * QUARTERS)
                    load_x(b + 1)
                store_x(B - 1)
                sp.wait_ge(x_out, 16 * QUARTERS * B)

            @block.vector
            def _(dve):
                with dve.Fori(0, B) as b:
                    def peak(qt):
                        dve.wait_ge(s_psum, b * QT + qt + 1)
                        diag = pS[:, qt * 128:(qt + 1) * 128]
                        nc.vector.tensor_tensor(diag, diag, above[:], ALU.add).then_inc(masked, 1)
                        dve.wait_ge(masked, b * QT + qt + 1)
                        nc.vector.reduce_max(smax[:, qt:qt + 1], pS[:, 0:(qt + 1) * 128], AXIS_X).then_inc(max_ready, 1)
                        dve.wait_ge(max_ready, b * QT + qt + 1)
                        nc.vector.tensor_scalar(nmax[:, qt:qt + 1], smax[:, qt:qt + 1], -SCALE, None, ALU.mult).then_inc(nmax_ready, 1)

                    def spread(qt):
                        dve.wait_ge(exp_done, b * QT + qt + 1)
                        if qt == 0:
                            dve.wait_ge(rw_in, (b + 1) * 16)
                        nc.vector.reciprocal(rsum[:, qt:qt + 1], ssum[:, qt:qt + 1]).then_inc(rsum_ready, 1)
                        dve.wait_ge(rsum_ready, b * QT + qt + 1)
                        dve.wait_ge(attn_psum, b * QT + qt + 1)
                        nc.vector.tensor_scalar(attn[:, qt % 2, :], pA[:, 0:HD], rsum[:, qt:qt + 1], None, ALU.mult).then_inc(attn_ready, 1)
                        dve.wait_ge(attn_ready, b * QT + qt + 1)
                        if qt >= 2:
                            dve.wait_ge(mT_psum, 2 * (b * QT + qt - 1))
                        nc.vector.tensor_tensor(mixed[:, qt % 2, :, :], attn[:, qt % 2, :].unsqueeze(1).broadcast_to([128, NE, HD]),
                                                rw[:, qt, :].unsqueeze(2).broadcast_to([128, NE, HD]), ALU.mult).then_inc(mix_ready, 1)

                    def add(qt):
                        dve.wait_ge(o_psum, b * QT + qt + 1)
                        if qt == 0:
                            dve.wait_ge(x_in, (b + 1) * 16)
                        nc.vector.tensor_tensor(x[:, qt, :], pO[:, 0:D], x[:, qt, :], ALU.add).then_inc(x_ready, 1)

                    def move(qt, g):
                        n = FIRST[qt] + g
                        w = min(GRP, qt + 1 - g * GRP) * 128
                        dve.wait_ge(pT_psum, b * PER_B + n + 1)
                        nc.vector.tensor_copy(probsT[:, bank("p", n), 0:w], pT[:, bank("p", n), 0:w]).then_inc(pT_moved, 1)

                    dve.wait_ge(w_in, 48)
                    for qt in range(QT + 2):
                        if qt < QT:
                            peak(qt)
                        if 1 <= qt <= QT:
                            move(qt - 1, 0)
                        if 2 <= qt:
                            add(qt - 2)
                        if 1 <= qt <= QT:
                            for g in range(1, GRPS[qt - 1]):
                                move(qt - 1, g)
                            spread(qt - 1)

            @block.scalar
            def _(act):
                with act.Fori(0, B) as b:
                    for qt in range(QT + 2):
                        if 2 <= qt:
                            for hlf in range(2):
                                n = 2 * (qt - 2) + hlf
                                act.wait_ge(mT_psum, b * 2 * QT + n + 1)
                                if hlf == 0:
                                    act.wait_ge(o_psum, b * QT + qt - 2)
                                nc.scalar.activation(mixedT[:, 4 * hlf:4 * hlf + 4, :], pT[:, bank("m", n), :], ACT.Copy).then_inc(mT_moved, 1)
                        if qt < QT:
                            act.wait_ge(nmax_ready, b * QT + qt + 1)
                            if qt >= 2:
                                act.wait_ge(attn_psum, b * QT + qt - 1)
                            else:
                                act.wait_ge(attn_psum, b * QT)
                            n = (qt + 1) * 128
                            nc.scalar.activation(probs[:, qt % 2, 0:n], pS[:, 0:n], ACT.Exp, bias=nmax[:, qt:qt + 1], scale=SCALE, accum_out=ssum[:, qt:qt + 1]).then_inc(exp_done, 1)

            @block.tensor
            def _(pe):
                with pe.Fori(0, B) as b:
                    def scores(qt):
                        pe.wait_ge(exp_done, b * QT + qt)
                        n = (qt + 1) * 128
                        for k0 in range(0, n, CH):
                            w = min(CH, n - k0)
                            last = nc.tensor.matmul(pS[:, k0:k0 + w], qT[:, qt * 128:(qt + 1) * 128], kT[:, k0:k0 + w], start=True, stop=True)
                        last.then_inc(s_psum, 1)

                    def bank_free(kind, n):
                        at = uses.index((kind, n)) - 2
                        if at < 0:
                            pe.wait_ge(mT_moved, b * 2 * QT)
                        elif uses[at][0] == "m":
                            pe.wait_ge(mT_moved, b * 2 * QT + uses[at][1] + 1)
                        else:
                            pe.wait_ge(pT_moved, b * PER_B + uses[at][1] + 1)

                    def mixed_transposes(t):
                        pe.wait_ge(mix_ready, b * QT + t + 1)
                        src = mixed[:, t % 2, :, :].rearrange("p e d -> p (e d)")
                        for hlf in range(2):
                            bank_free("m", 2 * t + hlf)
                            for i in range(4):
                                m = 4 * hlf + i
                                last = nc.tensor.transpose(pT[:, bank("m", 2 * t + hlf), i * 128:(i + 1) * 128], src[:, m * 128:(m + 1) * 128], ident[:])
                            last.then_inc(mT_psum, 1)

                    def outputs(t, m0, m1):
                        for m in range(m0, m1):
                            if m == 0:
                                pe.wait_ge(x_ready, b * QT + t)
                            if m % 4 == 0:
                                pe.wait_ge(mT_moved, b * 2 * QT + 2 * t + m // 4 + 1)
                            ins = nc.tensor.matmul(pO[:, 0:D], mixedT[:, m, :], w_o[:, m, :], start=(m == 0), stop=(m == KO - 1))
                        if m1 == KO:
                            ins.then_inc(o_psum, 1)

                    def prob_transposes(t, g):
                        n = FIRST[t] + g
                        bank_free("p", n)
                        for i in range(min(GRP, t + 1 - g * GRP)):
                            kt = g * GRP + i
                            last = nc.tensor.transpose(pT[:, bank("p", n), i * 128:(i + 1) * 128], probs[:, t % 2, kt * 128:(kt + 1) * 128], ident[:])
                        last.then_inc(pT_psum, 1)

                    def attend(t, g):
                        n = FIRST[t] + g
                        pe.wait_ge(pT_moved, b * PER_B + n + 1)
                        if g == 0:
                            pe.wait_ge(attn_ready, b * QT + t)
                        for i in range(min(GRP, t + 1 - g * GRP)):
                            kt = g * GRP + i
                            last = nc.tensor.matmul(pA[:, 0:HD], probsT[:, bank("p", n), i * 128:(i + 1) * 128], v[:, kt, :], start=(kt == 0), stop=(kt == t))
                        if g == GRPS[t] - 1:
                            last.then_inc(attn_psum, 1)

                    pe.wait_ge(qk_in, (b + 1) * 32)
                    for qt in range(QT + 2):
                        if qt < QT:
                            scores(qt)
                        if qt == 0:
                            pe.wait_ge(w_in, 48)
                            pe.wait_ge(v_in, (b + 1) * 16)
                        if 2 <= qt:
                            mixed_transposes(qt - 2)
                            outputs(qt - 2, 0, KO - 2)
                        if 1 <= qt <= QT:
                            pe.wait_ge(exp_done, b * QT + qt)
                            prob_transposes(qt - 1, 0)
                        if 2 <= qt:
                            outputs(qt - 2, KO - 2, KO)
                        if 1 <= qt <= QT:
                            for g in range(1, GRPS[qt - 1]):
                                prob_transposes(qt - 1, g)
                                attend(qt - 1, g - 1)
                            attend(qt - 1, GRPS[qt - 1] - 1)
        s.clear()

NH, NKV, HW = 16, 4, 16
KVD = NKV * HW


def rotary_front(nc, a):
    with Scope(nc, "rot") as s:
        NQ = D // 128
        ROWS = [128] * NQ + [KVD]
        NPC = len(ROWS)
        ident, mhalf = s.sb("ident", [128, 128]), s.sb("mhalf", [128, TPC])
        w_qk = s.sb("w_qk", [128, KD, 2 * (D + KVD)])
        w_v, b_v = s.sb("w_v", [128, KD, KVD]), s.sb("b_v", [128, KVD])
        b_qk = s.sb("b_qk", [128, 2 * NPC])
        cos, sin = s.sb("cos", [128, L]), s.sb("sin", [128, L])
        x, xh = s.sb("x", [128, 2, TPC, D]), s.sb("xh", [128, TPC, D])
        st, var, rstd = s.sb("st", [128, TPC, 8]), s.sb("var", [128, TPC]), s.sb("rstd", [128, TPC])
        xT = s.sb("xT", [128, 2, KD, CH])
        straight, crossed, q, rest = (s.sb(n, [128, NPC, CH]) for n in ("straight", "crossed", "q", "rest"))
        part = [s.sb(f"part{i}", [128, NPC, CH], BF16) for i in range(3)]
        v = s.sb("v", [128, TPC, KVD])
        pP = s.ps("pP", [128, 4, CH])
        pT = s.ps("pT", [128, KD, CH])
        pV = s.ps("pV", [128, CH])

        w_in = s.sem("w_in")
        x_in = [s.sem("x_in_even"), s.sem("x_in_odd")]
        (dve_sem, half_set, var_ready, rstd_ready, xh_ready, xT_psum, xT_ready, p_psum, straight_ready, crossed_ready,
         q_ready, part0, part1, rest_ready, part2, v_psum, v_ready, parts_out, v_out) = (s.sem(n) for n in (
             "dve_sem", "half_set", "var_ready", "rstd_ready", "xh_ready", "xT_psum", "xT_ready", "p_psum", "straight_ready",
             "crossed_ready", "q_ready", "part0", "part1", "rest_ready", "part2", "v_psum", "v_ready", "parts_out", "v_out"))
        x_view, v_view = (a[n].rearrange("(n p) d -> p n d", p=128) for n in ("x2", "v1"))
        W = D + KVD
        NW = 9
        NOUT = 3 * 2

        def every_chunk(eng, body):
            with eng.Fori(0, NCH // 2 - 1) as pair:
                for par in range(2):
                    body(pair * 2 + par, pair, par, False)
            body(NCH - 2, NCH // 2 - 1, 0, False)
            body(NCH - 1, NCH // 2 - 1, 1, True)

        with nc.Block() as block:
            @block.sync
            def _(sp):
                sp.dma_start(x[:, 0, :, :], x_view[:, 0:TPC, :]).then_inc(x_in[0], 16)
                for dst, src in ((ident[:], a["ident"]), (w_qk[:, 0, :], a["w_qk"][0:128, :]), (w_qk[:, 1, :], a["w_qk"][128:256, :]),
                                 (w_v[:, 0, :], a["w_v"][0:128, :]), (w_v[:, 1, :], a["w_v"][128:256, :]),
                                 (b_v[:], a["b_v"].broadcast_to([128, KVD])), (b_qk[:], a["b_qk"]), (cos[:], a["cos"]), (sin[:], a["sin"])):
                    sp.dma_start(dst, src).then_inc(w_in, 16)
                sp.dma_start(x[:, 1, :, :], x_view[:, TPC:2 * TPC, :]).then_inc(x_in[1], 16)

                def body(c, pair, par, last):
                    if not (isinstance(c, int) and c + 2 >= NCH):
                        sp.wait_ge(xh_ready, c + 1)
                        sp.dma_start(x[:, par, :, :], x_view[:, ds((c + 2) * TPC, TPC), :]).then_inc(x_in[par], 16)
                    sp.wait_ge(v_ready, (c + 1) * TPC)
                    sp.dma_start(v_view[:, ds(c * TPC, TPC), :], v[:]).then_inc(v_out, 16)
                    for i, done in enumerate((part0, part1, part2)):
                        sp.wait_ge(done, (c + 1) * NPC)
                        q_dst = a["q_parts"][i, :, ds(c * CH, CH)].rearrange("(m p) t -> p m t", p=128)
                        sp.dma_start(q_dst, part[i][:, 0:NQ, :]).then_inc(parts_out, 16)
                        sp.dma_start(a["k_parts"][i, :, ds(c * CH, CH)], part[i][0:KVD, NQ, :]).then_inc(parts_out, 16)

                every_chunk(sp, body)
                sp.wait_ge(v_out, 16 * NCH)
                sp.wait_ge(parts_out, 16 * NOUT * NCH)

            @block.gpsimd
            def _(pool):
                nc.gpsimd.memset(mhalf[:], -0.5).then_inc(half_set, 1)
                pool.wait_ge(half_set, 1)

                def root(c):
                    pool.wait_ge(var_ready, c + 1)
                    nc.gpsimd.tensor_tensor(rstd[:], var[:], mhalf[:], ALU.pow).then_inc(rstd_ready, 1)

                def add(c):
                    for m, r in enumerate(ROWS):
                        pool.wait_ge(crossed_ready, c * NPC + m + 1)
                        pool.wait_ge(rest_ready, c * NPC)
                        nc.gpsimd.tensor_tensor(q[0:r, m, :], straight[0:r, m, :], crossed[0:r, m, :], ALU.add).then_inc(q_ready, 1)

                root(0)
                with pool.Fori(0, NCH - 1) as c:
                    root(c + 1)
                    add(c)
                add(NCH - 1)

            @block.vector
            def _(dve):
                LN = CHUNK_LN_MARKS

                def norm(c, pair, par):
                    ch = Chain(dve, dve_sem, c * LN)
                    dve.wait_ge(x_in[par], (pair + 1) * 16)
                    at_least(dve, xT_psum, c)
                    chunk_layernorm(nc, ch, x[:, par, :, :], xh, st, var, rstd, var_ready, rstd_ready, c + 1)
                    ch.wait()
                    dve.sem_inc(xh_ready, 1)

                norm(0, 0, 0)
                dve.wait_ge(w_in, 16 * NW)

                def body(c, pair, par, last):
                    if not last:
                        norm(c + 1, pair + par, 1 - par)
                    t0 = (pair % (CPB // 2)) * 2 * CH + par * CH
                    dve.wait_ge(q_ready, c * NPC)
                    for m, r in enumerate(ROWS):
                        for w, (dst, table, done) in enumerate(((straight, cos, straight_ready), (crossed, sin, crossed_ready))):
                            n = 2 * m + w
                            dve.wait_ge(p_psum, c * 2 * NPC + n + 1)
                            nc.vector.scalar_tensor_tensor(dst[0:r, m, :], pP[0:r, n % 4, :], b_qk[0:r, w * NPC + m:w * NPC + m + 1],
                                                           table[0:r, ds(t0, CH)], ALU.add, ALU.mult).then_inc(done, 1)
                    dve.wait_ge(v_psum, c + 1)
                    dve.wait_ge(v_out, c * 16)
                    for j in range(TPC):
                        nc.vector.tensor_tensor(v[:, j, :], pV[:, j * KVD:(j + 1) * KVD], b_v[:], ALU.add).then_inc(v_ready, 1)
                    dve.wait_ge(parts_out, c * 16 * NOUT)
                    for m, r in enumerate(ROWS):
                        dve.wait_ge(part0, c * NPC + m + 1)
                        nc.vector.tensor_tensor(rest[0:r, m, :], q[0:r, m, :], part[0][0:r, m, :], ALU.subtract).then_inc(rest_ready, 1)
                    for m, r in enumerate(ROWS):
                        dve.wait_ge(part1, c * NPC + m + 1)
                        nc.vector.tensor_tensor(part[2][0:r, m, :], rest[0:r, m, :], part[1][0:r, m, :], ALU.subtract).then_inc(part2, 1)

                every_chunk(dve, body)

            @block.scalar
            def _(act):
                def move_in(c, par):
                    act.wait_ge(xT_psum, c + 1)
                    at_least(act, v_psum, c - 1)
                    for k in range(KD):
                        nc.scalar.activation(xT[:, par, k, :], pT[:, k, :], ACT.Copy).then_inc(xT_ready, 1)

                move_in(0, 0)

                def body(c, pair, par, last):
                    if not last:
                        move_in(c + 1, 1 - par)
                    act.wait_ge(parts_out, c * 16 * NOUT)
                    for m, r in enumerate(ROWS):
                        act.wait_ge(q_ready, c * NPC + m + 1)
                        nc.scalar.activation(part[0][0:r, m, :], q[0:r, m, :], ACT.Copy).then_inc(part0, 1)
                    for m, r in enumerate(ROWS):
                        act.wait_ge(rest_ready, c * NPC + m + 1)
                        nc.scalar.activation(part[1][0:r, m, :], rest[0:r, m, :], ACT.Copy).then_inc(part1, 1)

                every_chunk(act, body)

            @block.tensor
            def _(pe):
                def transposes(c):
                    pe.wait_ge(xh_ready, c + 1)
                    at_least(pe, xT_ready, c * KD)
                    for j in range(TPC):
                        for k in range(KD):
                            last = nc.tensor.transpose(pT[:, k, j * 128:(j + 1) * 128], xh[:, j, k * 128:(k + 1) * 128], ident[:])
                    last.then_inc(xT_psum, 1)

                pe.wait_ge(w_in, 16 * NW)
                transposes(0)

                def body(c, pair, par, last):
                    pe.wait_ge(xT_ready, (c + 1) * KD)
                    for m, r in enumerate(ROWS):
                        for w, done in enumerate((straight_ready, crossed_ready)):
                            n = 2 * m + w
                            if n < 4:
                                pe.wait_ge(done, c * NPC)
                            else:
                                pe.wait_ge(done, c * NPC + m - 1)
                            for k in range(KD):
                                ins = nc.tensor.matmul(pP[0:r, n % 4, :], w_qk[:, k, w * W + m * 128:w * W + m * 128 + r], xT[:, par, k, :], start=(k == 0), stop=(k == KD - 1))
                            ins.then_inc(p_psum, 1)
                    if not last:
                        transposes(c + 1)
                    pe.wait_ge(v_ready, c * TPC)
                    for j in range(TPC):
                        for k in range(KD):
                            ins = nc.tensor.matmul(pV[:, j * KVD:(j + 1) * KVD], xT[:, par, k, j * 128:(j + 1) * 128], w_v[:, k, :], start=(k == 0), stop=(k == KD - 1))
                    ins.then_inc(v_psum, 1)

                every_chunk(pe, body)
        s.clear()

def full_attention(nc, a):
    G = NH // NKV
    QC = L // CH
    KT = L // TILE
    NB = B * NKV
    RUNS = ((0, 3), (1, 2), (2, 1))
    COMBOS = [(qp, kp) for qp, n in RUNS for kp in range(n)]
    ROWS = len(COMBOS) * HW
    PARTS = 3
    SCALE = float(HW) ** -0.5
    NM = 3

    next_pass = []
    for h in range(G):
        for n in range(16):
            if n == 8 and h:
                next_pass.append(("row", h - 1))
            next_pass.append(("max", h, n // 4, n % 4))
    NP = len(next_pass)
    OUT_AT = 7
    ROW_AT = [next_pass.index(("row", h)) for h in range(G - 1)]
    PER_UNIT = NP + 2
    assert (2 * NP + 1) % NM == 0 and PER_UNIT % NM == 0 and OUT_AT < ROW_AT[0]

    def unit_items(first, last):
        items = [("row", G - 1)]
        if not last:
            items += next_pass
        if not first:
            items.insert(1 if last else OUT_AT, ("out",))
        return items

    def items_before(u):
        if isinstance(u, int):
            return NP if u == 0 else 2 * NP + 1 + PER_UNIT * (u - 1)
        return u * PER_UNIT + (2 * NP + 1 - PER_UNIT)

    with Scope(nc, "attn") as s:
        ident, ident_bf = s.sb("ident", [128, 128]), s.sb("ident_bf", [128, 128], BF16)
        k_max, k_exp = s.sb("k_max", [ROWS, 2, L], BF16), s.sb("k_exp", [ROWS + PARTS, 2, L], BF16)
        v = s.sb("v", [128, 2, KT, 32])
        q = s.sb("q", [ROWS + PARTS, QC, G, CH], BF16)
        probs = s.sb("probs", [128, 2, G, CH])
        part_max = s.sb("part_max", [128, G, 4, 4])
        peak, rest = s.sb("peak", [128, G, 4]), s.sb("rest", [128, G, 4])
        peak_parts = s.sb("peak_parts", [128, G, 4, PARTS], BF16)
        o_rows = s.sb("o_rows", [128, CH])
        inv = s.sb("inv", [128, 4, G])
        ctx = s.sb("ctx", [128, 4, G, HW])
        pE = s.ps("pE", [128, G, CH])
        pM = s.ps("pM", [128, NM, CH])
        pA = s.ps("pA", [128, CH])

        ident_made = s.sem("ident_made")
        const_in, ones_set, ctx_out = (s.sem(n) for n in ("const_in", "ones_set", "ctx_out"))
        kmax_in, kexp_in, v_in = ([s.sem(f"{n}_{par}") for par in ("even", "odd")] for n in ("kmax_in", "kexp_in", "v_in"))
        q_in = [s.sem(f"q_in{qc}") for qc in range(QC)]
        e_psum, exp_done, pv_done, o_moved, m_psum, m_free, parts_ready, split_sem, inv_ready, ctx_ready = (s.sem(n) for n in (
            "e_psum", "exp_done", "pv_done", "o_moved", "m_psum", "m_free", "parts_ready", "split_sem", "inv_ready", "ctx_ready"))
        v_view = a["v1"].rearrange("(n p) d -> p n d", p=128)
        ctx_view = a["ctx"].rearrange("(n p) d -> p n d", p=128)

        def every_bg(eng, body):
            def both(pair, first, last):
                for par in range(2):
                    body(pair * 2 + par, pair, par, first and par == 0, last and par == 1)
            both(0, True, False)
            with eng.Fori(1, NB // 2 - 1) as pair:
                both(pair, False, False)
            both(NB // 2 - 1, False, True)

        with nc.Block() as block:
            @block.sync
            def _(sp):
                def load_k(dst, sem, bg, par):
                    b, g = bg // NKV, bg % NKV
                    row = 0
                    for _, n in RUNS:
                        src = a["k_parts"][0:n, ds(g * HW, HW), ds(b * L, L)]
                        sp.dma_start(dst[row:row + n * HW, par, :], src).then_inc(sem[par], 16)
                        row += n * HW

                def load_v(bg, par):
                    b, g = bg // NKV, bg % NKV
                    sp.dma_start(v[:, par, :, 0:HW], v_view[:, ds(b * KT, KT), ds(g * HW, HW)]).then_inc(v_in[par], 16)

                def load_q(bg, qc):
                    b, g = bg // NKV, bg % NKV
                    for i, (qp, _) in enumerate(COMBOS):
                        src = a["q_parts"][qp, ds(g * G * HW, G * HW), ds(b * L + qc * CH, CH)].rearrange("(h r) t -> r h t", h=G)
                        sp.dma_start(q[i * HW:(i + 1) * HW, qc, :, :], src).then_inc(q_in[qc], 16)

                def store(u_end, bg, qc):
                    b, g = bg // NKV, bg % NKV
                    sp.wait_ge(ctx_ready, u_end)
                    sp.dma_start(ctx_view[:, ds(b * KT + qc * 4, 4), ds(g * G * HW, G * HW)], ctx[:].rearrange("p j h d -> p j (h d)")).then_inc(ctx_out, 16)

                load_q(0, 0)
                load_k(k_max, kmax_in, 0, 0)
                sp.dma_start(ident[:], a["ident"]).then_inc(const_in, 16)
                load_k(k_exp, kexp_in, 0, 0)
                load_q(0, 1)
                sp.wait_ge(ones_set, 2)
                load_v(0, 0)

                def body(bg, pair, par, first, last):
                    for qc in range(QC):
                        u = bg * QC + qc
                        if not (first and qc == 0):
                            sp.wait_ge(e_psum, u * 2 * KT)
                        if not (last and qc >= QC - 2):
                            load_q(bg if qc < QC - 2 else bg + 1, (qc + 2) % QC)
                        if qc == 0 and not last:
                            at_least(sp, m_psum, items_before(u) - NP)
                            load_k(k_max, kmax_in, bg + 1, 1 - par)
                            load_k(k_exp, kexp_in, bg + 1, 1 - par)
                            at_least(sp, pv_done, u * KT)
                            load_v(bg + 1, 1 - par)
                        if not (first and qc == 0):
                            store(u, bg if qc else bg - 1, qc - 1 if qc else QC - 1)
                    if last:
                        store(NB * QC, bg, QC - 1)

                every_bg(sp, body)
                sp.wait_ge(ctx_out, 16 * NB * QC)

            @block.gpsimd
            def _(pool):
                nc.gpsimd.memset(v[:], 0.0).then_inc(ones_set, 1)
                pool.wait_ge(ones_set, 1)
                nc.gpsimd.memset(v[:, :, :, HW:HW + 1], 1.0).then_inc(ones_set, 1)
                pool.wait_ge(ones_set, 2)
                nc.gpsimd.memset(k_exp[ROWS:ROWS + PARTS, :, :], 1.0).then_inc(ones_set, 1)

            @block.scalar
            def _(act):
                def body(bg, pair, par, first, last):
                    for qc in range(QC):
                        u = bg * QC + qc
                        for kt in range(KT):
                            for hp in range(2):
                                act.wait_ge(e_psum, u * 2 * KT + 2 * kt + hp + 1)
                                if hp == 0:
                                    at_least(act, pv_done, u * KT + kt - 1)
                                nc.scalar.activation(probs[:, kt % 2, 2 * hp:2 * hp + 2, :], pE[:, 2 * hp:2 * hp + 2, :], ACT.Exp, scale=SCALE).then_inc(exp_done, 1)
                            if kt == 0 and not (first and qc == 0):
                                move_out(u - 1, first and qc == 1, False)
                    if last:
                        move_out(NB * QC - 1, False, True)

                def move_out(u, first, last):
                    act.wait_ge(pv_done, (u + 1) * KT)
                    if not first:
                        act.wait_ge(m_psum, items_before(u) + (1 if last else OUT_AT) + 1)
                    nc.scalar.activation(o_rows[:], pA[:], ACT.Copy).then_inc(o_moved, 1)

                every_bg(act, body)

            @block.vector
            def _(dve):
                SPLITS = 4

                def split_step(i, h, u, n):
                    if i == 0:
                        dve.wait_ge(m_free, n + 1)
                        ins = nc.vector.reduce_max(peak[:, h, :], part_max[:, h, :, :], AXIS_X)
                    else:
                        dve.wait_ge(split_sem, (u * G + h) * SPLITS + i)
                        if i == 1:
                            ins = nc.vector.tensor_scalar(peak_parts[:, h, :, 0], peak[:, h, :], -1.0, None, ALU.mult)
                        elif i == 2:
                            ins = nc.vector.scalar_tensor_tensor(rest[:, h, :], peak[:, h, :], -1.0, peak_parts[:, h, :, 0], ALU.mult, ALU.subtract)
                        elif i == 3:
                            ins = nc.vector.tensor_scalar(peak_parts[:, h, :, 1], rest[:, h, :], 1.0, None, ALU.mult)
                        else:
                            ins = nc.vector.tensor_tensor(peak_parts[:, h, :, 2], rest[:, h, :], peak_parts[:, h, :, 1], ALU.subtract)
                    ins.then_inc(split_sem if i < SPLITS else parts_ready, 1)

                def take(item, slot, n, u, par):
                    dve.wait_ge(m_psum, n + 1)
                    if item[0] == "max":
                        _, h, j, kc = item
                        nc.vector.reduce_max(part_max[:, h, j, kc:kc + 1], pM[:, slot, :], AXIS_X).then_inc(m_free, 1)
                        step = 4 * j + kc
                        if h and step <= SPLITS:
                            split_step(step, h - 1, u, n - 1 - step)
                        if h == G - 1 and step == 15:
                            for i in range(SPLITS + 1):
                                split_step(i, h, u, n)
                    elif item[0] == "row":
                        nc.vector.tensor_copy(q[ROWS:ROWS + PARTS, par, item[1], :], pM[ROWS:ROWS + PARTS, slot, :]).then_inc(m_free, 1)
                    else:
                        out(slot, u)

                def out(slot, u):
                    heads = pM[:, slot, :].rearrange("p (j h d) -> p j h d", j=4, h=G)
                    nc.vector.reciprocal(inv[:], heads[:, :, :, HW]).then_inc(inv_ready, 1)
                    dve.wait_ge(inv_ready, u + 1)
                    at_least(dve, ctx_out, u * 16)
                    nc.vector.tensor_tensor(ctx[:], heads[:, :, :, 0:HW], inv[:].unsqueeze(3).broadcast_to([128, 4, G, HW]), ALU.mult).then_inc(ctx_ready, 1)
                    dve.wait_ge(ctx_ready, u + 1)
                    dve.sem_inc(m_free, 1)

                dve.wait_ge(const_in, 16)
                nc.vector.tensor_copy(ident_bf[:], ident[:]).then_inc(ident_made, 1)
                for n, item in enumerate(next_pass):
                    take(item, n % NM, n, 0, 0)

                def body(bg, pair, par, first, last):
                    for qc in range(QC):
                        u = bg * QC + qc
                        start, end = first and qc == 0, last and qc == QC - 1
                        slot0 = NP % NM if start else 0
                        for i, item in enumerate(unit_items(start, end)):
                            of = u if i == 0 else u - 1 if item[0] == "out" else u + 1
                            take(item, (slot0 + i) % NM, items_before(u) + i, of, qc if i == 0 else (qc + 1) % QC)
                        if end:
                            take(("out",), 2, items_before(u) + 2, u, 0)

                every_bg(dve, body)

            @block.tensor
            def _(pe):
                def give(item, slot, n, u, par, qc):
                    at_least(pe, m_free, n - NM + 1)
                    if item[0] == "max":
                        _, h, j, kc = item
                        nc.tensor.matmul(pM[:, slot, :], q[0:ROWS, qc, h, j * 128:(j + 1) * 128], k_max[0:ROWS, par, kc * CH:(kc + 1) * CH], start=True, stop=True).then_inc(m_psum, 1)
                    elif item[0] == "row":
                        h = item[1]
                        pe.wait_ge(parts_ready, u * G + h + 1)
                        for j in range(4):
                            last = nc.tensor.matmul(pM[ROWS:ROWS + PARTS, slot, j * 128:(j + 1) * 128], peak_parts[:, h, j, :], ident_bf[:], start=True, stop=True)
                        last.then_inc(m_psum, 1)
                    else:
                        pe.wait_ge(o_moved, u + 1)
                        for j in range(4):
                            last = nc.tensor.transpose(pM[:, slot, j * 128:(j + 1) * 128], o_rows[:, j * 128:(j + 1) * 128], ident[:])
                        last.then_inc(m_psum, 1)

                def sums(u, kt, par):
                    pe.wait_ge(exp_done, u * 2 * KT + 2 * kt + 2)
                    if kt == 0:
                        at_least(pe, o_moved, u)
                    for h in range(G):
                        last = nc.tensor.matmul(pA[32 * h:32 * h + 32, :], v[:, par, kt, :], probs[:, kt % 2, h, :], start=(kt == 0), stop=(kt == KT - 1))
                    last.then_inc(pv_done, 1)

                pe.wait_ge(const_in, 16)
                pe.wait_ge(ident_made, 1)
                pe.wait_ge(q_in[0], 16 * len(COMBOS))
                pe.wait_ge(kmax_in[0], 16 * len(RUNS))
                for n, item in enumerate(next_pass):
                    give(item, n % NM, n, 0, 0, 0)
                pe.wait_ge(ones_set, 3)

                def body(bg, pair, par, first, last):
                    for qc in range(QC):
                        u = bg * QC + qc
                        start, end = first and qc == 0, last and qc == QC - 1
                        n0, slot0 = items_before(u), NP % NM if start else 0
                        items = list(enumerate(unit_items(start, end)))
                        nbg = par if qc < QC - 1 else 1 - par

                        def give_next(count):
                            for i, item in items[:count]:
                                of = u if i == 0 else u - 1 if item[0] == "out" else u + 1
                                if i == 1 and item[0] == "max":
                                    pe.wait_ge(q_in[(qc + 1) % QC], (bg + (1 if qc < QC - 1 else 2)) * 16 * len(COMBOS))
                                    if qc == QC - 1:
                                        pe.wait_ge(kmax_in[nbg], (pair + (1 if par == 0 else 2)) * 16 * len(RUNS))
                                give(item, (slot0 + i) % NM, n0 + i, of, nbg, qc if i == 0 else (qc + 1) % QC)
                            del items[:count]

                        def scores(kt, hp):
                            at_least(pe, exp_done, u * 2 * KT + 2 * kt + hp - 1)
                            for h in (2 * hp, 2 * hp + 1):
                                last_mm = nc.tensor.matmul(pE[:, h, :], k_exp[:, par, kt * 128:(kt + 1) * 128], q[:, qc, h, :], start=True, stop=True)
                            last_mm.then_inc(e_psum, 1)

                        for kt in range(KT):
                            if kt == 0:
                                pe.wait_ge(m_free, n0 - NP + ROW_AT[1] + 1)
                                pe.wait_ge(kexp_in[par], (pair + 1) * 16 * len(RUNS))
                            scores(kt, 0)
                            give_next(1 if end else 2)
                            if kt == 0:
                                if not start:
                                    sums(u - 1, KT - 1, par if qc else 1 - par)
                                pe.wait_ge(v_in[par], (pair + 1) * 16)
                                pe.wait_ge(m_free, n0 + 1)
                            scores(kt, 1)
                            give_next(0 if end else 1)
                            if kt:
                                sums(u, kt - 1, par)
                            give_next(0 if end else 2 if kt <= 5 else 1)
                        assert not items
                    if last:
                        sums(u, KT - 1, par)
                        give(("out",), 2, n0 + 2, u, 0, 0)

                every_bg(pe, body)
        s.clear()

BOT, RD, NK, TOP, UH = 128, 48, 1024, 8, 64


def key_lookup(nc, a):
    KV = NK // 128
    GONE = -3.0e38
    with Scope(nc, "look") as s:
        ident, ones, mhalf = s.sb("ident", [128, 128]), s.sb("ones", [128, 128]), s.sb("mhalf", [128, TPC])
        w_o, b_o = s.sb("w_o", [128, KD, D]), s.sb("b_o", [128, D])
        w_q, w_r = s.sb("w_q", [128, KD, BOT]), s.sb("w_r", [128, RD])
        keysT, values = s.sb("keysT", [128, NK]), s.sb("values", [128, KV, D])
        w_u1, b_u1, w_u2 = s.sb("w_u1", [128, KD, UH]), s.sb("b_u1", [UH, 1]), s.sb("w_u2", [UH, 1])
        scalars = s.sb("scalars", [128, 3])
        rk, rq = s.sb("rk", [RD + 1, NK]), s.sb("rq", [64, CH])
        ctx, x2 = s.sb("ctx", [128, TPC, D]), s.sb("x2", [128, TPC, D])
        ctxT, xT = s.sb("ctxT", [128, KD, CH]), s.sb("xT", [128, KD, CH])
        x3, xh = s.sb("x3", [128, TPC, D]), s.sb("xh", [128, TPC, D])
        st, var, rstd, st_h = s.sb("st", [128, TPC, 8]), s.sb("var", [128, TPC]), s.sb("rstd", [128, TPC]), s.sb("st_h", [128, TPC, 6])
        query, h1 = s.sb("query", [BOT, CH]), s.sb("h1", [UH, CH])
        top, ntop = s.sb("top", [128, 2, TOP]), s.sb("ntop", [128, 2])
        left, expd, weight = s.sb("left", [128, NK]), s.sb("expd", [128, 2, NK]), s.sb("weight", [128, 2, NK])
        wsum, winv = s.sb("wsum", [128, 2]), s.sb("winv", [128, 2])
        weightT = s.sb("weightT", [128, KV, TILE])
        sum_all, look_all = s.sb("sum_all", [128, NT, D]), s.sb("look_all", [128, NT, D])
        stats_all, learned_all = s.sb("stats_all", [128, NT, 6]), s.sb("learned_all", [128, NT])
        mean_v, var_v, tmp_v, logv, gate = (s.sb(n, [128, NT]) for n in ("mean_v", "var_v", "tmp_v", "logv", "gate"))
        logsum = s.sb("logsum", [128, 1])
        result = s.sb("result", [128, 2, TPC, D])

        pS = s.ps("pS", [128, 2, NK])
        pT = s.ps("pT", [128, 2, CH])
        pL, pX = s.ps("pL", [128, CH]), s.ps("pX", [128, CH])

        w_in = s.sem("w_in")
        c_in = s.sem("c_in")
        (dve_sem, const_set, biased, var_ready, rstd_ready, xh_ready, t_psum, t_moved, x_psum, x_read, x3_ready,
         query_ready, rq_ready, h1_ready, s_psum, ntop_ready, exp_ready, weight_ready, look_psum, look_ready, s_free) = (s.sem(n) for n in (
             "dve_sem", "const_set", "biased", "var_ready", "rstd_ready", "xh_ready", "t_psum", "t_moved", "x_psum", "x_read", "x3_ready",
             "query_ready", "rq_ready", "h1_ready", "s_psum", "ntop_ready", "exp_ready", "weight_ready", "look_psum", "look_ready", "s_free"))
        rk_psum, rk_moved, logv_ready, lsum_ready, lsum_psum, learn_ready, unc_ready, gate_ready, var_all = (s.sem(n) for n in (
            "rk_psum", "rk_moved", "logv_ready", "lsum_ready", "lsum_psum", "learn_ready", "unc_ready", "gate_ready", "var_all"))
        out_ready, winv_ready = s.sem("out_ready"), s.sem("winv_ready")
        out_done = [s.sem("out_even"), s.sem("out_odd")]

        ctx_view, x2_view, out_view = (a[n].rearrange("(n p) d -> p n d", p=128) for n in ("ctx", "x2", "out"))
        NW = 14
        TPER = TPC + 2
        XPER = 6

        def t_use(c, what):
            if isinstance(c, int) and c == 0 and what in ("ctx", "xh"):
                return 0 if what == "ctx" else 1
            if what in ("ctx", "xh"):
                body = (c - 1) * TPER + 2
                return body + (0 if what == "ctx" else 3)
            body = c * TPER + 2
            if isinstance(c, int) and c == NCH - 1:
                return body + what
            return body + (1, 2, 4, 5)[what]

        with nc.Block() as block:
            @block.sync
            def _(sp):
                two = lambda n: a[n].rearrange("(k p) n -> p k n", p=128)
                for dst, src in ((ident[:], a["ident"]), (w_r[:], a["w_r"]), (keysT[:], a["keysT"]), (rk[RD:RD + 1, :], a["reliability"]),
                                 (w_o[:], two("w_ho")), (b_o[:], a["b_ho"].broadcast_to([128, D])), (w_q[:], two("w_fq")),
                                 (w_u1[:], two("w_u1")), (b_u1[:], a["b_u1"]), (w_u2[:], a["w_u2"]),
                                 (scalars[:, 0:1], a["unc_b2"].broadcast_to([128, 1])), (scalars[:, 1:2], a["gate_w1"].broadcast_to([128, 1])),
                                 (scalars[:, 2:3], a["gate_bias"].broadcast_to([128, 1])), (values[:], two("values"))):
                    sp.dma_start(dst, src).then_inc(w_in, 16)
                with sp.Fori(0, NCH) as c:
                    sp.wait_ge(x3_ready, c * TPC)
                    sp.dma_start(ctx[:], ctx_view[:, ds(c * TPC, TPC), :]).then_inc(c_in, 16)
                    sp.dma_start(x2[:], x2_view[:, ds(c * TPC, TPC), :]).then_inc(c_in, 16)
                with sp.Fori(0, NCH // 2) as pair:
                    for par in range(2):
                        c = pair * 2 + par
                        sp.wait_ge(out_ready, (c + 1) * TPC)
                        sp.dma_start(out_view[:, ds(c * TPC, TPC), :], result[:, par, :, :]).then_inc(out_done[par], 16)
                for par in range(2):
                    sp.wait_ge(out_done[par], 16 * (NCH // 2))

            @block.gpsimd
            def _(pool):
                nc.gpsimd.memset(mhalf[:], -0.5).then_inc(const_set, 1)
                nc.gpsimd.memset(ones[:], 1.0).then_inc(const_set, 1)
                nc.gpsimd.memset(rq[:], 1.0).then_inc(const_set, 1)
                pool.wait_ge(const_set, 3)
                pool.wait_ge(w_in, 16 * NW)
                with pool.Fori(0, NCH) as c:
                    pool.wait_ge(c_in, (c + 1) * 32)
                    nc.gpsimd.tensor_tensor(x2[:], x2[:], b_o[:].unsqueeze(1).broadcast_to([128, TPC, D]), ALU.add).then_inc(biased, 1)
                    pool.wait_ge(var_ready, c + 1)
                    nc.gpsimd.tensor_tensor(rstd[:], var[:], mhalf[:], ALU.pow).then_inc(rstd_ready, 1)

            HEAD = CHUNK_LN_MARKS + TPC + 2
            TILE_MARKS = 3

            @block.vector
            def _(dve):
                def head(c, base):
                    ch = Chain(dve, dve_sem, base)
                    dve.wait_ge(biased, c + 1)
                    for j in range(TPC):
                        dve.wait_ge(x_psum, c * XPER + j // 2 + 1)
                        nc.vector.tensor_tensor(x3[:, j, :], pX[:, (j % 2) * D:(j % 2 + 1) * D], x2[:, j, :], ALU.add).then_inc(x3_ready, 1)
                    dve.wait_ge(x3_ready, (c + 1) * TPC)
                    dve.wait_ge(t_psum, t_use(c, "ctx") + 1)
                    chunk_layernorm(nc, ch, x3, xh, st, var, rstd, var_ready, rstd_ready, c + 1)
                    ch.wait()
                    dve.sem_inc(xh_ready, 1)
                    assert ch.n == CHUNK_LN_MARKS

                def keep(c, base):
                    ch = Chain(dve, dve_sem, base)
                    ch.mark(nc.vector.tensor_tensor(sum_all[:, ds(c * TPC, TPC), :], x3[:], xh[:], ALU.add))
                    for j in range(TPC):
                        ch.mark(nc.vector.bn_stats(st_h[:, j, :], xh[:, j, :]))
                    ch.wait()
                    ch.step(nc.vector.tensor_scalar(stats_all[:, ds(c * TPC, TPC), :], st_h[:], 1.0, None, ALU.mult))
                    assert ch.n == HEAD - CHUNK_LN_MARKS, ch.n

                def learned(c):
                    dve.wait_ge(x_psum, (c + 1) * XPER)
                    nc.vector.tensor_scalar(learned_all[:, ds(c * TPC, TPC)], pX[:, 0:TPC], 1.0, None, ALU.mult).then_inc(learn_ready, 1)

                def choose(c, j, base):
                    ch = Chain(dve, dve_sem, base)
                    n, b = c * TPC + j, j % 2
                    dve.wait_ge(s_psum, n + 1)
                    nc.vector.memset(wsum[:, b:b + 1], 0.0).then_inc(dve_sem, 1)
                    ch.n += 1
                    ch.step(nc.vector.max(top[:, b, :], pS[:, b, :]))
                    nc.vector.tensor_scalar(ntop[:, b:b + 1], top[:, b, 0:1], -1.0, None, ALU.mult).then_inc(ntop_ready, 1)
                    ch.mark(nc.vector.match_replace(out=left[:], in_to_replace=top[:, b, :], in_values=pS[:, b, :], imm_value=GONE))
                    ch.wait()
                    dve.sem_inc(s_free, 1)
                    dve.wait_ge(exp_ready, n + 1)
                    nc.vector.scalar_tensor_tensor(weight[:, b, :], left[:], GONE, expd[:, b, :], ALU.is_equal, ALU.mult, accum_out=wsum[:, b:b + 1]).then_inc(weight_ready, 1)
                    assert ch.n == TILE_MARKS

                def finish(c, j):
                    n, b = c * TPC + j, j % 2
                    dve.wait_ge(weight_ready, n + 1)
                    nc.vector.reciprocal(winv[:, b:b + 1], wsum[:, b:b + 1]).then_inc(winv_ready, 1)
                    dve.wait_ge(winv_ready, n + 1)
                    dve.wait_ge(look_psum, n + 1)
                    nc.vector.tensor_scalar(look_all[:, ds(n, 1), :], pL[:, 0:D], winv[:, b:b + 1], None, ALU.mult).then_inc(look_ready, 1)

                dve.wait_ge(w_in, 16 * NW)
                for i in range(2):
                    dve.wait_ge(rk_psum, i + 1)
                    nc.vector.tensor_copy(rk[0:RD, i * CH:(i + 1) * CH], (pX, pL)[i][0:RD, :]).then_inc(rk_moved, 1)
                head(0, 0)
                keep(0, CHUNK_LN_MARKS)
                learned(0)
                PER = HEAD + TPC * TILE_MARKS

                def body(c, more, base):
                    choose(c, 0, base)
                    choose(c, 1, base + TILE_MARKS)
                    finish(c, 0)
                    if more:
                        head(c + 1, base + 2 * TILE_MARKS)
                        base = base + CHUNK_LN_MARKS
                    choose(c, 2, base + 2 * TILE_MARKS)
                    finish(c, 1)
                    choose(c, 3, base + 3 * TILE_MARKS)
                    finish(c, 2)
                    finish(c, 3)
                    if more:
                        learned(c + 1)
                        keep(c + 1, base + 4 * TILE_MARKS)

                with dve.Fori(0, NCH - 1) as c:
                    body(c, True, HEAD + c * PER)
                body(NCH - 1, False, HEAD + (NCH - 1) * PER)
                ch = Chain(dve, dve_sem, HEAD + (NCH - 1) * PER + TPC * TILE_MARKS)
                ch.wait()
                me, mo, ve, vo = (stats_all[:, :, k] for k in (1, 4, 2, 5))
                ch.mark(nc.vector.tensor_tensor(tmp_v[:], me, mo, ALU.subtract))
                ch.step(nc.vector.tensor_tensor(var_v[:], ve, vo, ALU.add))
                ch.mark(nc.vector.tensor_tensor(tmp_v[:], tmp_v[:], tmp_v[:], ALU.mult))
                ch.step(nc.vector.tensor_scalar(var_v[:], var_v[:], 1.0 / D, None, ALU.mult))
                nc.vector.scalar_tensor_tensor(var_v[:], tmp_v[:], 0.25, var_v[:], ALU.mult, ALU.add).then_inc(var_all, 1)
                dve.wait_ge(lsum_psum, 1)
                ch.step(nc.vector.tensor_scalar(logsum[:], pX[:, 0:1], 1.0 / T, 1e-6, ALU.mult, ALU.add))
                ch.step(nc.vector.reciprocal(logsum[:], logsum[:]))
                ch.step(nc.vector.tensor_scalar(logv[:], logv[:], logsum[:, 0:1], 0.5, ALU.mult, ALU.mult))
                dve.wait_ge(unc_ready, 1)
                ch.step(nc.vector.scalar_tensor_tensor(gate[:], gate[:], 2.5, logv[:], ALU.mult, ALU.add))
                nc.vector.tensor_scalar(gate[:], gate[:], 0.0, 5.0, ALU.max, ALU.min).then_inc(unc_ready, 1)
                dve.wait_ge(gate_ready, 1)
                dve.wait_ge(look_ready, NT)
                with dve.Fori(0, NCH // 2) as pair:
                    for par in range(2):
                        c = pair * 2 + par
                        dve.wait_ge(out_done[par], pair * 16)
                        for j in range(TPC):
                            n = c * TPC + j
                            nc.vector.scalar_tensor_tensor(result[:, par, j, :], look_all[:, ds(n, 1), :], gate[:, ds(n, 1)], sum_all[:, ds(n, 1), :], ALU.mult, ALU.add).then_inc(out_ready, 1)

            @block.scalar
            def _(act):
                def move(c, what, dst):
                    n = t_use(c, what)
                    act.wait_ge(t_psum, n + 1)
                    for k in range(2):
                        ins = nc.scalar.activation(dst(k), pT[:, k, :], ACT.Copy)
                    ins.then_inc(t_moved, 1)

                def head(c):
                    act.wait_ge(x_psum, c * XPER + 3)
                    nc.scalar.activation(query[:], pX[:], ACT.Copy).then_inc(query_ready, 1)

                def tail(c):
                    act.wait_ge(x_psum, c * XPER + 4)
                    nc.scalar.activation(rq[0:RD, :], pX[0:RD, :], ACT.Copy, scale=float(RD) ** -0.5).then_inc(rq_ready, 1)
                    act.wait_ge(x_psum, c * XPER + 5)
                    nc.scalar.activation(h1[:], pX[0:UH, :], ACT.Gelu, bias=b_u1[:, 0:1]).then_inc(h1_ready, 1)

                def expo(c, j):
                    n, b = c * TPC + j, j % 2
                    act.wait_ge(ntop_ready, n + 1)
                    act.wait_ge(dve_done_scores, n + 1)
                    nc.scalar.activation(expd[:, b, :], pS[:, b, :], ACT.Exp, bias=ntop[:, b:b + 1]).then_inc(exp_ready, 1)

                dve_done_scores = s_free
                act.wait_ge(w_in, 16 * NW)
                act.wait_ge(const_set, 3)
                move(0, "ctx", lambda k: ctxT[:, k, :])
                move(0, "xh", lambda k: xT[:, k, :])
                head(0)
                tail(0)
                wT = lambda k: weightT[:, 4 * k:4 * k + 4, :]

                def body(c, more):
                    expo(c, 0)
                    if more:
                        move(c + 1, "ctx", lambda k: ctxT[:, k, :])
                    expo(c, 1)
                    move(c, 0, wT)
                    move(c, 1, wT)
                    expo(c, 2)
                    if more:
                        move(c + 1, "xh", lambda k: xT[:, k, :])
                        head(c + 1)
                    expo(c, 3)
                    move(c, 2, wT)
                    move(c, 3, wT)
                    if more:
                        tail(c + 1)

                with act.Fori(0, NCH - 1) as c:
                    body(c, True)
                body(NCH - 1, False)
                act.wait_ge(var_all, 1)
                nc.scalar.activation(logv[:], var_v[:], ACT.Ln, bias=1.0, accum_out=tmp_v[:, 0:1]).then_inc(lsum_ready, 1)
                act.wait_ge(learn_ready, NCH)
                nc.scalar.activation(gate[:], learned_all[:], ACT.Sigmoid, bias=scalars[:, 0:1]).then_inc(unc_ready, 1)
                act.wait_ge(unc_ready, 2)
                nc.scalar.activation(gate[:], gate[:], ACT.Sigmoid, bias=scalars[:, 2:3], scale=scalars[:, 1:2]).then_inc(gate_ready, 1)

            @block.tensor
            def _(pe):
                def flip(c, what, src):
                    n = t_use(c, what)
                    pe.wait_ge(t_moved, n)
                    for i in range(8):
                        last = nc.tensor.transpose(pT[:, i // 4, (i % 4) * 128:(i % 4 + 1) * 128], src(i // 4, i % 4), ident[:])
                    last.then_inc(t_psum, 1)

                def flip_ctx(c):
                    pe.wait_ge(c_in, (c + 1) * 32)
                    flip(c, "ctx", lambda k, j: ctx[:, j, k * 128:(k + 1) * 128])

                def x3_pair(c, hlf):
                    if hlf == 0:
                        pe.wait_ge(t_moved, t_use(c, "ctx") + 1)
                        pe.wait_ge(learn_ready, c)
                    else:
                        pe.wait_ge(x3_ready, c * TPC + 2)
                    for j in (2 * hlf, 2 * hlf + 1):
                        for k in range(KD):
                            last = nc.tensor.matmul(pX[:, (j % 2) * D:(j % 2 + 1) * D], ctxT[:, k, j * 128:(j + 1) * 128], w_o[:, k, :], start=(k == 0), stop=(k == KD - 1))
                    last.then_inc(x_psum, 1)

                def flip_xh(c):
                    pe.wait_ge(xh_ready, c + 1)
                    flip(c, "xh", lambda k, j: xh[:, j, k * 128:(k + 1) * 128])

                def project(c):
                    pe.wait_ge(t_moved, t_use(c, "xh") + 1)
                    pe.wait_ge(x3_ready, (c + 1) * TPC)
                    for k in range(KD):
                        last = nc.tensor.matmul(pX[:], w_q[:, k, :], xT[:, k, :], start=(k == 0), stop=(k == KD - 1))
                    last.then_inc(x_psum, 1)

                def route(c):
                    pe.wait_ge(query_ready, c + 1)
                    nc.tensor.matmul(pX[0:RD, :], w_r[:], query[:], start=True, stop=True).then_inc(x_psum, 1)
                    pe.wait_ge(rq_ready, c + 1)
                    for k in range(KD):
                        last = nc.tensor.matmul(pX[0:UH, :], w_u1[:, k, :], xT[:, k, :], start=(k == 0), stop=(k == KD - 1))
                    last.then_inc(x_psum, 1)

                def learn(c):
                    pe.wait_ge(h1_ready, c + 1)
                    for j in range(TPC):
                        last = nc.tensor.matmul(pX[:, j:j + 1], h1[:, j * 128:(j + 1) * 128], w_u2[:], start=True, stop=True)
                    last.then_inc(x_psum, 1)

                def scores(c, j):
                    n, b = c * TPC + j, j % 2
                    if j >= 2:
                        pe.wait_ge(exp_ready, n - 1)
                    else:
                        pe.wait_ge(exp_ready, c * TPC)
                        pe.wait_ge(rq_ready, c + 1)
                    for i in range(NK // CH):
                        last = nc.tensor.matmul(pS[:, b, i * CH:(i + 1) * CH], rq[0:RD + 1, j * 128:(j + 1) * 128], rk[:, i * CH:(i + 1) * CH], start=True, stop=True)
                    last.then_inc(s_psum, 1)

                def flip_weights(c, j):
                    n, b = c * TPC + j, j % 2
                    pe.wait_ge(weight_ready, n + 1)
                    pe.wait_ge(look_psum, n)
                    flip(c, j, lambda k, i: weight[:, b, (4 * k + i) * 128:(4 * k + i + 1) * 128])

                def lookup(c, j):
                    n = c * TPC + j
                    pe.wait_ge(t_moved, t_use(c, j) + 1)
                    pe.wait_ge(look_ready, n)
                    for k in range(KV):
                        last = nc.tensor.matmul(pL[:, 0:D], weightT[:, k, :], values[:, k, :], start=(k == 0), stop=(k == KV - 1))
                    last.then_inc(look_psum, 1)

                pe.wait_ge(w_in, 16 * NW)
                pe.wait_ge(const_set, 3)
                for i in range(2):
                    nc.tensor.matmul((pX, pL)[i][0:RD, :], w_r[:], keysT[:, i * CH:(i + 1) * CH], start=True, stop=True).then_inc(rk_psum, 1)
                flip_ctx(0)
                pe.wait_ge(rk_moved, 2)
                x3_pair(0, 0)
                x3_pair(0, 1)
                flip_xh(0)
                project(0)
                route(0)
                learn(0)

                def body(c, more):
                    scores(c, 0)
                    scores(c, 1)
                    if more:
                        flip_ctx(c + 1)
                        x3_pair(c + 1, 0)
                    flip_weights(c, 0)
                    scores(c, 2)
                    lookup(c, 0)
                    if more:
                        x3_pair(c + 1, 1)
                    flip_weights(c, 1)
                    scores(c, 3)
                    lookup(c, 1)
                    if more:
                        flip_xh(c + 1)
                        project(c + 1)
                    flip_weights(c, 2)
                    lookup(c, 2)
                    flip_weights(c, 3)
                    if more:
                        route(c + 1)
                    lookup(c, 3)
                    if more:
                        learn(c + 1)

                with pe.Fori(0, NCH - 1) as c:
                    body(c, True)
                body(NCH - 1, False)
                pe.wait_ge(lsum_ready, 1)
                nc.tensor.matmul(pX[:, 0:1], ones[:], tmp_v[:, 0:1], start=True, stop=True).then_inc(lsum_psum, 1)
        s.clear()


def build_program(nc, inputs, out):
    a = dict(inputs)
    a["out"] = out
    for name, shape, dt in (("xr", (T, D), FP32), ("uT", (DI, T), FP32), ("gT", (DI, T), FP32), ("dT", (DI, T), FP32),
                            ("BC", (2 * NS, T), FP32), ("c_split", (3, NS, T), BF16), ("yT", (DI, T), FP32),
                            ("x1", (T, D), FP32), ("rw", (T, NE), FP32), ("qkT", (2 * HD, T), FP32), ("v0", (T, HD), FP32),
                            ("x2", (T, D), FP32), ("q_parts", (3, D, T), BF16), ("k_parts", (3, KVD, T), BF16), ("v1", (T, KVD), FP32),
                            ("ctx", (T, D), FP32)):
        a[name] = nc.dram_tensor(f"mid_{name}", shape, dt, kind="Internal").ap()
    for stage in (mamba_front, selective_scan, expert_front, causal_attention, rotary_front, full_attention, key_lookup):
        stage(nc, a)


def columns(v, parts=128):
    v = np.asarray(v)
    return np.ascontiguousarray(np.swapaxes(v.reshape((-1, parts) + v.shape[1:]), 0, 1))


def lay_out(i):
    g = {k.replace('L0_attn_', 'm_').replace('L0_ffn_', 'e_').replace('L1_attn_', 'h_').replace('L1_ffn_', 'f_'): np.ascontiguousarray(np.asarray(v)) for k, v in i.items()}
    a = {'x': g['m_x'].reshape(-1, 256), 'ident': np.eye(128, dtype=np.float32)}
    a['W_in'], a['W_x'], a['W_dt'], a['W_out'] = g['m_W_in'], g['m_W_x'], g['m_W_dt'], g['m_W_out']
    for n in ('norm_w', 'norm_b', 'conv_b', 'b_dt', 'A_log', 'D'):
        a[n] = columns(g['m_' + n])
    a['conv_w'] = columns(g['m_conv_w'].reshape(512, 4))
    a['part_of'] = np.tile(np.eye(32, 16, dtype=np.float32), (3, 1))
    a['a_log_d'] = np.ascontiguousarray(np.concatenate([columns(g['m_A_log']), columns(g['m_D'])[:, :, None]], axis=2))
    a['sim'] = g['e_sim_matrix']
    a['gates'] = g['e_gates'].reshape(1, 16)
    a['expert_no'] = np.tile(np.arange(16, dtype=np.float32), (128, 1))
    qkv = np.concatenate([g['e_q_proj'], g['e_k_proj'], g['e_v_proj']], axis=2)
    a['w_qkv'] = np.ascontiguousarray(qkv.transpose(1, 0, 2).reshape(256, -1))
    a['w_o'] = g['e_o_proj'].reshape(1024, 256)
    a['above'] = np.triu(np.full((128, 128), -1e30, np.float32), 1)
    place = np.arange(16)
    partner = np.where(place < 8, 2 * place + 1, 2 * (place - 8))
    rows = lambda n: (np.arange(n) // 16) * 16 + partner[np.arange(n) % 16]
    w = [g['h_Wq'], g['h_Wk'], g['h_Wq'][rows(256)], g['h_Wk'][rows(64)]]
    a['w_qk'] = np.ascontiguousarray(np.concatenate(w, axis=0).T)
    a['w_v'] = np.ascontiguousarray(g['h_Wv'].T)
    a['b_v'] = g['h_bv'].reshape(1, 64)
    b_qk = np.zeros((128, 6), np.float32)
    for i, v in enumerate((g['h_bq'][:128], g['h_bq'][128:], g['h_bk'], g['h_bq'][rows(256)][:128], g['h_bq'][rows(256)][128:], g['h_bk'][rows(64)])):
        b_qk[:len(v), i] = v
    a['b_qk'] = b_qk
    freq = (1.0 / np.float32(10000.0) ** (np.arange(0, 16, 2, dtype=np.float32) / np.float32(16))).astype(np.float32)
    turn = (np.arange(2048, dtype=np.float32)[None, :] * freq[np.arange(128) % 8][:, None]).astype(np.float32)
    a['cos'] = np.cos(turn).astype(np.float32)
    a['sin'] = np.sin(turn).astype(np.float32) * np.where(np.arange(128) % 16 < 8, -1, 1).astype(np.float32)[:, None]
    t = lambda v: np.ascontiguousarray(v.T)
    a['w_ho'], a['b_ho'] = t(g['h_Wo']), g['h_bo'].reshape(1, 256)
    a['w_fq'], a['w_r'], a['keysT'] = t(g['f_q_proj_w']), t(g['f_router_w']), t(g['f_aux_keys'])
    a['reliability'], a['values'] = g['f_reliability_mask'].reshape(1, 1024), g['f_aux_values']
    a['w_u1'], a['b_u1'], a['w_u2'] = t(g['f_unc_w1']), g['f_unc_b1'].reshape(64, 1), t(g['f_unc_w2'])
    for n in ('unc_b2', 'gate_w1', 'gate_bias'):
        a[n] = g['f_' + n].reshape(1, 1)
    return a


def kernel(**inputs):
    import concourse.bacc as bacc
    from concourse.bass_utils import run_bass_kernel_spmd

    nc = bacc.Bacc("TRN2", target_bir_lowering=False, num_devices=1)
    arrays = lay_out(inputs)
    tensors = {n: nc.dram_tensor(f"in_{n}", v.shape, mybir.dt.from_np(v.dtype), kind="ExternalInput").ap() for n, v in arrays.items()}
    out = nc.dram_tensor("out_0", (T, D), FP32, kind="ExternalOutput").ap()
    build_program(nc, tensors, out)
    r = run_bass_kernel_spmd(nc, [{f"in_{n}": v for n, v in arrays.items()}], core_ids=[0])
    return r.results[0]["out_0"].reshape(B, L, D)
```
